# Optimizing a Trainium2 kernel written in Bass

```python
import numpy as np
import jax
import jax.numpy as jnp

def _softmax(x, axis=-1):
    return jax.nn.softmax(x, axis=axis)

def _gelu(x):
    return jax.nn.gelu(x, approximate=True)

def _silu(x):
    return jax.nn.silu(x)

def _sigmoid(x):
    return jax.nn.sigmoid(x)

def _layernorm(x, axis=-1, eps=1e-05):
    m = jnp.mean(x, axis=axis, keepdims=True)
    v = jnp.var(x, axis=axis, keepdims=True)
    return (x - m) / jnp.sqrt(v + eps)

def _scatter_add(tgt, idx, src, axis=0):
    return tgt.at[idx].add(src)

def _segment_sum(src, seg, n):
    return jax.ops.segment_sum(src, seg, n)
kernel_name = 'mk_prb_d1_jaxref_r4_27c7b6'

def setup_inputs(seed: int=0):
    np.random.seed(seed)
    _w = jnp.asarray

    def _L0_attn_setup():
        import jax, jax.numpy as jnp
        import numpy as np
        B, S, D = (4, 512, 256)
        key = jax.random.key(seed)
        k1, k2 = jax.random.split(key)
        x = jax.random.normal(k1, (B, S, D), dtype=jnp.float32)
        W = jax.random.normal(k2, (2 * D, D), dtype=jnp.float32) * 0.02
        return {'x': x, 'W': W}
    _L0_attn_in = _L0_attn_setup()

    def _L0_ffn_setup():
        import jax, jax.numpy as jnp
        import numpy as np
        D = 256
        H = 16
        DH = D // H
        DC = D // 4
        HID = 512
        G = 2
        EPG = 4
        E = G * EPG
        TOPK = 2
        EPS = 1e-06
        B, T = (2, 512)

        def _rope_sincos(t, dh):
            inv_freq = 1.0 / 10000.0 ** (jnp.arange(0, dh, 2, dtype=jnp.float32) / dh)
            ang = jnp.arange(t, dtype=jnp.float32)[:, None] * inv_freq[None, :]
            return (jnp.sin(ang), jnp.cos(ang))

        def _apply_rope(x, sin, cos):
            x1 = x[..., ::2]
            x2 = x[..., 1::2]
            r = jnp.stack([x1 * cos - x2 * sin, x1 * sin + x2 * cos], axis=-1)
            return r.reshape(x.shape)

        def _swiglu(x):
            a, b = jnp.split(x, 2, axis=-1)
            return jax.nn.silu(a) * b

        def _rmsnorm(x, w):
            return x * jax.lax.rsqrt(jnp.mean(x * x, axis=-1, keepdims=True) + EPS) * w
        key = jax.random.key(seed)
        ks = jax.random.split(key, 14)
        s = 0.02
        return {'src': jax.random.normal(ks[0], (B, T, D), jnp.float32), 'Wq': jax.random.normal(ks[1], (D, D), jnp.float32) * s, 'Wk_c': jax.random.normal(ks[2], (D, DC), jnp.float32) * s, 'Wv_c': jax.random.normal(ks[3], (D, DC), jnp.float32) * s, 'Wk': jax.random.normal(ks[4], (DC, D), jnp.float32) * s, 'Wv': jax.random.normal(ks[5], (DC, D), jnp.float32) * s, 'Wo': jax.random.normal(ks[6], (D, D), jnp.float32) * s, 'W_shared_in': jax.random.normal(ks[7], (D, 2 * HID), jnp.float32) * s, 'W_shared_out': jax.random.normal(ks[8], (HID, D), jnp.float32) * s, 'W1_shared': jax.random.normal(ks[9], (D, 2 * HID), jnp.float32) * s, 'W2_experts': jax.random.normal(ks[10], (E, HID, D), jnp.float32) * s, 'Wg_gate': jax.random.normal(ks[11], (D, G), jnp.float32) * s, 'We_gate': jax.random.normal(ks[12], (D, E), jnp.float32) * s, 'group_bias': jnp.zeros((G,), jnp.float32), 'expert_bias': jnp.zeros((E,), jnp.float32), 'norm1_w': jnp.ones((D,), jnp.float32), 'norm2_w': jnp.ones((D,), jnp.float32)}
    _L0_ffn_in = _L0_ffn_setup()
    _d = {'L0_attn_x': _L0_attn_in['x'], 'L0_attn_W': _L0_attn_in['W'], 'L0_ffn_Wq': _L0_ffn_in['Wq'], 'L0_ffn_Wk_c': _L0_ffn_in['Wk_c'], 'L0_ffn_Wv_c': _L0_ffn_in['Wv_c'], 'L0_ffn_Wk': _L0_ffn_in['Wk'], 'L0_ffn_Wv': _L0_ffn_in['Wv'], 'L0_ffn_Wo': _L0_ffn_in['Wo'], 'L0_ffn_W_shared_in': _L0_ffn_in['W_shared_in'], 'L0_ffn_W_shared_out': _L0_ffn_in['W_shared_out'], 'L0_ffn_W1_shared': _L0_ffn_in['W1_shared'], 'L0_ffn_W2_experts': _L0_ffn_in['W2_experts'], 'L0_ffn_Wg_gate': _L0_ffn_in['Wg_gate'], 'L0_ffn_We_gate': _L0_ffn_in['We_gate'], 'L0_ffn_group_bias': _L0_ffn_in['group_bias'], 'L0_ffn_expert_bias': _L0_ffn_in['expert_bias'], 'L0_ffn_norm1_w': _L0_ffn_in['norm1_w'], 'L0_ffn_norm2_w': _L0_ffn_in['norm2_w']}
    _x0 = _d['L0_attn_x']
    _d['L0_attn_x'] = jax.random.normal(jax.random.fold_in(jax.random.key(seed), 1), (4, 1024, 256), dtype=_x0.dtype)
    del _x0
    return _d

def reference(L0_attn_x, L0_attn_W, L0_ffn_Wq, L0_ffn_Wk_c, L0_ffn_Wv_c, L0_ffn_Wk, L0_ffn_Wv, L0_ffn_Wo, L0_ffn_W_shared_in, L0_ffn_W_shared_out, L0_ffn_W1_shared, L0_ffn_W2_experts, L0_ffn_Wg_gate, L0_ffn_We_gate, L0_ffn_group_bias, L0_ffn_expert_bias, L0_ffn_norm1_w, L0_ffn_norm2_w):

    def _L0_attn_ref(x, W):
        import jax, jax.numpy as jnp
        import numpy as np
        B, S, D = (4, 512, 256)
        d = x.shape[-1]
        kv = x @ W.T
        K, V = (kv[..., :d], kv[..., d:])
        n = x.shape[-2]
        causal = jnp.tril(jnp.ones((n, n), dtype=bool))
        mask = jnp.where(causal, jnp.float32(0.0), -jnp.inf).astype(x.dtype)
        scores = jnp.einsum('bqd,bkd->bqk', x, K) + mask
        attn = jax.nn.softmax(scores, axis=-1)
        return x + jnp.einsum('bqk,bkd->bqd', attn, V)

    def _L0_ffn_ref(src, Wq, Wk_c, Wv_c, Wk, Wv, Wo, W_shared_in, W_shared_out, W1_shared, W2_experts, Wg_gate, We_gate, group_bias, expert_bias, norm1_w, norm2_w):
        import jax, jax.numpy as jnp
        import numpy as np
        D = 256
        H = 16
        DH = D // H
        DC = D // 4
        HID = 512
        G = 2
        EPG = 4
        E = G * EPG
        TOPK = 2
        EPS = 1e-06
        B, T = (2, 512)

        def _rope_sincos(t, dh):
            inv_freq = 1.0 / 10000.0 ** (jnp.arange(0, dh, 2, dtype=jnp.float32) / dh)
            ang = jnp.arange(t, dtype=jnp.float32)[:, None] * inv_freq[None, :]
            return (jnp.sin(ang), jnp.cos(ang))

        def _apply_rope(x, sin, cos):
            x1 = x[..., ::2]
            x2 = x[..., 1::2]
            r = jnp.stack([x1 * cos - x2 * sin, x1 * sin + x2 * cos], axis=-1)
            return r.reshape(x.shape)

        def _swiglu(x):
            a, b = jnp.split(x, 2, axis=-1)
            return jax.nn.silu(a) * b

        def _rmsnorm(x, w):
            return x * jax.lax.rsqrt(jnp.mean(x * x, axis=-1, keepdims=True) + EPS) * w
        Bb, Tt, C = src.shape
        q = (src @ Wq).reshape(Bb, Tt, H, DH).transpose(0, 2, 1, 3)
        k = (src @ Wk_c @ Wk).reshape(Bb, Tt, H, DH).transpose(0, 2, 1, 3)
        v = (src @ Wv_c @ Wv).reshape(Bb, Tt, H, DH).transpose(0, 2, 1, 3)
        sin, cos = _rope_sincos(Tt, DH)
        q = _apply_rope(q, sin, cos)
        k = _apply_rope(k, sin, cos)
        attn = jnp.einsum('bhqd,bhkd->bhqk', q, k) / np.sqrt(DH).astype(np.float32)
        attn = jax.nn.softmax(attn, axis=-1)
        sa = jnp.einsum('bhqk,bhkd->bhqd', attn, v)
        sa = sa.transpose(0, 2, 1, 3).reshape(Bb, Tt, C) @ Wo
        x = _rmsnorm(src + sa, norm1_w)
        S = Bb * Tt
        flat = x.reshape(S, C)
        shared = _swiglu(flat @ W_shared_in) @ W_shared_out
        g_probs = jax.nn.softmax(flat @ Wg_gate + group_bias, -1)
        g_idx = jnp.argmax(g_probs, axis=-1)
        e_logits = flat @ We_gate + expert_bias
        e_group = jnp.arange(E) // EPG
        in_group = e_group[None, :] == g_idx[:, None]
        e_probs = jax.nn.softmax(jnp.where(in_group, e_logits, -jnp.inf), -1)
        g_prob = jnp.take_along_axis(g_probs, g_idx[:, None], axis=1)
        p_expert = e_probs * g_prob
        topv, topi = jax.lax.top_k(p_expert, TOPK)
        w = jnp.zeros((S, E), flat.dtype).at[jnp.arange(S)[:, None], topi].set(topv)
        h = _swiglu(flat @ W1_shared)
        routed = jnp.zeros_like(shared)
        for e in range(E):
            routed = routed + h @ W2_experts[e] * w[:, e:e + 1]
        out = x + (shared + routed).reshape(Bb, Tt, C)
        return _rmsnorm(out, norm2_w)
    x = L0_attn_x
    xn = _layernorm(x, axis=-1)
    x = x + _L0_attn_ref(xn, L0_attn_W) + _L0_ffn_ref(xn, L0_ffn_Wq, L0_ffn_Wk_c, L0_ffn_Wv_c, L0_ffn_Wk, L0_ffn_Wv, L0_ffn_Wo, L0_ffn_W_shared_in, L0_ffn_W_shared_out, L0_ffn_W1_shared, L0_ffn_W2_experts, L0_ffn_Wg_gate, L0_ffn_We_gate, L0_ffn_group_bias, L0_ffn_expert_bias, L0_ffn_norm1_w, L0_ffn_norm2_w)
    return x

_drawn_inputs = setup_inputs


def setup_inputs(seed=0):
    import zlib

    import numpy as np

    out = dict(_drawn_inputs(seed))
    spreads = {'L0_ffn_group_bias': (0.0, 0.8),
     'L0_ffn_expert_bias': (0.0, 0.8),
     'L0_ffn_norm1_w': (1.0, 0.2),
     'L0_ffn_norm2_w': (1.0, 0.2)}
    factors = {'L0_ffn_Wq': 8.0,
     'L0_ffn_Wk_c': 8.0,
     'L0_ffn_Wv_c': 8.0,
     'L0_ffn_Wk': 8.0,
     'L0_ffn_Wv': 8.0,
     'L0_ffn_Wo': 8.0,
     'L0_ffn_W_shared_in': 6.492,
     'L0_ffn_W_shared_out': 6.516,
     'L0_ffn_W1_shared': 8.0,
     'L0_ffn_W2_experts': 8.0,
     'L0_ffn_Wg_gate': 8.0,
     'L0_ffn_We_gate': 8.0}
    for name, (base, spread) in spreads.items():
        noise = np.random.default_rng([zlib.crc32(name.encode()), seed]).standard_normal(out[name].shape)
        drawn = base * np.exp(spread * noise) if base else spread * noise
        out[name] = jnp.asarray(drawn.astype(out[name].dtype))
    for name, factor in factors.items():
        out[name] = (out[name] * factor).astype(out[name].dtype)
    return out
```

```python
import concourse.bass as bass
from concourse import mybir
from contextlib import ExitStack

F32 = mybir.dt.float32
BF16 = mybir.dt.bfloat16
ACT = mybir.ActivationFunctionType
ALU = mybir.AluOpType
AX = mybir.AxisListType

P = 128
B, S, D = 4, 1024, 256
N = B * S
CH = 512
NCH = N // CH
TPC = CH // P
KD = D // P
H, DH = 16, 16
GH = 4
NG = H // GH
VW = 32
HID, E = 512, 8
EPG = 4
DC = D // 4
QT = S // P
LN_EPS, RMS_EPS = 1e-5, 1e-6
MASKED = -3.0e38
QTERM = (0, 0, 1, 0, 2, 1)
KTERM = (0, 1, 0, 2, 0, 1)
NT = len(QTERM)
DOTS = NT * DH
SHIFT = 3


class Waits:

    def __init__(self, sp, begun):
        self.sp, self.begun = sp, begun
        sp.sem_inc(begun, 1)

    def ge(self, sem, value):
        self.sp.wait_ge(self.begun, 1)
        self.sp.wait_ge(sem, value)


def project(nc, x, w_kv_t, w_q, w_kc, w_vc, w_k, w_v, rope_cos, rope_sin,
            xn_d, xx_d, xnT_d, kaT_d, va_d, vh_d, q_d, k_d):
    with ExitStack() as ctx:
        sb = lambda name, shape, dt=F32: ctx.enter_context(nc.sbuf_tensor(name, shape, dt))
        sem = lambda name: ctx.enter_context(nc.semaphore(name))
        sems = lambda name: [sem(f"{name}{s}") for s in range(2)]
        two = lambda name, shape, dt=F32: [sb(f"{name}{s}", shape, dt) for s in range(2)]
        wkv = sb("p_wkv", [P, KD, 2 * D])
        wq = sb("p_wq", [P, KD, D])
        wkvc = sb("p_wkvc", [P, KD, 2 * DC])
        wk = sb("p_wk", [P, D])
        wv = sb("p_wv", [P, D])
        cos = sb("p_cos", [P, 2, CH])
        sin = sb("p_sin", [P, 2, CH])
        ident = sb("p_ident", [P, P])
        xin = two("p_xin", [P, TPC, D])
        xn = two("p_xn", [P, TPC, D])
        xx = two("p_xx", [P, TPC, D])
        stats = sb("p_stats", [P, TPC, 6])
        fence = sb("p_fence", [P, 1])
        mv = sb("p_mv", [P, TPC, 2])
        veps = two("p_veps", [P, TPC])
        sd = two("p_sd", [P, TPC])
        rstd = sb("p_rstd", [P, TPC])
        xnT = two("p_xnT", [P, KD, CH])
        kaT = two("p_kaT", [P, KD, CH])
        va = two("p_va", [P, TPC, D])
        kvc = two("p_kvc", [P, CH])
        vh = two("p_vh", [P, TPC, H, VW])
        qk = sb("p_qk", [P, 2 * KD, CH])
        swap = sb("p_swap", [P, 2 * KD, CH])
        tcos = sb("p_tcos", [P, 2 * KD, CH])
        tsin = sb("p_tsin", [P, 2 * KD, CH])
        rot = sb("p_rot", [P, 2 * KD, CH])
        rest = sb("p_rest", [P, 2 * KD, CH])
        parts = two("p_parts", [P, 3, 2 * KD, CH], BF16)
        ps = [ctx.enter_context(nc.psum_tensor(f"p_ps{i}", [P, 2, CH], F32)) for i in range(4)]
        T, KA, VA, Q, KVC, K, V = range(7)
        BANKS = {T: 0, KA: 1, VA: 2, Q: 3, KVC: 0, K: 1, V: 2}

        weights = sem("p_weights")
        tables = sem("p_tables")
        ones_set = sem("p_ones_set")
        ident_set = sem("p_ident_set")
        x_in = sems("p_x_in")
        xn_done = sems("p_xn_done")
        xx_done = sems("p_xx_done")
        var_done = sems("p_var_done")
        sd_done = sems("p_sd_done")
        made = [sems(f"p_made{j}") for j in range(7)]
        taken = [sems(f"p_taken{j}") for j in range(7)]
        sw_done = sems("p_sw_done")
        sin_done = sems("p_sin_done")
        rot_done = sems("p_rot_done")
        hi_done = sems("p_hi_done")
        rest_done = sems("p_rest_done")
        mid_done = sems("p_mid_done")
        lo_done = sems("p_lo_done")
        st = {n: sems("p_st_" + n) for n in ("xn", "xx", "xnT", "kaT", "va", "vh", "parts")}
        chain = sem("p_chain")
        LINKS = 3
        TURNS = NCH // 2
        begun = sem("p_begun")
        with nc.Block() as block:

            @block.gpsimd
            def _(pool):
                nc.gpsimd.memset(ident[:, :], 0.0).then_inc(ident_set, 1)
                pool.wait_ge(ident_set, 1)
                nc.gpsimd.affine_select(out=ident[:, :], in_=ident[:, :], compare_op=ALU.not_equal, fill=1.0,
                                        base=0, pattern=[[-1, P]], channel_multiplier=1).then_inc(ident_set, 1)
                pool.wait_ge(tables, 32)

                def add(it, s):
                    pool.wait_ge(xn_done[s], it + 1)
                    pool.wait_ge(st["xx"][s], it * 16)
                    nc.gpsimd.tensor_tensor(xx[s][:, :, :], xin[s][:, :, :], xn[s][:, :, :],
                                            ALU.add).then_inc(xx_done[s], 1)

                def sine(it, s):
                    pool.wait_ge(sw_done[s], it + 1)
                    for j in range(2 * KD):
                        last = nc.gpsimd.tensor_tensor(tsin[:, j, :], swap[:, j, :], sin[:, s, :], ALU.mult)
                    last.then_inc(sin_done[s], 1)

                add(0, 0)
                with pool.Fori(0, TURNS - 1) as it:
                    add(it, 1)
                    sine(it, 0)
                    add(it + 1, 0)
                    sine(it, 1)
                add(TURNS - 1, 1)
                sine(TURNS - 1, 0)
                sine(TURNS - 1, 1)

            @block.sync
            def _(sp):
                wait = Waits(sp, begun)
                sp.dma_start(cos[:, :, :], rope_cos.rearrange("p (s n) -> p s n", s=2)).then_inc(tables, 16)
                sp.dma_start(sin[:, :, :], rope_sin.rearrange("p (s n) -> p s n", s=2)).then_inc(tables, 16)
                rows = lambda a, t0: a[bass.ds(t0, CH), :].rearrange("(j p) d -> p j d", p=P)
                cols = lambda a, t0: a[:, bass.ds(t0, CH)].rearrange("(m p) t -> p m t", p=P)

                def load(it, s):
                    t0 = (it * 2 + s) * CH
                    sp.dma_start(xin[s][:, :, :], rows(x, t0)).then_inc(x_in[s], 16)

                def store_norm(it, s):
                    t0 = (it * 2 + s) * CH
                    wait.ge(xn_done[s], it + 1)
                    sp.dma_start(rows(xn_d, t0), xn[s][:, :, :]).then_inc(st["xn"][s], 16)
                    wait.ge(xx_done[s], it + 1)
                    sp.dma_start(rows(xx_d, t0), xx[s][:, :, :]).then_inc(st["xx"][s], 16)

                def store_products(it, s):
                    t0 = (it * 2 + s) * CH
                    wait.ge(taken[T][s], it + 1)
                    sp.dma_start(cols(xnT_d, t0), xnT[s][:, :, :]).then_inc(st["xnT"][s], 16)
                    wait.ge(taken[KA][s], it + 1)
                    sp.dma_start(cols(kaT_d, t0), kaT[s][:, :, :]).then_inc(st["kaT"][s], 16)
                    wait.ge(taken[VA][s], it + 1)
                    sp.dma_start(rows(va_d, t0), va[s][:, :, :]).then_inc(st["va"][s], 16)
                    wait.ge(taken[V][s], it + 1)
                    sp.dma_start(rows(vh_d, t0), vh[s][:, :, :, :].rearrange("p j h w -> p j (h w)"))\
                        .then_inc(st["vh"][s], 16)
                    wait.ge(lo_done[s], it + 1)
                    for r in range(3):
                        sp.dma_start(cols(q_d[r], t0), parts[s][:, r, 0:KD, :]).then_inc(st["parts"][s], 16)
                        sp.dma_start(cols(k_d[r], t0), parts[s][:, r, KD:2 * KD, :]).then_inc(st["parts"][s], 16)

                for s in range(2):
                    load(0, s)
                with sp.Fori(0, TURNS - 1) as it:
                    for s in range(2):
                        store_norm(it, s)
                        load(it + 1, s)
                    for s in range(2):
                        store_products(it, s)
                for s in range(2):
                    store_norm(TURNS - 1, s)
                for s in range(2):
                    store_products(TURNS - 1, s)
                for name, each in st.items():
                    for s in range(2):
                        sp.wait_ge(each[s], NCH // 2 * (96 if name == "parts" else 16))

            @block.scalar
            def _(act):
                act.dma_start(wkv[:, :, :], w_kv_t.rearrange("(k p) m -> p k m", p=P)).then_inc(weights, 16)
                act.dma_start(wq[:, :, :], w_q.rearrange("(k p) m -> p k m", p=P)).then_inc(weights, 16)
                act.dma_start(wkvc[:, :, 0:DC], w_kc.rearrange("(k p) m -> p k m", p=P)).then_inc(weights, 16)
                act.dma_start(wkvc[:, :, DC:2 * DC], w_vc.rearrange("(k p) m -> p k m", p=P)).then_inc(weights, 16)
                act.wait_ge(ones_set, 2)
                act.dma_start(wk[0:DC, :], w_k).then_inc(weights, 16)
                act.dma_start(wv[DC:2 * DC, :], w_v).then_inc(weights, 16)
                act.wait_ge(ones_set, 4)

                def root(it, s):
                    act.wait_ge(var_done[s], it + 1)
                    nc.scalar.activation(sd[s][:, :], veps[s][:, :], ACT.Sqrt).then_inc(sd_done[s], 1)

                def products(it, s):
                    def take(j, dst, src, stored=None):
                        act.wait_ge(made[j][s], it + 1)
                        if stored:
                            act.wait_ge(st[stored][s], it * 16)
                        nc.scalar.activation(dst, src, ACT.Copy).then_inc(taken[j][s], 1)

                    take(T, xnT[s][:, :, :], ps[BANKS[T]][:, :, :], "xnT")
                    take(KA, kaT[s][:, :, :], ps[BANKS[KA]][:, :, :], "kaT")
                    take(VA, va[s][:, :, :].rearrange("p j d -> p (j d)"),
                         ps[BANKS[VA]][:, :, :].rearrange("p a b -> p (a b)"), "va")
                    if s:
                        act.wait_ge(rot_done[0], it + 1)
                    else:
                        act.wait_ge(rot_done[1], it)
                    take(Q, qk[:, 0:KD, :], ps[BANKS[Q]][:, :, :])
                    take(KVC, kvc[s][:, :], ps[BANKS[KVC]][:, 0, :])
                    take(K, qk[:, KD:2 * KD, :], ps[BANKS[K]][:, :, :])
                    take(V, vh[s][:, :, :, 0:DH],
                         ps[BANKS[V]][:, :, :].rearrange("p a (b h d) -> p (a b) h d", h=H, d=DH), "vh")
                    act.wait_ge(rot_done[s], it + 1)
                    act.wait_ge(st["parts"][s], it * 96)
                    nc.scalar.activation(parts[s][:, 0, :, :], rot[:, :, :], ACT.Copy).then_inc(hi_done[s], 1)
                    act.wait_ge(rest_done[s], it + 1)
                    nc.scalar.activation(parts[s][:, 1, :, :], rest[:, :, :], ACT.Copy).then_inc(mid_done[s], 1)

                root(0, 0)
                with act.Fori(0, TURNS - 1) as it:
                    root(it, 1)
                    products(it, 0)
                    root(it + 1, 0)
                    products(it, 1)
                root(TURNS - 1, 1)
                products(TURNS - 1, 0)
                products(TURNS - 1, 1)

            @block.vector
            def _(dve):
                nc.vector.memset(wk[DC:2 * DC, :], 0.0).then_inc(ones_set, 1)
                nc.vector.memset(wv[0:DC, :], 0.0).then_inc(ones_set, 1)
                for s in range(2):
                    nc.vector.memset(vh[s][:, :, :, :].rearrange("p j h w -> p (j h w)"), 1.0).then_inc(ones_set, 1)
                dve.wait_ge(tables, 32)

                def link(ins, count):
                    ins.then_inc(chain, 1)
                    dve.wait_ge(chain, count)

                def norm(it, s):
                    n = it * 2 + s
                    dve.wait_ge(x_in[s], it * 16 + 16)
                    for j in range(TPC):
                        ins = nc.vector.bn_stats(stats[:, j, :], xin[s][:, j, :])
                    link(ins, n * LINKS + 1)
                    nc.vector.memset(fence[:, :], 0.0)
                    for j in range(TPC):
                        ins = nc.vector.bn_aggr(mv[:, j, :], stats[:, j, :])
                    link(ins, n * LINKS + 2)
                    nc.vector.tensor_scalar(veps[s][:, :], mv[:, :, 1], LN_EPS, None, ALU.add).then_inc(var_done[s], 1)
                    dve.wait_ge(sd_done[s], it + 1)
                    link(nc.vector.reciprocal(rstd[:, :], sd[s][:, :]), n * LINKS + 3)
                    dve.wait_ge(st["xn"][s], it * 16)
                    dve.wait_ge(made[T][s], it)
                    dve.wait_ge(xx_done[s], it)
                    for j in range(TPC):
                        ins = nc.vector.tensor_scalar(xn[s][:, j, :], xin[s][:, j, :], mv[:, j, 0:1],
                                                      rstd[:, j:j + 1], ALU.subtract, ALU.mult)
                    ins.then_inc(xn_done[s], 1)

                def rotate(it, s):
                    dve.wait_ge(taken[Q][s], it + 1)
                    dve.wait_ge(taken[K][s], it + 1)
                    nc.vector.tensor_tensor(tcos[:, :, :], qk[:, :, :],
                                            cos[:, s:s + 1, :].broadcast_to([P, 2 * KD, CH]), ALU.mult)
                    nc.vector.stream_shuffle(swap[:, :, :], qk[:, :, :],
                                             [i ^ 1 for i in range(32)]).then_inc(sw_done[s], 1)
                    dve.wait_ge(sin_done[s], it + 1)
                    if s:
                        dve.wait_ge(mid_done[0], it + 1)
                    else:
                        dve.wait_ge(mid_done[1], it)
                    nc.vector.tensor_tensor(rot[:, :, :], tcos[:, :, :], tsin[:, :, :],
                                            ALU.add).then_inc(rot_done[s], 1)
                    dve.wait_ge(rot_done[s], it + 1)
                    dve.wait_ge(hi_done[s], it + 1)
                    nc.vector.tensor_tensor(rest[:, :, :], rot[:, :, :], parts[s][:, 0, :, :],
                                            ALU.subtract).then_inc(rest_done[s], 1)
                    dve.wait_ge(rest_done[s], it + 1)
                    dve.wait_ge(mid_done[s], it + 1)
                    nc.vector.tensor_tensor(parts[s][:, 2, :, :], rest[:, :, :], parts[s][:, 1, :, :],
                                            ALU.subtract).then_inc(lo_done[s], 1)

                norm(0, 0)
                with dve.Fori(0, TURNS - 1) as it:
                    norm(it, 1)
                    rotate(it, 0)
                    norm(it + 1, 0)
                    rotate(it, 1)
                norm(TURNS - 1, 1)
                rotate(TURNS - 1, 0)
                rotate(TURNS - 1, 1)

            @block.tensor
            def _(pe):
                pe.wait_ge(weights, 6 * 16)
                pe.wait_ge(ident_set, 2)
                with pe.Fori(0, NCH // 2) as it:
                    for s in range(2):
                        def free(j):
                            if s:
                                pe.wait_ge(taken[j][0], it + 1)
                            else:
                                pe.wait_ge(taken[j][1], it)

                        def product(j, out, lhs, rhs, signal):
                            for k in range(KD):
                                ins = nc.tensor.matmul(out, lhs(k), rhs(k), start=k == 0, stop=k == KD - 1)
                            if signal:
                                ins.then_inc(made[j][s], 1)

                        pe.wait_ge(xn_done[s], it + 1)
                        free(KVC)
                        pe.wait_ge(taken[T][s], it)
                        for m in range(KD):
                            for j in range(TPC):
                                ins = nc.tensor.transpose(ps[BANKS[T]][:, m, j * P:(j + 1) * P],
                                                          xn[s][:, j, m * P:(m + 1) * P], ident[:, :])
                        ins.then_inc(made[T][s], 1)
                        pe.wait_ge(taken[T][s], it + 1)
                        free(K)
                        for m in range(KD):
                            product(KA, ps[BANKS[KA]][:, m, :], lambda k: wkv[:, k, m * P:(m + 1) * P],
                                    lambda k: xnT[s][:, k, :], m == KD - 1)
                        free(V)
                        for j in range(TPC):
                            product(VA, ps[BANKS[VA]][:, j // 2, (j % 2) * D:(j % 2 + 1) * D],
                                    lambda k: xnT[s][:, k, j * P:(j + 1) * P], lambda k: wkv[:, k, D:2 * D],
                                    j == TPC - 1)
                        free(Q)
                        for m in range(KD):
                            product(Q, ps[BANKS[Q]][:, m, :], lambda k: wq[:, k, m * P:(m + 1) * P],
                                    lambda k: xnT[s][:, k, :], m == KD - 1)
                        product(KVC, ps[BANKS[KVC]][:, 0, :], lambda k: wkvc[:, k, :],
                                lambda k: xnT[s][:, k, :], True)
                        pe.wait_ge(taken[KVC][s], it + 1)
                        pe.wait_ge(taken[KA][s], it + 1)
                        for m in range(KD):
                            ins = nc.tensor.matmul(ps[BANKS[K]][:, m, :], wk[:, m * P:(m + 1) * P],
                                                   kvc[s][:, :], start=True, stop=True)
                        ins.then_inc(made[K][s], 1)
                        pe.wait_ge(taken[VA][s], it + 1)
                        for j in range(TPC):
                            ins = nc.tensor.matmul(ps[BANKS[V]][:, j // 2, (j % 2) * D:(j % 2 + 1) * D],
                                                   kvc[s][:, j * P:(j + 1) * P], wv[:, :], start=True, stop=True)
                        ins.then_inc(made[V][s], 1)


def causal_attention(nc, xnT_d, kaT_d, va_d, xx_d, ya_d):
    with ExitStack() as ctx:
        sb = lambda name, shape, dt=F32: ctx.enter_context(nc.sbuf_tensor(name, shape, dt))
        sem = lambda name: ctx.enter_context(nc.semaphore(name))
        sems = lambda name: [sem(f"{name}{s}") for s in range(2)]
        two = lambda name, shape: [sb(f"{name}{s}", shape) for s in range(2)]
        ident = sb("a_ident", [P, P])
        mask = sb("a_mask", [P, P])
        qT = two("a_qT", [P, KD, S])
        kT = two("a_kT", [P, KD, S])
        va = two("a_va", [P, QT, D])
        xx = two("a_xx", [P, QT, D])
        negm = two("a_negm", [P, 1])
        probs = two("a_probs", [P, S])
        rowsum = two("a_rowsum", [P, 1])
        inv = two("a_inv", [P, 1])
        pT = two("a_pT", [P, QT, P])
        ya = two("a_ya", [P, D])
        sc = [ctx.enter_context(nc.psum_tensor(f"a_sc{i}", [P, S], F32)) for i in range(2)]
        tp = [ctx.enter_context(nc.psum_tensor(f"a_tp{i}", [P, 4, P], F32)) for i in range(2)]
        out = [ctx.enter_context(nc.psum_tensor(f"a_out{i}", [P, CH], F32)) for i in range(2)]

        const_set = sem("a_const_set")
        loaded = sems("a_loaded")
        scored = sems("a_scored")
        masked = sems("a_masked")
        max_done = sems("a_max_done")
        exp_done = sems("a_exp_done")
        turned = sems("a_turned")
        turned_out = sems("a_turned_out")
        mixed = sems("a_mixed")
        inv_done = sems("a_inv_done")
        ya_done = sems("a_ya_done")
        ya_stored = sems("a_ya_stored")
        U = 2 * QT
        GROUPS = [[(g, min(4, i + 1 - g)) for g in range(0, i + 1, 4)] for i in range(QT)]
        FIRST = [sum(len(GROUPS[v % QT]) for v in range(u)) for u in range(U)]
        PER = FIRST[-1] + len(GROUPS[QT - 1])
        with nc.Block() as block:

            @block.gpsimd
            def _(pool):
                nc.gpsimd.memset(ident[:, :], 0.0).then_inc(const_set, 1)
                nc.gpsimd.memset(mask[:, :], 0.0).then_inc(const_set, 1)
                pool.wait_ge(const_set, 2)
                nc.gpsimd.affine_select(out=ident[:, :], in_=ident[:, :], compare_op=ALU.not_equal, fill=1.0,
                                        base=0, pattern=[[-1, P]], channel_multiplier=1).then_inc(const_set, 1)
                nc.gpsimd.affine_select(out=mask[:, :], in_=mask[:, :], compare_op=ALU.is_ge, fill=MASKED,
                                        base=0, pattern=[[-1, P]], channel_multiplier=1).then_inc(const_set, 1)

            @block.sync
            def _(sp):
                def load(b, s):
                    rows = lambda a: a[bass.ds(b * S, S), :].rearrange("(j p) d -> p j d", p=P)
                    cols = lambda a: a[:, bass.ds(b * S, S)].rearrange("(m p) t -> p m t", p=P)
                    sp.dma_start(qT[s][:, :, :], cols(xnT_d)).then_inc(loaded[s], 16)
                    sp.dma_start(kT[s][:, :, :], cols(kaT_d)).then_inc(loaded[s], 16)
                    sp.dma_start(va[s][:, :, :], rows(va_d)).then_inc(loaded[s], 16)
                    sp.dma_start(xx[s][:, :, :], rows(xx_d)).then_inc(loaded[s], 16)

                for s in range(2):
                    load(s, s)
                with sp.Fori(0, B // 2 - 1) as it:
                    for s in range(2):
                        u = s * QT + QT - 1
                        sp.wait_ge(ya_done[u % 2], it * (U // 2) + u // 2 + 1)
                        load(it * 2 + 2 + s, s)

            @block.gpsimd
            def _(pool):
                with pool.Fori(0, B // 2) as it:
                    for u in range(U):
                        pool.wait_ge(ya_done[u % 2], it * (U // 2) + u // 2 + 1)
                        pool.dma_start(ya_d[bass.ds(it * 2 * S + u * P, P), :], ya[u % 2][:, :])\
                            .then_inc(ya_stored[u % 2], 16)
                for r in range(2):
                    pool.wait_ge(ya_stored[r], B * QT // 2 * 16)

            @block.tensor
            def _(pe):
                pe.wait_ge(const_set, 4)
                with pe.Fori(0, B // 2) as it:
                    def score(u):
                        s, i = divmod(u, QT)
                        if i == 0:
                            pe.wait_ge(loaded[s], it * 64 + 64)
                        pe.wait_ge(exp_done[u % 2], it * (U // 2) + u // 2)
                        n = (i + 1) * P
                        for c in range(0, n, CH):
                            w = min(CH, n - c)
                            for k in range(KD):
                                ins = nc.tensor.matmul(sc[u % 2][:, c:c + w], qT[s][:, k, i * P:(i + 1) * P],
                                                       kT[s][:, k, c:c + w], start=k == 0, stop=k == KD - 1)
                        ins.then_inc(scored[u % 2], 1)

                    score(0)
                    for u in range(U):
                        s, i = divmod(u, QT)
                        if u + 1 < U:
                            score(u + 1)
                        pe.wait_ge(exp_done[u % 2], it * (U // 2) + u // 2 + 1)
                        for g, (first, count) in enumerate(GROUPS[i]):
                            f = FIRST[u] + g
                            pe.wait_ge(turned_out[f % 2], it * (PER // 2) + f // 2)
                            for j in range(first, first + count):
                                ins = nc.tensor.transpose(tp[f % 2][:, j - first, :],
                                                          probs[u % 2][:, j * P:(j + 1) * P], ident[:, :])
                            ins.then_inc(turned[f % 2], 1)
                        pe.wait_ge(ya_done[u % 2], it * (U // 2) + u // 2)
                        for g, (first, count) in enumerate(GROUPS[i]):
                            f = FIRST[u] + g
                            pe.wait_ge(turned_out[f % 2], it * (PER // 2) + f // 2 + 1)
                            for j in range(first, first + count):
                                ins = nc.tensor.matmul(out[u % 2][:, 0:D], pT[u % 2][:, j, :], va[s][:, j, :],
                                                       start=j == 0, stop=j == i)
                        ins.then_inc(mixed[u % 2], 1)

            @block.scalar
            def _(act):
                with act.Fori(0, B // 2) as it:
                    for u in range(U):
                        i = u % QT
                        act.wait_ge(max_done[u % 2], it * (U // 2) + u // 2 + 1)
                        act.wait_ge(mixed[u % 2], it * (U // 2) + u // 2)
                        act.wait_ge(inv_done[u % 2], it * (U // 2) + u // 2)
                        nc.scalar.activation(probs[u % 2][:, 0:(i + 1) * P], sc[u % 2][:, 0:(i + 1) * P], ACT.Exp,
                                             bias=negm[u % 2][:, :], accum_out=rowsum[u % 2][:, :])\
                            .then_inc(exp_done[u % 2], 1)

            @block.vector
            def _(dve):
                dve.wait_ge(const_set, 4)
                with dve.Fori(0, B // 2) as it:
                    def maximum(u):
                        i = u % QT
                        dve.wait_ge(scored[u % 2], it * (U // 2) + u // 2 + 1)
                        diag = sc[u % 2][:, i * P:(i + 1) * P]
                        nc.vector.tensor_tensor(diag, diag, mask[:, :], ALU.add).then_inc(masked[u % 2], 1)
                        dve.wait_ge(masked[u % 2], it * (U // 2) + u // 2 + 1)
                        nc.vector.tensor_reduce(negm[u % 2][:, :], sc[u % 2][:, 0:(i + 1) * P], AX.X, ALU.max,
                                                negate=True).then_inc(max_done[u % 2], 1)

                    def finish(u):
                        s, i = divmod(u, QT)
                        dve.wait_ge(mixed[u % 2], it * (U // 2) + u // 2 + 1)
                        dve.wait_ge(inv_done[u % 2], it * (U // 2) + u // 2 + 1)
                        dve.wait_ge(ya_stored[u % 2], (it * (U // 2) + u // 2) * 16)
                        nc.vector.scalar_tensor_tensor(ya[u % 2][:, :], out[u % 2][:, 0:D], inv[u % 2][:, :],
                                                       xx[s][:, i, :], ALU.mult, ALU.add).then_inc(ya_done[u % 2], 1)

                    maximum(0)
                    for u in range(U):
                        i = u % QT
                        if u + 1 < U:
                            maximum(u + 1)
                        dve.wait_ge(exp_done[u % 2], it * (U // 2) + u // 2 + 1)
                        dve.wait_ge(ya_done[u % 2], it * (U // 2) + u // 2)
                        nc.vector.reciprocal(inv[u % 2][:, :], rowsum[u % 2][:, :]).then_inc(inv_done[u % 2], 1)
                        for g, (first, count) in enumerate(GROUPS[i]):
                            f = FIRST[u] + g
                            dve.wait_ge(turned[f % 2], it * (PER // 2) + f // 2 + 1)
                            nc.vector.tensor_copy(pT[u % 2][:, first:first + count, :],
                                                  tp[f % 2][:, 0:count, :]).then_inc(turned_out[f % 2], 1)
                        if u >= 1:
                            finish(u - 1)
                    finish(U - 1)


def head_attention(nc, q_d, k_d, vh_d, ot_d):
    with ExitStack() as ctx:
        sb = lambda name, shape, dt=F32: ctx.enter_context(nc.sbuf_tensor(name, shape, dt))
        sem = lambda name: ctx.enter_context(nc.semaphore(name))
        sems = lambda name, n: [sem(f"{name}{i}") for i in range(n)]
        RING = 3
        STEPS = B * NG
        TURNS = (STEPS - 1) // RING
        assert TURNS * RING == STEPS - 1
        NQ = S // CH
        UNITS = NQ * QT
        FILLS = UNITS * GH
        ITEMS = GH * QT * NQ
        BANKS = 3
        LAST = UNITS - 2
        PR = 4
        LOADS = 2 * NT + 1
        SPLIT = 5
        q6 = [sb(f"h_q{i}", [P, GH, S], BF16) for i in range(RING)]
        k6 = [sb(f"h_k{i}", [P, GH, S], BF16) for i in range(RING)]
        vh = [sb(f"h_v{i}", [P, QT, GH, VW]) for i in range(RING)]
        probs = [sb(f"h_p{i}", [P, GH, CH]) for i in range(PR)]
        outT = [sb(f"h_o{i}", [P, CH]) for i in range(NQ)]
        ident = sb("h_ident", [P, P])
        halfmax = sb("h_halfmax", [P, ITEMS])
        negm = sb("h_negm", [P, GH * QT])
        mT = sb("h_mT", [GH * QT, P])
        mrest = sb("h_mrest", [GH * QT, P])
        mparts = sb("h_mparts", [GH * QT, SHIFT, P], BF16)
        bank = lambda name: ctx.enter_context(nc.psum_tensor(name, [P, CH], F32))
        sk = [bank(f"h_sk{i}") for i in range(BANKS)]
        sq = [bank(f"h_sq{i}") for i in range(BANKS)]
        po = bank("h_po")
        pm = bank("h_pm")

        const_set = sem("h_const_set")
        ones_set = sem("h_ones_set")
        loaded = sems("h_loaded", RING)
        shifted = sems("h_shifted", RING)
        scored = sem("h_scored")
        exp_done = sems("h_exp_done", BANKS)
        pv_done = sems("h_pv_done", PR)
        out_taken = sem("h_out_taken")
        stored = sems("h_stored", NQ)
        item_scored = sem("h_item_scored")
        item_max = sems("h_item_max", BANKS)
        max_done = sem("h_max_done")
        m_turned = sem("h_m_turned")
        m_split = sem("h_m_split")

        def items_before(w):
            return min(ITEMS, -(-ITEMS * w // LAST))

        begun = sem("h_begun")
        with nc.Block() as block:

            @block.gpsimd
            def _(pool):
                nc.gpsimd.memset(ident[:, :], 0.0).then_inc(const_set, 1)
                pool.wait_ge(const_set, 1)
                nc.gpsimd.affine_select(out=ident[:, :], in_=ident[:, :], compare_op=ALU.not_equal, fill=1.0,
                                        base=0, pattern=[[-1, P]], channel_multiplier=1).then_inc(const_set, 1)
                with pool.Fori(0, STEPS) as n:
                    for c in range(NQ):
                        pool.wait_ge(out_taken, n * NQ + c + 1)
                        pool.dma_start(ot_d[n, :, c * CH:(c + 1) * CH], outT[c][:, :]).then_inc(stored[c], 16)
                for c in range(NQ):
                    pool.wait_ge(stored[c], STEPS * 16)

            @block.sync
            def _(sp):
                wait = Waits(sp, begun)
                def load(n, r):
                    t0 = (n // NG) * S
                    h0 = (n % NG) * GH
                    if r is not n:
                        t0, h0 = sp.snap(t0), sp.snap(h0)
                        wait.ge(pv_done[(UNITS - 1) % PR], (n - RING + 1) * (UNITS // PR))
                    for t in range(NT):
                        for dst, src, term in ((q6, q_d, QTERM[t]), (k6, k_d, KTERM[t])):
                            sp.dma_start(dst[r][t * DH:(t + 1) * DH, :, :],
                                         src[term, bass.ds(h0 * DH, GH * DH), bass.ds(t0, S)]
                                         .rearrange("(h d) t -> d h t", d=DH)).then_inc(loaded[r], 16)
                    sp.dma_start(vh[r][:, :, :, :].rearrange("p j h w -> p j (h w)"),
                                 vh_d[bass.ds(t0, S), bass.ds(h0 * VW, GH * VW)]
                                 .rearrange("(j p) c -> p j c", p=P)).then_inc(loaded[r], 16)

                def shift(n, r):
                    wait.ge(m_split, n * SPLIT + SPLIT)
                    for j in range(SHIFT):
                        sp.dma_start(q6[r][DOTS + j:DOTS + j + 1, :, :].rearrange("p h t -> p (h t)"),
                                     mparts[:, j, :]).then_inc(shifted[r], 16)

                for n in range(RING - 1):
                    load(n, n)
                shift(0, 0)
                for first, turns in ((0, TURNS - 1), (TURNS - 1, 1)):
                    with sp.Fori(first, first + turns) as it:
                        for s in range(RING):
                            n = it * RING + s
                            if first == 0 or (TURNS - 1) * RING + s + RING - 1 < STEPS:
                                load(n + RING - 1, (s + RING - 1) % RING)
                            shift(n + 1, (s + 1) % RING)

            @block.tensor
            def _(pe):
                pe.wait_ge(const_set, 2)
                pe.wait_ge(ones_set, RING)

                def item(it, place, m):
                    h, i, half = m // (QT * NQ), m // NQ % QT, m % NQ
                    f = ITEMS * place + m
                    r = place % RING
                    pe.wait_ge(item_max[f % BANKS], it * ITEMS + f // BANKS)
                    nc.tensor.matmul(sq[f % BANKS][:, :], q6[r][0:DOTS, h, i * P:(i + 1) * P],
                                     k6[r][0:DOTS, h, half * CH:(half + 1) * CH],
                                     start=True, stop=True).then_inc(item_scored, 1)

                def turn_maxima(it, place):
                    n = it * RING + place
                    pe.wait_ge(max_done, n + 1)
                    pe.wait_ge(m_split, n * SPLIT)
                    nc.tensor.transpose(pm[0:GH * QT, 0:P], negm[:, :], ident[:, :]).then_inc(m_turned, 1)

                def mix(it, place, w):
                    c, j = divmod(w, QT)
                    if j == 0:
                        pe.wait_ge(out_taken, (it * RING + place) * NQ + c)
                    last = FILLS * place + GH * w + GH - 1
                    for b in range(BANKS):
                        f = last - (last - b) % BANKS
                        pe.wait_ge(exp_done[b], it * FILLS + f // BANKS + 1)
                    for h in range(GH):
                        ins = nc.tensor.matmul(po[h * VW:(h + 1) * VW, :], vh[place % RING][:, j, h, :],
                                               probs[w % PR][:, h, :], start=j == 0, stop=j == QT - 1)
                    ins.then_inc(pv_done[w % PR], 1)

                def step(it, place, follow):
                    r = place
                    pe.wait_ge(shifted[r], (it + 1) * SHIFT * 16)
                    if follow:
                        pe.wait_ge(loaded[(r + 1) % RING], (it + (place + 1) // RING + 1) * LOADS * 16)
                    m = 0
                    for w in range(UNITS):
                        c, j = divmod(w, QT)
                        for h in range(GH):
                            f = FILLS * place + GH * w + h
                            pe.wait_ge(exp_done[f % BANKS], it * FILLS + f // BANKS)
                            nc.tensor.matmul(sk[f % BANKS][:, :], k6[r][0:DOTS + SHIFT, h, j * P:(j + 1) * P],
                                             q6[r][0:DOTS + SHIFT, h, c * CH:(c + 1) * CH],
                                             start=True, stop=True).then_inc(scored, 1)
                            if follow:
                                now = items_before(w + 1) - items_before(w)
                                while m < items_before(w) + -(-now * (h + 1) // GH):
                                    item(it, place + 1, m)
                                    m += 1
                        if w:
                            mix(it, place, w - 1)
                        if w == LAST and follow:
                            turn_maxima(it, place + 1)
                    mix(it, place, UNITS - 1)

                pe.wait_ge(loaded[0], LOADS * 16)
                for m in range(ITEMS):
                    item(0, 0, m)
                turn_maxima(0, 0)
                with pe.Fori(0, TURNS) as it:
                    for place in range(RING):
                        step(it, place, True)
                step(TURNS, 0, False)

            @block.scalar
            def _(act):
                def step(it, place):
                    n = it * RING + place
                    for w in range(UNITS):
                        act.wait_ge(pv_done[w % PR], n * (UNITS // PR) + w // PR)
                        for h in range(GH):
                            f = FILLS * place + GH * w + h
                            act.wait_ge(scored, it * (RING * FILLS) + f + 1)
                            nc.scalar.activation(probs[w % PR][:, h, :], sk[f % BANKS][:, :], ACT.Exp,
                                                 scale=DH ** -0.5).then_inc(exp_done[f % BANKS], 1)
                        if w == QT:
                            take_out(n, 0)
                    take_out(n, 1)

                def take_out(n, c):
                    w = (c + 1) * QT - 1
                    act.wait_ge(pv_done[w % PR], n * (UNITS // PR) + w // PR + 1)
                    act.wait_ge(stored[c], n * 16)
                    nc.scalar.activation(outT[c][:, :], po[:, :], ACT.Copy).then_inc(out_taken, 1)

                with act.Fori(0, TURNS) as it:
                    for place in range(RING):
                        step(it, place)
                step(TURNS, 0)

            @block.vector
            def _(dve):
                for i in range(RING):
                    nc.vector.memset(k6[i][DOTS:P, :, :].rearrange("p h t -> p (h t)"), 1.0).then_inc(ones_set, 1)

                def maxima(it, place):
                    for m in range(ITEMS):
                        f = ITEMS * place + m
                        dve.wait_ge(item_scored, it * (RING * ITEMS) + f + 1)
                        nc.vector.tensor_reduce(halfmax[:, m:m + 1], sq[f % BANKS][:, :], AX.X, ALU.max)\
                            .then_inc(item_max[f % BANKS], 1)

                def split(it, place):
                    n = it * RING + place
                    last = ITEMS * place + ITEMS - 1
                    for b in range(BANKS):
                        f = last - (last - b) % BANKS
                        dve.wait_ge(item_max[b], it * ITEMS + f // BANKS + 1)
                    nc.vector.tensor_reduce(negm[:, :], halfmax[:, :].rearrange("p (t a) -> p t a", a=NQ),
                                            AX.X, ALU.max, negate=True).then_inc(max_done, 1)
                    dve.wait_ge(m_turned, n + 1)
                    nc.vector.tensor_copy(mT[:, :], pm[0:GH * QT, 0:P]).then_inc(m_split, 1)
                    dve.wait_ge(m_split, n * SPLIT + 1)
                    if place:
                        dve.wait_ge(shifted[place - 1], (it + 1) * SHIFT * 16)
                    nc.vector.tensor_copy(mparts[:, 0, :], mT[:, :]).then_inc(m_split, 1)
                    dve.wait_ge(m_split, n * SPLIT + 2)
                    nc.vector.tensor_tensor(mrest[:, :], mT[:, :], mparts[:, 0, :], ALU.subtract).then_inc(m_split, 1)
                    dve.wait_ge(m_split, n * SPLIT + 3)
                    nc.vector.tensor_copy(mparts[:, 1, :], mrest[:, :]).then_inc(m_split, 1)
                    dve.wait_ge(m_split, n * SPLIT + 4)
                    nc.vector.tensor_tensor(mparts[:, 2, :], mrest[:, :], mparts[:, 1, :], ALU.subtract)\
                        .then_inc(m_split, 1)

                maxima(0, 0)
                split(0, 0)
                with dve.Fori(0, TURNS) as it:
                    for place in range(RING):
                        maxima(it, place + 1)
                        split(it, place + 1)


def feed_forward(nc, ot_d, xn_d, ya_d, w_o, ws_in, ws_out, w1, w2, w_g, w_e, b_g, b_e, n1_w, n2_w, out):
    with ExitStack() as ctx:
        sb = lambda name, shape, dt=F32: ctx.enter_context(nc.sbuf_tensor(name, shape, dt))
        sem = lambda name: ctx.enter_context(nc.semaphore(name))
        sems = lambda name, n=2: [sem(f"{name}{s}") for s in range(n)]
        two = lambda name, shape, dt=F32: [sb(f"{name}{s}", shape, dt) for s in range(2)]
        KH = HID // P
        R = 2 + E
        TURNS = NCH // 2 - 1
        wo = sb("f_wo", [P, KD, D])
        wsi = sb("f_wsi", [P, KD, 2 * HID])
        wsi1 = sb("f_w1", [P, KD, 2 * HID])
        wso = sb("f_wso", [P, KH, D])
        w2s = sb("f_w2", [P, E, KH, D])
        wr = sb("f_wr", [P, KD, R])
        bias = sb("f_bias", [P, 1, R])
        n1 = sb("f_n1", [P, D])
        n2 = sb("f_n2", [P, D])
        ident = sb("f_ident", [P, P])
        before = sb("f_before", [P, 1, E * E])
        val = two("f_val", [P, KD, CH])
        tot = two("f_tot", [P, KD, CH])
        itot = sb("f_itot", [P, KD, CH])
        saT = sb("f_saT", [P, KD, CH])
        xn = two("f_xn", [P, TPC, D])
        ya = two("f_ya", [P, TPC, D])
        xs = sb("f_xs", [P, TPC, D])
        sq = sb("f_sq", [P, D])
        ss = sb("f_ss", [P, TPC])
        ms = sb("f_ms", [P, TPC])
        sd = sb("f_sd", [P, TPC])
        rstd = sb("f_rstd", [P, TPC])
        x1 = two("f_x1", [P, TPC, D])
        x1T = two("f_x1T", [P, KD, CH])
        sil = two("f_sil", [P, CH])
        hs = two("f_hs", [P, KH, CH])
        h1 = two("f_h1", [P, KH, CH])
        lg = sb("f_lg", [P, TPC, R])
        gmax = sb("f_gmax", [P, TPC, 1])
        emax = sb("f_emax", [P, TPC, 2])
        ex = sb("f_ex", [P, TPC, R])
        exs = sb("f_exs", [P, TPC, R])
        gsum = sb("f_gsum", [P, TPC, 1])
        esum = sb("f_esum", [P, TPC, 2])
        ginv = sb("f_ginv", [P, TPC, 1])
        einv = sb("f_einv", [P, TPC, 2])
        gp = sb("f_gp", [P, TPC, 2])
        pe_ = sb("f_pe", [P, TPC, E])
        gt = sb("f_gt", [P, TPC, E, E])
        ge = sb("f_ge", [P, TPC, E, E])
        rank = sb("f_rank", [P, TPC, E])
        wt = two("f_wt", [P, TPC, E])
        acc = two("f_acc", [P, TPC, D])
        fin = two("f_fin", [P, TPC, D])
        sq2 = sb("f_sq2", [P, D])
        ss2 = sb("f_ss2", [P, TPC])
        ms2 = sb("f_ms2", [P, TPC])
        sd2 = sb("f_sd2", [P, TPC])
        rstd2 = sb("f_rstd2", [P, TPC])
        pair = [ctx.enter_context(nc.psum_tensor(f"f_pair{i}", [P, 2, CH], F32)) for i in range(2)]
        ob = [ctx.enter_context(nc.psum_tensor(f"f_ob{i}", [P, CH], F32)) for i in range(4)]
        FILLS = 3 + 2 * KH
        OUTS = E // 2 + 1

        weights = sem("f_weights")
        const_set = sem("f_const_set")
        loaded = sems("f_loaded")
        sa_done = sems("f_sa_done")
        made = sem("f_made")
        free = sems("f_free")
        squared = sem("f_squared")
        ms_done = sem("f_ms_done")
        sd_done = sem("f_sd_done")
        x1_done = sems("f_x1_done")
        logits = sem("f_logits")
        exped = sem("f_exped")
        sil_done = sems("f_sil_done")
        routed = sems("f_routed")
        tile_made = sem("f_tile_made")
        tile_free = sems("f_tile_free", 4)
        squared2 = sem("f_squared2")
        ms2_done = sem("f_ms2_done")
        sd2_done = sem("f_sd2_done")
        fin_done = sems("f_fin_done")
        stored = sems("f_stored")
        chain = sem("f_chain")
        FRONT, BACK = 20, TPC * E // 2 + 2

        begun = sem("f_begun")
        with nc.Block() as block:

            @block.gpsimd
            def _(pool):
                nc.gpsimd.memset(ident[:, :], 0.0).then_inc(const_set, 1)
                nc.gpsimd.memset(before[:, :, :].rearrange("p o n -> p (o n)"), 1.0).then_inc(const_set, 1)
                pool.wait_ge(const_set, 2)
                nc.gpsimd.affine_select(out=ident[:, :], in_=ident[:, :], compare_op=ALU.not_equal, fill=1.0,
                                        base=0, pattern=[[-1, P]], channel_multiplier=1).then_inc(const_set, 1)
                b2 = before[:, 0, :].rearrange("p (e j) -> p e j", j=E)
                nc.gpsimd.affine_select(out=b2, in_=b2, compare_op=ALU.is_gt, fill=0.0,
                                        base=0, pattern=[[1, E], [-1, E]], channel_multiplier=0).then_inc(const_set, 1)

            @block.sync
            def _(sp):
                wait = Waits(sp, begun)
                fan = lambda v: v.rearrange("(o n) -> o n", o=1).broadcast_to([P, v.shape[0]])
                part = lambda w: w.rearrange("(k p) m -> p k m", p=P)
                for dst, src in ((wo[:, :, :], part(w_o)), (n1[:, :], fan(n1_w)), (n2[:, :], fan(n2_w)),
                                 (wr[:, :, 0:2], part(w_g)), (wr[:, :, 2:R], part(w_e)),
                                 (bias[:, 0, 0:2], fan(b_g)), (bias[:, 0, 2:R], fan(b_e)),
                                 (wsi1[:, :, :], part(w1)), (wsi[:, :, :], part(ws_in)),
                                 (wso[:, :, :], part(ws_out)),
                                 (w2s[:, :, :, :], w2.rearrange("e (k p) m -> p e k m", p=P))):
                    sp.dma_start(dst, src).then_inc(weights, 16)

                def load(it, place):
                    c = it * 2 + place
                    s = place % 2
                    rows = lambda a: a[bass.ds(c * CH, CH), :].rearrange("(j p) d -> p j d", p=P)
                    for m in range(KD):
                        for g in range(2):
                            src = ot_d[(c // 2) * NG + 2 * m + g, :, bass.ds((c % 2) * CH, CH)]\
                                .rearrange("(h w) t -> h w t", w=VW)
                            at = slice(g * P // 2, (g + 1) * P // 2)
                            sp.dma_start(val[s][at, m, :], src[:, 0:DH, :]).then_inc(loaded[s], 16)
                            sp.dma_start(tot[s][at, m, :], src[:, DH:VW, :]).then_inc(loaded[s], 16)
                    sp.dma_start(xn[s][:, :, :], rows(xn_d)).then_inc(loaded[s], 16)
                    sp.dma_start(ya[s][:, :, :], rows(ya_d)).then_inc(loaded[s], 16)

                def store(it, place):
                    s = place % 2
                    wait.ge(fin_done[s], it + 1)
                    sp.dma_start(out[bass.ds((it * 2 + place) * CH, CH), :].rearrange("(j p) d -> p j d", p=P),
                                 fin[s][:, :, :]).then_inc(stored[s], 16)

                load(0, 0)
                load(0, 1)
                with sp.Fori(0, TURNS) as it:
                    for s in range(2):
                        store(it, s)
                        load(it, s + 2)
                for s in range(2):
                    store(TURNS, s)
                for s in range(2):
                    sp.wait_ge(stored[s], (TURNS + 1) * 16)

            LOADS = 4 * KD + 2
            pair_at = lambda place, j: (FILLS * place + j) % 2
            uses = lambda it, place, j: it * FILLS + (FILLS * place + j) // 2
            fills = lambda it, place, j: it * 2 * FILLS + FILLS * place + j
            WO, XT, GATE, HIDDEN = 0, 1, 2, 3

            def hidden_done(eng, it, place, f):
                for j in (HIDDEN + f - 1, HIDDEN + f):
                    eng.wait_ge(free[pair_at(place, j)], uses(it, place, j) + 1)

            def out_at(it, place, j, g):
                f = OUTS * (TPC * place + j) + g
                return f % 4, it * (2 * OUTS * TPC // 4) + f // 4

            @block.tensor
            def _(pe):
                def begin(it, place, j):
                    pe.wait_ge(free[pair_at(place, j)], uses(it, place, j))
                    return pair[pair_at(place, j)]

                def out_projection(it, place):
                    pe.wait_ge(sa_done[place % 2], it + place // 2 + 1)
                    ps = begin(it, place, WO)
                    for j in range(TPC):
                        for k in range(KD):
                            ins = nc.tensor.matmul(ps[:, j // 2, (j % 2) * D:(j % 2 + 1) * D],
                                                   saT[:, k, j * P:(j + 1) * P], wo[:, k, :],
                                                   start=k == 0, stop=k == KD - 1)
                    ins.then_inc(made, 1)

                def turn(it, place):
                    s = place % 2
                    pe.wait_ge(x1_done[s], it + place // 2 + 1)
                    ps = begin(it, place, XT)
                    for m in range(KD):
                        for j in range(TPC):
                            ins = nc.tensor.transpose(ps[:, m, j * P:(j + 1) * P],
                                                      x1[s][:, j, m * P:(m + 1) * P], ident[:, :])
                    ins.then_inc(made, 1)

                def gates(it, place):
                    s = place % 2
                    pe.wait_ge(free[pair_at(place, XT)], uses(it, place, XT) + 1)
                    ps = begin(it, place, GATE)
                    for j in range(TPC):
                        for k in range(KD):
                            ins = nc.tensor.matmul(ps[:, 0, j * R:(j + 1) * R], x1T[s][:, k, j * P:(j + 1) * P],
                                                   wr[:, k, :], start=k == 0, stop=k == KD - 1)
                    ins.then_inc(made, 1)

                def hidden(it, place):
                    s = place % 2
                    for f in range(2 * KH):
                        w = wsi1 if f < KH else wsi
                        ps = begin(it, place, HIDDEN + f)
                        for half in range(2):
                            at = half * HID + f % KH * P
                            for k in range(KD):
                                ins = nc.tensor.matmul(ps[:, half, :], w[:, k, at:at + P], x1T[s][:, k, :],
                                                       start=k == 0, stop=k == KD - 1)
                        ins.then_inc(made, 1)

                def outputs(it, place, j):
                    s = place % 2
                    for g in range(OUTS):
                        b, used = out_at(it, place, j, g)
                        pe.wait_ge(tile_free[b], used)
                        if g == 0 and j == 0:
                            hidden_done(pe, it, place, KH - 1)
                        if g == OUTS - 1 and j == 0:
                            hidden_done(pe, it, place, 2 * KH - 1)
                        for k in range(KH):
                            if g < OUTS - 1:
                                ins = nc.tensor.matmul(ob[b][:, :], h1[s][:, k, j * P:(j + 1) * P],
                                                       w2s[:, 2 * g:2 * g + 2, k, :],
                                                       start=k == 0, stop=k == KH - 1)
                            else:
                                ins = nc.tensor.matmul(ob[b][:, 0:D], hs[s][:, k, j * P:(j + 1) * P],
                                                       wso[:, k, :], start=k == 0, stop=k == KH - 1)
                        ins.then_inc(tile_made, 1)

                def step(it, place, follow):
                    outputs(it, place, 0)
                    if follow:
                        out_projection(it, place + 1)
                    outputs(it, place, 1)
                    outputs(it, place, 2)
                    if follow:
                        turn(it, place + 1)
                    outputs(it, place, 3)
                    if follow:
                        gates(it, place + 1)
                        hidden(it, place + 1)

                pe.wait_ge(weights, 11 * 16)
                pe.wait_ge(const_set, 4)
                out_projection(0, 0)
                turn(0, 0)
                gates(0, 0)
                hidden(0, 0)
                with pe.Fori(0, TURNS) as it:
                    for s in range(2):
                        step(it, s, True)
                step(TURNS, 0, True)
                step(TURNS, 1, False)

            @block.scalar
            def _(act):
                def squares(it, place):
                    n = it * 2 + place
                    act.wait_ge(free[pair_at(place, WO)], uses(it, place, WO) + 1)
                    for j in range(TPC):
                        nc.scalar.activation(sq[:, :], xs[:, j, :], ACT.Square,
                                             accum_out=ss[:, j:j + 1]).then_inc(squared, 1)
                        act.wait_ge(squared, n * TPC + j + 1)
                    act.wait_ge(ms_done, n + 1)
                    nc.scalar.activation(sd[:, :], ms[:, :], ACT.Sqrt).then_inc(sd_done, 1)

                def take_turned(it, place):
                    act.wait_ge(made, fills(it, place, XT) + 1)
                    nc.scalar.activation(x1T[place % 2][:, :, :], pair[pair_at(place, XT)][:, :, :], ACT.Copy)\
                        .then_inc(free[pair_at(place, XT)], 1)

                def hidden(it, place):
                    n = it * 2 + place
                    act.wait_ge(logits, n + 1)
                    nc.scalar.activation(ex[:, :, :], exs[:, :, :], ACT.Exp).then_inc(exped, 1)
                    for f in range(2 * KH):
                        act.wait_ge(made, fills(it, place, HIDDEN + f) + 1)
                        j, before = (HIDDEN + f - 2, place) if f >= 2 else (HIDDEN + f - 2 + 2 * KH, place - 1)
                        act.wait_ge(free[pair_at(before, j)], uses(it, before, j) + 1)
                        nc.scalar.activation(sil[f % 2][:, :], pair[pair_at(place, HIDDEN + f)][:, 0, :], ACT.Silu)\
                            .then_inc(sil_done[f % 2], 1)

                def final(it, place):
                    n = it * 2 + place
                    s = place % 2
                    b, used = out_at(it, place, TPC - 1, OUTS - 1)
                    act.wait_ge(tile_free[b], used + 1)
                    for j in range(TPC):
                        nc.scalar.activation(sq2[:, :], acc[s][:, j, :], ACT.Square,
                                             accum_out=ss2[:, j:j + 1]).then_inc(squared2, 1)
                        act.wait_ge(squared2, n * TPC + j + 1)
                    act.wait_ge(ms2_done, n + 1)
                    nc.scalar.activation(sd2[:, :], ms2[:, :], ACT.Sqrt).then_inc(sd2_done, 1)

                def step(it, place, follow):
                    if follow:
                        squares(it, place + 1)
                        take_turned(it, place + 1)
                        hidden(it, place + 1)
                    final(it, place)

                squares(0, 0)
                take_turned(0, 0)
                hidden(0, 0)
                with act.Fori(0, TURNS) as it:
                    for s in range(2):
                        step(it, s, True)
                step(TURNS, 0, True)
                step(TURNS, 1, False)

            @block.vector
            def _(dve):
                dve.wait_ge(weights, 11 * 16)
                dve.wait_ge(const_set, 4)

                class Links:

                    def __init__(self, base):
                        self.base, self.n = base, 0

                    def __call__(self, ins):
                        self.n += 1
                        ins.then_inc(chain, 1)
                        dve.wait_ge(chain, self.base + self.n)

                def head(it, place, link):
                    s = place % 2
                    dve.wait_ge(loaded[s], (it + place // 2 + 1) * LOADS * 16)
                    link(nc.vector.reciprocal(itot[:, :, :], tot[s][:, :, :]))
                    nc.vector.tensor_tensor(saT[:, :, :], val[s][:, :, :], itot[:, :, :], ALU.mult)\
                        .then_inc(sa_done[s], 1)

                def residual(it, place, link):
                    s = place % 2
                    dve.wait_ge(made, fills(it, place, WO) + 1)
                    nc.vector.tensor_tensor(xs[:, :, :].rearrange("p j d -> p (j d)"),
                                            pair[pair_at(place, WO)][:, :, :].rearrange("p a b -> p (a b)"),
                                            xn[s][:, :, :].rearrange("p j d -> p (j d)"), ALU.add)\
                        .then_inc(free[pair_at(place, WO)], 1)

                def normalise(it, place, link):
                    n = it * 2 + place
                    s = place % 2
                    dve.wait_ge(squared, n * TPC + TPC)
                    nc.vector.tensor_scalar(ms[:, :], ss[:, :], 1.0 / D, RMS_EPS, ALU.mult, ALU.add)\
                        .then_inc(ms_done, 1)
                    dve.wait_ge(sd_done, n + 1)
                    link(nc.vector.reciprocal(rstd[:, :], sd[:, :]))
                    for j in range(TPC):
                        ins = nc.vector.scalar_tensor_tensor(x1[s][:, j, :], xs[:, j, :], rstd[:, j:j + 1], n1[:, :],
                                                             ALU.mult, ALU.mult)
                    ins.then_inc(x1_done[s], 1)

                def route(it, place, link):
                    s = place % 2
                    ps = pair[pair_at(place, GATE)]
                    done = uses(it, place, GATE) + 1
                    four = [P, TPC, E, E]
                    dve.wait_ge(made, fills(it, place, GATE) + 1)
                    nc.vector.tensor_tensor(lg[:, :, :], ps[:, 0, 0:TPC * R].rearrange("p (j r) -> p j r", r=R),
                                            bias[:, :, :].broadcast_to([P, TPC, R]), ALU.add)\
                        .then_inc(free[pair_at(place, GATE)], 1)
                    dve.wait_ge(free[pair_at(place, GATE)], done)
                    link(nc.vector.tensor_reduce(gmax[:, :, 0], lg[:, :, 0:2], AX.X, ALU.max))
                    for g in range(2):
                        link(nc.vector.tensor_reduce(emax[:, :, g], lg[:, :, 2 + g * EPG:2 + (g + 1) * EPG],
                                                     AX.X, ALU.max))
                    nc.vector.tensor_tensor(exs[:, :, 0:2], lg[:, :, 0:2], gmax[:, :, :].broadcast_to([P, TPC, 2]),
                                            ALU.subtract)
                    for g in range(2):
                        at = slice(2 + g * EPG, 2 + (g + 1) * EPG)
                        ins = nc.vector.tensor_tensor(exs[:, :, at], lg[:, :, at],
                                                      emax[:, :, g:g + 1].broadcast_to([P, TPC, EPG]), ALU.subtract)
                    ins.then_inc(logits, 1)
                    dve.wait_ge(exped, it * 2 + place + 1)
                    link(nc.vector.tensor_reduce(gsum[:, :, 0], ex[:, :, 0:2], AX.X, ALU.add))
                    link(nc.vector.tensor_reduce(esum[:, :, :],
                                                 ex[:, :, 2:R].rearrange("p t (g e) -> p t g e", g=2), AX.X, ALU.add))
                    link(nc.vector.reciprocal(ginv[:, :, :], gsum[:, :, :]))
                    link(nc.vector.reciprocal(einv[:, :, :], esum[:, :, :]))
                    link(nc.vector.tensor_tensor(gp[:, :, 0], ex[:, :, 0], ex[:, :, 1], ALU.is_ge))
                    link(nc.vector.tensor_scalar(gp[:, :, 1], gp[:, :, 0], -1.0, 1.0, ALU.mult, ALU.add))
                    link(nc.vector.tensor_tensor(gp[:, :, :], gp[:, :, :], ginv[:, :, :].broadcast_to([P, TPC, 2]),
                                                 ALU.mult))
                    link(nc.vector.tensor_tensor(gp[:, :, :], gp[:, :, :], einv[:, :, :], ALU.mult))
                    for g in range(2):
                        at = slice(g * EPG, (g + 1) * EPG)
                        link(nc.vector.tensor_tensor(pe_[:, :, at], ex[:, :, 2 + g * EPG:2 + (g + 1) * EPG],
                                                     gp[:, :, g:g + 1].broadcast_to([P, TPC, EPG]), ALU.mult))
                    theirs = pe_[:, :, :].unsqueeze(2).broadcast_to(four)
                    own = pe_[:, :, :].unsqueeze(3).broadcast_to(four)
                    link(nc.vector.tensor_tensor(gt[:, :, :, :], theirs, own, ALU.is_gt))
                    link(nc.vector.tensor_tensor(ge[:, :, :, :], theirs, own, ALU.is_ge))
                    flat = lambda a: a[:, :, :, :].rearrange("p t e j -> p t (e j)")
                    link(nc.vector.tensor_tensor(flat(ge), flat(ge), before[:, :, :].broadcast_to([P, TPC, E * E]),
                                                 ALU.mult))
                    link(nc.vector.tensor_tensor(flat(gt), flat(gt), flat(ge), ALU.max))
                    link(nc.vector.tensor_reduce(rank[:, :, :], gt[:, :, :, :], AX.X, ALU.add))
                    nc.vector.scalar_tensor_tensor(wt[s][:, :, :], rank[:, :, :], 2.0, pe_[:, :, :],
                                                   ALU.is_lt, ALU.mult).then_inc(routed[s], 1)

                def gate_hidden(it, place, link):
                    s = place % 2
                    for f in range(2 * KH):
                        p = pair_at(place, HIDDEN + f)
                        dve.wait_ge(sil_done[f % 2], (it * 2 + place) * KH + f // 2 + 1)
                        nc.vector.tensor_tensor((h1 if f < KH else hs)[s][:, f % KH, :], sil[f % 2][:, :],
                                                pair[p][:, 1, :], ALU.mult).then_inc(free[p], 1)

                def sums(it, place, j, link):
                    s = place % 2
                    if j == 0:
                        dve.wait_ge(routed[s], it + place // 2 + 1)
                    for g in range(OUTS):
                        b, used = out_at(it, place, j, g)
                        dve.wait_ge(tile_made, (it * 2 + place) * TPC * OUTS + OUTS * j + g + 1)
                        if g < OUTS - 1:
                            link(nc.vector.scalar_tensor_tensor(
                                acc[s][:, j, :], ob[b][:, 0:D], wt[s][:, j, 2 * g:2 * g + 1],
                                acc[s][:, j, :] if g else x1[s][:, j, :], ALU.mult, ALU.add))
                            nc.vector.scalar_tensor_tensor(
                                acc[s][:, j, :], ob[b][:, D:2 * D], wt[s][:, j, 2 * g + 1:2 * g + 2],
                                acc[s][:, j, :], ALU.mult, ALU.add).then_inc(tile_free[b], 1)
                        else:
                            nc.vector.tensor_tensor(acc[s][:, j, :], ob[b][:, 0:D], acc[s][:, j, :], ALU.add)\
                                .then_inc(tile_free[b], 1)
                        dve.wait_ge(tile_free[b], used + 1)

                def final(it, place, link):
                    n = it * 2 + place
                    s = place % 2
                    dve.wait_ge(squared2, n * TPC + TPC)
                    nc.vector.tensor_scalar(ms2[:, :], ss2[:, :], 1.0 / D, RMS_EPS, ALU.mult, ALU.add)\
                        .then_inc(ms2_done, 1)
                    dve.wait_ge(sd2_done, n + 1)
                    link(nc.vector.reciprocal(rstd2[:, :], sd2[:, :]))
                    for j in range(TPC):
                        ins = nc.vector.scalar_tensor_tensor(acc[s][:, j, :], acc[s][:, j, :], rstd2[:, j:j + 1],
                                                             n2[:, :], ALU.mult, ALU.mult)
                    link(ins)
                    dve.wait_ge(stored[s], (it + place // 2) * 16)
                    nc.vector.tensor_tensor(fin[s][:, :, :], acc[s][:, :, :], ya[s][:, :, :], ALU.add)\
                        .then_inc(fin_done[s], 1)

                def front(it, place, link):
                    for part in (head, residual, normalise, route, gate_hidden):
                        part(it, place, link)

                def step(it, place, link, follow):
                    if follow:
                        head(it, place + 1, link)
                    sums(it, place, 0, link)
                    if follow:
                        residual(it, place + 1, link)
                    sums(it, place, 1, link)
                    if follow:
                        normalise(it, place + 1, link)
                    sums(it, place, 2, link)
                    sums(it, place, 3, link)
                    if follow:
                        route(it, place + 1, link)
                        gate_hidden(it, place + 1, link)
                    final(it, place, link)

                link = Links(0)
                front(0, 0, link)
                assert link.n == FRONT, link.n
                with dve.Fori(0, TURNS) as it:
                    link = Links(it * (2 * (FRONT + BACK)) + FRONT)
                    for s in range(2):
                        step(it, s, link, True)
                    assert link.n == 2 * (FRONT + BACK), link.n
                link = Links(TURNS * 2 * (FRONT + BACK) + FRONT)
                step(TURNS, 0, link, True)
                step(TURNS, 1, link, False)


def layer(nc, x, w_kv_t, w_q, w_kc, w_vc, w_k, w_v, w_o, ws_in, ws_out, w1, w2, w_g, w_e, b_g, b_e, n1_w, n2_w,
          rope_cos, rope_sin, out):
    dram = lambda name, shape, dt=F32: nc.dram_tensor(name, shape, dt, kind="Internal").ap()
    tokens = x.rearrange("b s d -> (b s) d")
    xn_d = dram("xn_d", (N, D))
    xx_d = dram("xx_d", (N, D))
    xnT_d = dram("xnT_d", (D, N))
    kaT_d = dram("kaT_d", (D, N))
    va_d = dram("va_d", (N, D))
    vh_d = dram("vh_d", (N, H * VW))
    q_d = dram("q_d", (3, D, N), BF16)
    k_d = dram("k_d", (3, D, N), BF16)
    ya_d = dram("ya_d", (N, D))
    ot_d = dram("ot_d", (B * NG, P, S))
    project(nc, tokens, w_kv_t, w_q, w_kc, w_vc, w_k, w_v, rope_cos, rope_sin,
            xn_d, xx_d, xnT_d, kaT_d, va_d, vh_d, q_d, k_d)
    causal_attention(nc, xnT_d, kaT_d, va_d, xx_d, ya_d)
    head_attention(nc, q_d, k_d, vh_d, ot_d)
    feed_forward(nc, ot_d, xn_d, ya_d, w_o, ws_in, ws_out, w1, w2, w_g, w_e, b_g, b_e, n1_w, n2_w,
                 out.rearrange("b s d -> (b s) d"))


def rope_tables():
    import numpy as np
    inv = (1.0 / np.float32(10000.0) ** (np.arange(0, DH, 2, dtype=np.float32) / np.float32(DH))).astype(np.float32)
    angle = (np.arange(S, dtype=np.float32)[None, :] * inv[:, None]).astype(np.float32)
    row = np.arange(P) % DH
    sign = np.where(row % 2 == 0, -1.0, 1.0).astype(np.float32)
    cos = np.cos(angle.astype(np.float64)).astype(np.float32)[row // 2]
    sin = np.sin(angle.astype(np.float64)).astype(np.float32)[row // 2] * sign[:, None]
    return np.ascontiguousarray(cos), np.ascontiguousarray(sin)


_INS = ["L0_attn_x", "L0_attn_W", "L0_ffn_Wq", "L0_ffn_Wk_c", "L0_ffn_Wv_c", "L0_ffn_Wk", "L0_ffn_Wv", "L0_ffn_Wo",
        "L0_ffn_W_shared_in", "L0_ffn_W_shared_out", "L0_ffn_W1_shared", "L0_ffn_W2_experts", "L0_ffn_Wg_gate",
        "L0_ffn_We_gate", "L0_ffn_group_bias", "L0_ffn_expert_bias", "L0_ffn_norm1_w", "L0_ffn_norm2_w"]


def kernel(**inputs):
    import numpy as np
    import concourse.bacc as bacc
    from concourse.bass_utils import run_bass_kernel_spmd

    nc = bacc.Bacc("TRN2", target_bir_lowering=False, num_devices=1)
    arrays = {}
    for name in _INS:
        a = np.asarray(inputs[name])
        arrays["in_" + name] = np.ascontiguousarray(a.T if name == "L0_attn_W" else a)
    arrays["in_rope_cos"], arrays["in_rope_sin"] = rope_tables()
    args = [nc.dram_tensor(n, a.shape, mybir.dt.from_np(a.dtype), kind="ExternalInput").ap()
            for n, a in arrays.items()]
    out = nc.dram_tensor("out_dram", (B, S, D), F32, kind="ExternalOutput").ap()
    layer(nc, *args, out)
    r = run_bass_kernel_spmd(nc, [arrays], core_ids=[0])
    return r.results[0]["out_dram"]
```

```python
import concourse.bass as bass
from concourse import mybir
from contextlib import ExitStack, contextmanager

F32 = mybir.dt.float32
BF16 = mybir.dt.bfloat16
F32R = mybir.dt.float32r
ACT = mybir.ActivationFunctionType
ALU = mybir.AluOpType
AX = mybir.AxisListType

P = 128
B, S, D = 4, 1024, 256
N = B * S
CH = 512
NCH = N // CH
TPC = CH // P
KD = D // P
H, DH = 16, 16
GH = 4
NG = H // GH
VW = 32
HID, E = 512, 8
EPG = 4
KH = HID // P
GATES = 2 + E
DC = D // 4
QT = S // P
LN_EPS, RMS_EPS = 1e-5, 1e-6
MASKED = -3.0e38
HI, LO = 0, 1
PASSES = ((HI, HI), (HI, LO), (LO, HI))
QTERM = (0, 0, 1, 0, 2, 1)
KTERM = (0, 1, 0, 2, 0, 1)
NT = len(QTERM)
DOTS = NT * DH
SHIFT = 3


@contextmanager
def stage_semaphores(nc):
    taken = []

    def take(name):
        taken.append(nc.alloc_semaphore(name))
        return taken[-1]

    yield take
    nc.clear_and_free_semaphores(taken)
    nc.all_engine_barrier()


class Waits:

    def __init__(self, sp, begun):
        self.sp, self.begun = sp, begun
        sp.sem_inc(begun, 1)

    def ge(self, sem, value):
        self.sp.wait_ge(self.begun, 1)
        self.sp.wait_ge(sem, value)


def project(nc, x, w_kv_t, w_q, w_kc, w_vc, w_k, w_v, rope_cos, rope_sin,
            xn_d, xx_d, xnT_d, kaT_d, va_d, vh_d, q_d, k_d):
    with ExitStack() as ctx:
        sb = lambda name, shape, dt=F32: ctx.enter_context(nc.sbuf_tensor(name, shape, dt))
        sem = ctx.enter_context(stage_semaphores(nc))
        sems = lambda name: [sem(f"{name}{s}") for s in range(2)]
        two = lambda name, shape, dt=F32: [sb(f"{name}{s}", shape, dt) for s in range(2)]
        wkv = sb("p_wkv", [P, KD, 2 * D])
        wq = sb("p_wq", [P, KD, D])
        wkvc = sb("p_wkvc", [P, KD, 2 * DC])
        wk = sb("p_wk", [P, D])
        wv = sb("p_wv", [P, D])
        cos = sb("p_cos", [P, 2, CH])
        sin = sb("p_sin", [P, 2, CH])
        ident = sb("p_ident", [P, P])
        xin = two("p_xin", [P, TPC, D])
        xn = two("p_xn", [P, TPC, D])
        xx = two("p_xx", [P, TPC, D])
        stats = sb("p_stats", [P, TPC, 6])
        fence = sb("p_fence", [P, 1])
        mv = sb("p_mv", [P, TPC, 2])
        veps = two("p_veps", [P, TPC])
        sd = two("p_sd", [P, TPC])
        rstd = sb("p_rstd", [P, TPC])
        xnT = two("p_xnT", [P, KD, CH])
        kaT = two("p_kaT", [P, KD, CH])
        va = two("p_va", [P, TPC, D])
        kvc = two("p_kvc", [P, CH])
        vh = two("p_vh", [P, TPC, H, VW])
        qk = sb("p_qk", [P, 2 * KD, CH])
        swap = sb("p_swap", [P, 2 * KD, CH])
        tcos = sb("p_tcos", [P, 2 * KD, CH])
        tsin = sb("p_tsin", [P, 2 * KD, CH])
        rot = sb("p_rot", [P, 2 * KD, CH])
        rest = sb("p_rest", [P, 2 * KD, CH])
        parts = two("p_parts", [P, 3, 2 * KD, CH], BF16)
        ps = [ctx.enter_context(nc.psum_tensor(f"p_ps{i}", [P, 2, CH], F32)) for i in range(4)]
        T, KA, VA, Q, KVC, K, V = range(7)
        BANKS = {T: 0, KVC: 1, KA: 2, VA: 3, Q: 0, K: 1, V: 2}

        weights = sem("p_weights")
        tables = sem("p_tables")
        ones_set = sem("p_ones_set")
        ident_set = sem("p_ident_set")
        x_in = sems("p_x_in")
        xn_done = sems("p_xn_done")
        xx_done = sems("p_xx_done")
        var_done = sems("p_var_done")
        sd_done = sems("p_sd_done")
        made = [sems(f"p_made{j}") for j in range(7)]
        taken = [sems(f"p_taken{j}") for j in range(7)]
        sw_done = sems("p_sw_done")
        sin_done = sems("p_sin_done")
        rot_done = sems("p_rot_done")
        hi_done = sems("p_hi_done")
        rest_done = sems("p_rest_done")
        mid_done = sems("p_mid_done")
        lo_done = sems("p_lo_done")
        st = {n: sems("p_st_" + n) for n in ("xn", "xx", "xnT", "kaT", "va", "vh", "parts")}
        chain = sem("p_chain")
        LINKS = 3
        TURNS = NCH // 2

        def near(it, s, d):
            return it + (s + d) // 2, (s + d) % 2

        def slots(eng, slot, after=0):
            for c in range(2):
                slot(0, c, c)
            with eng.Fori(1, TURNS - 1) as it:
                for s in range(2):
                    slot(it, s, None)
            for c in range(NCH - 2, NCH + after):
                slot(c // 2, c % 2, c)

        def exists(c, d):
            return c is None or 0 <= c + d < NCH

        begun = sem("p_begun")
        with nc.Block() as block:

            @block.gpsimd
            def _(pool):
                nc.gpsimd.memset(ident[:, :], 0.0).then_inc(ident_set, 1)
                pool.wait_ge(ident_set, 1)
                nc.gpsimd.affine_select(out=ident[:, :], in_=ident[:, :], compare_op=ALU.not_equal, fill=1.0,
                                        base=0, pattern=[[-1, P]], channel_multiplier=1).then_inc(ident_set, 1)
                pool.wait_ge(tables, 32)

                def add(it, s):
                    pool.wait_ge(xn_done[s], it + 1)
                    pool.wait_ge(st["xx"][s], it * 16)
                    nc.gpsimd.tensor_tensor(xx[s][:, :, :], xin[s][:, :, :], xn[s][:, :, :],
                                            ALU.add).then_inc(xx_done[s], 1)

                def sine(it, s):
                    pool.wait_ge(sw_done[s], it + 1)
                    for j in range(2 * KD):
                        last = nc.gpsimd.tensor_tensor(tsin[:, j, :], swap[:, j, :], sin[:, s, :], ALU.mult)
                    last.then_inc(sin_done[s], 1)

                def slot(it, s, c):
                    if exists(c, -1):
                        sine(*near(it, s, -1))
                    if exists(c, 1):
                        add(*near(it, s, 1))

                add(0, 0)
                slots(pool, slot, after=1)

            @block.sync
            def _(sp):
                wait = Waits(sp, begun)
                rows = lambda a, t0: a[bass.ds(t0, CH), :].rearrange("(j p) d -> p j d", p=P)
                cols = lambda a, t0: a[:, bass.ds(t0, CH)].rearrange("(m p) t -> p m t", p=P)

                def load(it, s):
                    t0 = (it * 2 + s) * CH
                    sp.dma_start(xin[s][:, :, :], rows(x, t0)).then_inc(x_in[s], 16)

                def store_norm(it, s):
                    t0 = (it * 2 + s) * CH
                    wait.ge(xn_done[s], it + 1)
                    sp.dma_start(rows(xn_d, t0), xn[s][:, :, :]).then_inc(st["xn"][s], 16)
                    wait.ge(xx_done[s], it + 1)
                    sp.dma_start(rows(xx_d, t0), xx[s][:, :, :]).then_inc(st["xx"][s], 16)

                def store_causal(it, s):
                    t0 = (it * 2 + s) * CH
                    wait.ge(taken[T][s], it + 1)
                    sp.dma_start(cols(xnT_d, t0), xnT[s][:, :, :]).then_inc(st["xnT"][s], 16)
                    wait.ge(taken[KA][s], it + 1)
                    sp.dma_start(cols(kaT_d, t0), kaT[s][:, :, :]).then_inc(st["kaT"][s], 16)
                    wait.ge(taken[VA][s], it + 1)
                    sp.dma_start(rows(va_d, t0), va[s][:, :, :]).then_inc(st["va"][s], 16)

                def store_values(it, s):
                    t0 = (it * 2 + s) * CH
                    wait.ge(taken[V][s], it + 1)
                    sp.dma_start(rows(vh_d, t0), vh[s][:, :, :, :].rearrange("p j h w -> p j (h w)"))\
                        .then_inc(st["vh"][s], 16)

                def store_parts(it, s):
                    t0 = (it * 2 + s) * CH
                    wait.ge(lo_done[s], it + 1)
                    for r in range(3):
                        sp.dma_start(cols(q_d[r], t0), parts[s][:, r, 0:KD, :]).then_inc(st["parts"][s], 16)
                        sp.dma_start(cols(k_d[r], t0), parts[s][:, r, KD:2 * KD, :]).then_inc(st["parts"][s], 16)

                def slot(it, s, c):
                    if exists(c, 2):
                        load(*near(it, s, 2))
                    if exists(c, 0):
                        store_causal(it, s)
                    if exists(c, -2):
                        store_parts(*near(it, s, -2))
                    if exists(c, 1):
                        store_norm(*near(it, s, 1))
                    if exists(c, 0):
                        store_values(it, s)

                load(0, 0)
                sp.dma_start(cos[:, :, :], rope_cos.rearrange("p (s n) -> p s n", s=2)).then_inc(tables, 16)
                sp.dma_start(sin[:, :, :], rope_sin.rearrange("p (s n) -> p s n", s=2)).then_inc(tables, 16)
                load(0, 1)
                store_norm(0, 0)
                slots(sp, slot, after=2)
                for name, each in st.items():
                    for s in range(2):
                        sp.wait_ge(each[s], NCH // 2 * (96 if name == "parts" else 16))

            @block.scalar
            def _(act):
                act.dma_start(wkv[:, :, :], w_kv_t.rearrange("(k p) m -> p k m", p=P)).then_inc(weights, 16)
                act.dma_start(wq[:, :, :], w_q.rearrange("(k p) m -> p k m", p=P)).then_inc(weights, 16)
                act.dma_start(wkvc[:, :, 0:DC], w_kc.rearrange("(k p) m -> p k m", p=P)).then_inc(weights, 16)
                act.dma_start(wkvc[:, :, DC:2 * DC], w_vc.rearrange("(k p) m -> p k m", p=P)).then_inc(weights, 16)
                act.wait_ge(ones_set, 2)
                act.dma_start(wk[0:DC, :], w_k).then_inc(weights, 16)
                act.dma_start(wv[DC:2 * DC, :], w_v).then_inc(weights, 16)
                def root(it, s):
                    act.wait_ge(var_done[s], it + 1)
                    nc.scalar.activation(sd[s][:, :], veps[s][:, :], ACT.Sqrt).then_inc(sd_done[s], 1)

                def take(it, s, j):
                    dst, src, stored = {
                        T: (xnT[s][:, :, :], ps[BANKS[T]][:, :, :], "xnT"),
                        KA: (kaT[s][:, :, :], ps[BANKS[KA]][:, :, :], "kaT"),
                        VA: (va[s][:, :, :].rearrange("p j d -> p (j d)"),
                             ps[BANKS[VA]][:, :, :].rearrange("p a b -> p (a b)"), "va"),
                        Q: (qk[:, 0:KD, :], ps[BANKS[Q]][:, :, :], None),
                        KVC: (kvc[s][:, :], ps[BANKS[KVC]][:, 0, :], None),
                        K: (qk[:, KD:2 * KD, :], ps[BANKS[K]][:, :, :], None),
                        V: (vh[s][:, :, :, 0:DH],
                            ps[BANKS[V]][:, :, :].rearrange("p a (b h d) -> p (a b) h d", h=H, d=DH), "vh")}[j]
                    act.wait_ge(made[j][s], it + 1)
                    if stored:
                        act.wait_ge(st[stored][s], it * 16)
                    nc.scalar.activation(dst, src, ACT.Copy).then_inc(taken[j][s], 1)

                def high(it, s):
                    act.wait_ge(rot_done[s], it + 1)
                    act.wait_ge(st["parts"][s], it * 96)
                    nc.scalar.activation(parts[s][:, 0, :, :], rot[:, :, :], ACT.Copy).then_inc(hi_done[s], 1)

                def middle(it, s):
                    act.wait_ge(rest_done[s], it + 1)
                    nc.scalar.activation(parts[s][:, 1, :, :], rest[:, :, :], ACT.Copy).then_inc(mid_done[s], 1)

                def slot(it, s, c):
                    if exists(c, 0):
                        take(it, s, KVC)
                        take(it, s, KA)
                    if exists(c, -2):
                        middle(*near(it, s, -2))
                    if exists(c, 0):
                        take(it, s, VA)
                    if exists(c, 1):
                        root(*near(it, s, 1))
                    if exists(c, 0):
                        if exists(c, -1):
                            before, half = near(it, s, -1)
                            act.wait_ge(sw_done[half], before + 1)
                        take(it, s, Q)
                        take(it, s, K)
                        if exists(c, 1):
                            take(*near(it, s, 1), T)
                        if c == 0:
                            act.wait_ge(ones_set, 4)
                        take(it, s, V)
                    if exists(c, -1):
                        high(*near(it, s, -1))

                root(0, 0)
                take(0, 0, T)
                slots(act, slot, after=2)

            @block.vector
            def _(dve):
                nc.vector.memset(wk[DC:2 * DC, :], 0.0).then_inc(ones_set, 1)
                nc.vector.memset(wv[0:DC, :], 0.0).then_inc(ones_set, 1)

                def link(ins, count):
                    ins.then_inc(chain, 1)
                    dve.wait_ge(chain, count)

                def variance(it, s):
                    n = it * 2 + s
                    dve.wait_ge(x_in[s], it * 16 + 16)
                    for j in range(TPC):
                        ins = nc.vector.bn_stats(stats[:, j, :], xin[s][:, j, :])
                    link(ins, n * LINKS + 1)
                    nc.vector.memset(fence[:, :], 0.0)
                    for j in range(TPC):
                        ins = nc.vector.bn_aggr(mv[:, j, :], stats[:, j, :])
                    link(ins, n * LINKS + 2)
                    nc.vector.tensor_scalar(veps[s][:, :], mv[:, :, 1], LN_EPS, None, ALU.add).then_inc(var_done[s], 1)

                def norm(it, s):
                    n = it * 2 + s
                    dve.wait_ge(sd_done[s], it + 1)
                    link(nc.vector.reciprocal(rstd[:, :], sd[s][:, :]), n * LINKS + 3)
                    dve.wait_ge(st["xn"][s], it * 16)
                    dve.wait_ge(made[T][s], it)
                    dve.wait_ge(xx_done[s], it)
                    for j in range(TPC):
                        ins = nc.vector.tensor_scalar(xn[s][:, j, :], xin[s][:, j, :], mv[:, j, 0:1],
                                                      rstd[:, j:j + 1], ALU.subtract, ALU.mult)
                    ins.then_inc(xn_done[s], 1)

                def turn(it, s, before):
                    dve.wait_ge(taken[Q][s], it + 1)
                    dve.wait_ge(taken[K][s], it + 1)
                    if before:
                        dve.wait_ge(rot_done[before[1]], before[0] + 1)
                    nc.vector.tensor_tensor(tcos[:, :, :], qk[:, :, :],
                                            cos[:, s:s + 1, :].broadcast_to([P, 2 * KD, CH]), ALU.mult)
                    nc.vector.stream_shuffle(swap[:, :, :], qk[:, :, :],
                                             [i ^ 1 for i in range(32)]).then_inc(sw_done[s], 1)

                def turned(it, s, before):
                    dve.wait_ge(sin_done[s], it + 1)
                    if before:
                        dve.wait_ge(rest_done[before[1]], before[0] + 1)
                    nc.vector.tensor_tensor(rot[:, :, :], tcos[:, :, :], tsin[:, :, :],
                                            ALU.add).then_inc(rot_done[s], 1)

                def first_rest(it, s, before):
                    dve.wait_ge(hi_done[s], it + 1)
                    if before:
                        dve.wait_ge(lo_done[before[1]], before[0] + 1)
                    nc.vector.tensor_tensor(rest[:, :, :], rot[:, :, :], parts[s][:, 0, :, :],
                                            ALU.subtract).then_inc(rest_done[s], 1)

                def low(it, s):
                    dve.wait_ge(mid_done[s], it + 1)
                    nc.vector.tensor_tensor(parts[s][:, 2, :, :], rest[:, :, :], parts[s][:, 1, :, :],
                                            ALU.subtract).then_inc(lo_done[s], 1)

                def slot(it, s, c):
                    if exists(c, -1):
                        turn(*near(it, s, -1), near(it, s, -2) if exists(c, -2) else None)
                    if exists(c, -2):
                        first_rest(*near(it, s, -2), near(it, s, -3) if exists(c, -3) else None)
                    if exists(c, 1):
                        variance(*near(it, s, 1))
                    if exists(c, 1):
                        norm(*near(it, s, 1))
                    if exists(c, -2):
                        low(*near(it, s, -2))
                    if exists(c, -1):
                        turned(*near(it, s, -1), near(it, s, -2) if exists(c, -2) else None)

                variance(0, 0)
                norm(0, 0)
                for s in range(2):
                    nc.vector.memset(vh[s][:, :, :, :].rearrange("p j h w -> p (j h w)"), 1.0).then_inc(ones_set, 1)
                slots(dve, slot, after=2)

            @block.tensor
            def _(pe):
                def free(it, s, j):
                    if s:
                        pe.wait_ge(taken[j][0], it + 1)
                    else:
                        pe.wait_ge(taken[j][1], it)

                def product(j, s, out, lhs, rhs, signal):
                    for k in range(KD):
                        ins = nc.tensor.matmul(out, lhs(k), rhs(k), start=k == 0, stop=k == KD - 1)
                    if signal:
                        ins.then_inc(made[j][s], 1)

                def transposes(it, s, before):
                    pe.wait_ge(xn_done[s], it + 1)
                    if before:
                        pe.wait_ge(taken[Q][before[1]], before[0] + 1)
                    for m in range(KD):
                        for j in range(TPC):
                            ins = nc.tensor.transpose(ps[BANKS[T]][:, m, j * P:(j + 1) * P],
                                                      xn[s][:, j, m * P:(m + 1) * P], ident[:, :])
                    ins.then_inc(made[T][s], 1)

                def slot(it, s, c):
                    x_t = lambda k: xnT[s][:, k, :]
                    pe.wait_ge(taken[T][s], it + 1)
                    free(it, s, K)
                    product(KVC, s, ps[BANKS[KVC]][:, 0, :], lambda k: wkvc[:, k, :], x_t, True)
                    free(it, s, V)
                    for m in range(KD):
                        product(KA, s, ps[BANKS[KA]][:, m, :], lambda k: wkv[:, k, m * P:(m + 1) * P],
                                x_t, m == KD - 1)
                    free(it, s, VA)
                    for j in range(TPC):
                        product(VA, s, ps[BANKS[VA]][:, j // 2, (j % 2) * D:(j % 2 + 1) * D],
                                lambda k: xnT[s][:, k, j * P:(j + 1) * P], lambda k: wkv[:, k, D:2 * D],
                                j == TPC - 1)
                    for m in range(KD):
                        product(Q, s, ps[BANKS[Q]][:, m, :], lambda k: wq[:, k, m * P:(m + 1) * P],
                                x_t, m == KD - 1)
                    pe.wait_ge(taken[KVC][s], it + 1)
                    for m in range(KD):
                        ins = nc.tensor.matmul(ps[BANKS[K]][:, m, :], wk[:, m * P:(m + 1) * P],
                                               kvc[s][:, :], start=True, stop=True)
                    ins.then_inc(made[K][s], 1)
                    if exists(c, 1):
                        transposes(*near(it, s, 1), (it, s))
                    pe.wait_ge(taken[KA][s], it + 1)
                    for j in range(TPC):
                        ins = nc.tensor.matmul(ps[BANKS[V]][:, j // 2, (j % 2) * D:(j % 2 + 1) * D],
                                               kvc[s][:, j * P:(j + 1) * P], wv[:, :], start=True, stop=True)
                    ins.then_inc(made[V][s], 1)

                pe.wait_ge(ident_set, 2)
                transposes(0, 0, None)
                pe.wait_ge(weights, 6 * 16)
                slots(pe, slot)


def causal_attention(nc, xnT_d, kaT_d, va_d, xx_d, ya_d):
    with ExitStack() as ctx:
        sb = lambda name, shape, dt=F32: ctx.enter_context(nc.sbuf_tensor(name, shape, dt))
        sem = ctx.enter_context(stage_semaphores(nc))
        sems = lambda name: [sem(f"{name}{s}") for s in range(2)]
        two = lambda name, shape: [sb(f"{name}{s}", shape) for s in range(2)]
        ident = sb("a_ident", [P, P])
        mask = sb("a_mask", [P, P])
        qT = two("a_qT", [P, KD, S])
        kT = two("a_kT", [P, KD, S])
        va = two("a_va", [P, QT, D])
        xx = two("a_xx", [P, QT, D])
        negm = two("a_negm", [P, 1])
        probs = two("a_probs", [P, S])
        rowsum = two("a_rowsum", [P, 1])
        inv = two("a_inv", [P, 1])
        pT = two("a_pT", [P, QT, P])
        ya = two("a_ya", [P, D])
        sc = [ctx.enter_context(nc.psum_tensor(f"a_sc{i}", [P, S], F32)) for i in range(2)]
        tp = [ctx.enter_context(nc.psum_tensor(f"a_tp{i}", [P, 4, P], F32)) for i in range(2)]
        out = [ctx.enter_context(nc.psum_tensor(f"a_out{i}", [P, CH], F32)) for i in range(2)]

        const_set = sem("a_const_set")
        loaded = sems("a_loaded")
        scored = sems("a_scored")
        masked = sems("a_masked")
        max_done = sems("a_max_done")
        exp_done = sems("a_exp_done")
        turned = sems("a_turned")
        turned_out = sems("a_turned_out")
        mixed = sems("a_mixed")
        inv_done = sems("a_inv_done")
        ya_done = sems("a_ya_done")
        ya_stored = sems("a_ya_stored")
        U = 2 * QT
        GROUPS = [[(g, min(4, i + 1 - g)) for g in range(0, i + 1, 4)] for i in range(QT)]
        FIRST = [sum(len(GROUPS[v % QT]) for v in range(u)) for u in range(U)]
        PER = FIRST[-1] + len(GROUPS[QT - 1])
        with nc.Block() as block:

            @block.gpsimd
            def _(pool):
                nc.gpsimd.memset(ident[:, :], 0.0).then_inc(const_set, 1)
                nc.gpsimd.memset(mask[:, :], 0.0).then_inc(const_set, 1)
                pool.wait_ge(const_set, 2)
                nc.gpsimd.affine_select(out=ident[:, :], in_=ident[:, :], compare_op=ALU.not_equal, fill=1.0,
                                        base=0, pattern=[[-1, P]], channel_multiplier=1).then_inc(const_set, 1)
                nc.gpsimd.affine_select(out=mask[:, :], in_=mask[:, :], compare_op=ALU.is_ge, fill=MASKED,
                                        base=0, pattern=[[-1, P]], channel_multiplier=1).then_inc(const_set, 1)

            @block.sync
            def _(sp):
                def load(b, s):
                    rows = lambda a: a[bass.ds(b * S, S), :].rearrange("(j p) d -> p j d", p=P)
                    cols = lambda a: a[:, bass.ds(b * S, S)].rearrange("(m p) t -> p m t", p=P)
                    sp.dma_start(qT[s][:, :, :], cols(xnT_d)).then_inc(loaded[s], 16)
                    sp.dma_start(kT[s][:, :, :], cols(kaT_d)).then_inc(loaded[s], 16)
                    sp.dma_start(va[s][:, :, :], rows(va_d)).then_inc(loaded[s], 16)
                    sp.dma_start(xx[s][:, :, :], rows(xx_d)).then_inc(loaded[s], 16)

                for s in range(2):
                    load(s, s)
                with sp.Fori(0, B // 2 - 1) as it:
                    for s in range(2):
                        u = s * QT + QT - 1
                        sp.wait_ge(ya_done[u % 2], it * (U // 2) + u // 2 + 1)
                        load(it * 2 + 2 + s, s)

            @block.gpsimd
            def _(pool):
                with pool.Fori(0, B // 2) as it:
                    for u in range(U):
                        pool.wait_ge(ya_done[u % 2], it * (U // 2) + u // 2 + 1)
                        pool.dma_start(ya_d[bass.ds(it * 2 * S + u * P, P), :], ya[u % 2][:, :])\
                            .then_inc(ya_stored[u % 2], 16)
                for r in range(2):
                    pool.wait_ge(ya_stored[r], B * QT // 2 * 16)

            @block.tensor
            def _(pe):
                pe.wait_ge(const_set, 4)
                with pe.Fori(0, B // 2) as it:
                    def score(u):
                        s, i = divmod(u, QT)
                        if i == 0:
                            pe.wait_ge(loaded[s], it * 64 + 64)
                        pe.wait_ge(exp_done[u % 2], it * (U // 2) + u // 2)
                        n = (i + 1) * P
                        for c in range(0, n, CH):
                            w = min(CH, n - c)
                            for k in range(KD):
                                ins = nc.tensor.matmul(sc[u % 2][:, c:c + w], qT[s][:, k, i * P:(i + 1) * P],
                                                       kT[s][:, k, c:c + w], start=k == 0, stop=k == KD - 1)
                        ins.then_inc(scored[u % 2], 1)

                    score(0)
                    for u in range(U):
                        s, i = divmod(u, QT)
                        if u + 1 < U:
                            score(u + 1)
                        pe.wait_ge(exp_done[u % 2], it * (U // 2) + u // 2 + 1)
                        for g, (first, count) in enumerate(GROUPS[i]):
                            f = FIRST[u] + g
                            pe.wait_ge(turned_out[f % 2], it * (PER // 2) + f // 2)
                            for j in range(first, first + count):
                                ins = nc.tensor.transpose(tp[f % 2][:, j - first, :],
                                                          probs[u % 2][:, j * P:(j + 1) * P], ident[:, :])
                            ins.then_inc(turned[f % 2], 1)
                        pe.wait_ge(ya_done[u % 2], it * (U // 2) + u // 2)
                        for g, (first, count) in enumerate(GROUPS[i]):
                            f = FIRST[u] + g
                            pe.wait_ge(turned_out[f % 2], it * (PER // 2) + f // 2 + 1)
                            for j in range(first, first + count):
                                ins = nc.tensor.matmul(out[u % 2][:, 0:D], pT[u % 2][:, j, :], va[s][:, j, :],
                                                       start=j == 0, stop=j == i)
                        ins.then_inc(mixed[u % 2], 1)

            @block.scalar
            def _(act):
                with act.Fori(0, B // 2) as it:
                    for u in range(U):
                        i = u % QT
                        act.wait_ge(max_done[u % 2], it * (U // 2) + u // 2 + 1)
                        act.wait_ge(mixed[u % 2], it * (U // 2) + u // 2)
                        act.wait_ge(inv_done[u % 2], it * (U // 2) + u // 2)
                        nc.scalar.activation(probs[u % 2][:, 0:(i + 1) * P], sc[u % 2][:, 0:(i + 1) * P], ACT.Exp,
                                             bias=negm[u % 2][:, :], accum_out=rowsum[u % 2][:, :])\
                            .then_inc(exp_done[u % 2], 1)

            @block.vector
            def _(dve):
                dve.wait_ge(const_set, 4)
                with dve.Fori(0, B // 2) as it:
                    def maximum(u):
                        i = u % QT
                        dve.wait_ge(scored[u % 2], it * (U // 2) + u // 2 + 1)
                        diag = sc[u % 2][:, i * P:(i + 1) * P]
                        nc.vector.tensor_tensor(diag, diag, mask[:, :], ALU.add).then_inc(masked[u % 2], 1)
                        dve.wait_ge(masked[u % 2], it * (U // 2) + u // 2 + 1)
                        nc.vector.tensor_reduce(negm[u % 2][:, :], sc[u % 2][:, 0:(i + 1) * P], AX.X, ALU.max,
                                                negate=True).then_inc(max_done[u % 2], 1)

                    def finish(u):
                        s, i = divmod(u, QT)
                        dve.wait_ge(mixed[u % 2], it * (U // 2) + u // 2 + 1)
                        dve.wait_ge(inv_done[u % 2], it * (U // 2) + u // 2 + 1)
                        dve.wait_ge(ya_stored[u % 2], (it * (U // 2) + u // 2) * 16)
                        nc.vector.scalar_tensor_tensor(ya[u % 2][:, :], out[u % 2][:, 0:D], inv[u % 2][:, :],
                                                       xx[s][:, i, :], ALU.mult, ALU.add).then_inc(ya_done[u % 2], 1)

                    maximum(0)
                    for u in range(U):
                        i = u % QT
                        if u + 1 < U:
                            maximum(u + 1)
                        dve.wait_ge(exp_done[u % 2], it * (U // 2) + u // 2 + 1)
                        dve.wait_ge(ya_done[u % 2], it * (U // 2) + u // 2)
                        nc.vector.reciprocal(inv[u % 2][:, :], rowsum[u % 2][:, :]).then_inc(inv_done[u % 2], 1)
                        for g, (first, count) in enumerate(GROUPS[i]):
                            f = FIRST[u] + g
                            dve.wait_ge(turned[f % 2], it * (PER // 2) + f // 2 + 1)
                            nc.vector.tensor_copy(pT[u % 2][:, first:first + count, :],
                                                  tp[f % 2][:, 0:count, :]).then_inc(turned_out[f % 2], 1)
                        if u >= 1:
                            finish(u - 1)
                    finish(U - 1)


class FeedForwardWeights:

    def __init__(self, nc, ctx, w_o, ws_in, w1, w2, w_g, w_e, b_g, b_e, n1_w, n2_w):
        sb = lambda name, shape, dt=F32: ctx.enter_context(nc.sbuf_tensor(name, shape, dt))
        self.out = sb("w_out", [P, KD, D])
        self.gate = sb("w_gate", [P, KD, GATES])
        self.bias = sb("w_bias", [P, 1, GATES])
        self.n1 = sb("w_n1", [P, D])
        self.n2 = sb("w_n2", [P, D])
        self.experts = [sb(f"w_experts{part}", [P, E, KH, D], F32R) for part in (HI, LO)]
        self.routed = [sb(f"w_routed{part}", [P, KD, 2 * HID], F32R) for part in (HI, LO)]
        self.shared = [sb(f"w_shared{part}", [P, KD, 2 * HID], F32R) for part in (HI, LO)]
        fan = lambda v: v.rearrange("(o n) -> o n", o=1).broadcast_to([P, v.shape[0]])
        part = lambda w: w.rearrange("(k p) m -> p k m", p=P)
        self.transfers = (
            (self.out[:, :, :], part(w_o)), (self.n1[:, :], fan(n1_w)), (self.n2[:, :], fan(n2_w)),
            (self.gate[:, :, 0:2], part(w_g)), (self.gate[:, :, 2:GATES], part(w_e)),
            (self.bias[:, 0, 0:2], fan(b_g)), (self.bias[:, 0, 2:GATES], fan(b_e)))
        self.pieces = [(part(w2[e]), [w[:, e, :, :] for w in self.experts]) for e in range(E)]
        for dst, src in ((self.routed, w1), (self.shared, ws_in)):
            self.pieces += [(src[k * P:(k + 1) * P, :], [w[:, k, :] for w in dst]) for k in range(KD)]


def head_attention(nc, q_d, k_d, vh_d, ot_d, ffw):
    with ExitStack() as ctx:
        sb = lambda name, shape, dt=F32: ctx.enter_context(nc.sbuf_tensor(name, shape, dt))
        sem = ctx.enter_context(stage_semaphores(nc))
        sems = lambda name, n: [sem(f"{name}{i}") for i in range(n)]
        RING = 3
        STEPS = B * NG
        TURNS = (STEPS - 2) // RING
        NQ = S // CH
        UNITS = NQ * QT
        FILLS = UNITS * GH
        ITEMS = GH * QT * NQ
        BANKS = 3
        PER = ITEMS // UNITS
        LEAD = 3
        EARLY = LEAD * PER
        HELD = PER
        PR = 4
        LOADS = 2 * NT + 1
        SPLIT = 5
        q6 = [sb(f"h_q{i}", [P, GH, S], BF16) for i in range(RING)]
        k6 = [sb(f"h_k{i}", [P, GH, S], BF16) for i in range(RING)]
        vh = [sb(f"h_v{i}", [P, QT, GH, VW]) for i in range(RING)]
        probs = [sb(f"h_p{i}", [P, GH, CH]) for i in range(PR)]
        outT = [sb(f"h_o{i}", [P, CH]) for i in range(NQ)]
        ident = sb("h_ident", [P, P])
        halfmax = sb("h_halfmax", [P, ITEMS])
        negm = sb("h_negm", [P, GH * QT])
        mT = sb("h_mT", [GH * QT, P])
        mrest = sb("h_mrest", [GH * QT, P])
        mparts = sb("h_mparts", [GH * QT, SHIFT, P], BF16)
        bank = lambda name: ctx.enter_context(nc.psum_tensor(name, [P, CH], F32))
        sk = [bank(f"h_sk{i}") for i in range(BANKS)]
        sq = [bank(f"h_sq{i}") for i in range(BANKS)]
        po = bank("h_po")
        pm = bank("h_pm")

        const_set = sem("h_const_set")
        ones_set = sem("h_ones_set")
        loaded = sems("h_loaded", RING)
        shifted = sems("h_shifted", RING)
        scored = sem("h_scored")
        exp_done = sems("h_exp_done", BANKS)
        pv_done = sems("h_pv_done", PR)
        out_taken = sem("h_out_taken")
        stored = sems("h_stored", NQ)
        item_scored = sem("h_item_scored")
        item_max = sems("h_item_max", BANKS)
        max_done = sem("h_max_done")
        m_turned = sem("h_m_turned")
        m_split = sem("h_m_split")
        piece = sb("h_piece", [P, KH * D])
        assert KH * D == 2 * HID
        piece_in = sem("h_piece_in")
        others_in = sem("h_others_in")
        rounded = sem("h_rounded")
        rests_done = sem("h_rests_done")

        def steps(eng, step):
            with eng.Fori(0, TURNS) as it:
                for place in range(RING):
                    step(it, place, None)
            for n in range(TURNS * RING, STEPS):
                step(n // RING, n % RING, n)

        def exists(n, d):
            return n is None or n + d < STEPS

        begun = sem("h_begun")
        with nc.Block() as block:

            @block.gpsimd
            def _(pool):
                nc.gpsimd.memset(ident[:, :], 0.0).then_inc(const_set, 1)
                pool.wait_ge(const_set, 1)
                nc.gpsimd.affine_select(out=ident[:, :], in_=ident[:, :], compare_op=ALU.not_equal, fill=1.0,
                                        base=0, pattern=[[-1, P]], channel_multiplier=1).then_inc(const_set, 1)
                for dst, src in ffw.transfers:
                    pool.dma_start(dst, src).then_inc(others_in, 16)
                for n, (src, (hi, lo)) in enumerate(ffw.pieces):
                    whole = piece[:, :].rearrange("p (k m) -> p k m", m=D) if len(src.shape) == 3 else piece[:, :]
                    pool.wait_ge(rests_done, n)
                    pool.dma_start(whole, src).then_inc(piece_in, 16)
                    pool.wait_ge(piece_in, n * 16 + 16)
                    nc.gpsimd.tensor_copy(hi, whole).then_inc(rounded, 1)
                    pool.wait_ge(rounded, n + 1)
                    nc.gpsimd.tensor_tensor(lo, whole, hi.bitcast(F32), ALU.subtract).then_inc(rests_done, 1)
                pool.wait_ge(rests_done, len(ffw.pieces))
                pool.wait_ge(others_in, len(ffw.transfers) * 16)

            @block.sync
            def _(sp):
                wait = Waits(sp, begun)
                def load(n, r):
                    t0 = (n // NG) * S
                    h0 = (n % NG) * GH
                    if not isinstance(n, int):
                        t0, h0 = sp.snap(t0), sp.snap(h0)
                    if not isinstance(n, int) or n >= RING:
                        wait.ge(pv_done[(UNITS - 1) % PR], (n - RING + 1) * (UNITS // PR))
                    for t in range(NT):
                        for dst, src, term in ((q6, q_d, QTERM[t]), (k6, k_d, KTERM[t])):
                            sp.dma_start(dst[r][t * DH:(t + 1) * DH, :, :],
                                         src[term, bass.ds(h0 * DH, GH * DH), bass.ds(t0, S)]
                                         .rearrange("(h d) t -> d h t", d=DH)).then_inc(loaded[r], 16)
                    sp.dma_start(vh[r][:, :, :, :].rearrange("p j h w -> p j (h w)"),
                                 vh_d[bass.ds(t0, S), bass.ds(h0 * VW, GH * VW)]
                                 .rearrange("(j p) c -> p j c", p=P)).then_inc(loaded[r], 16)

                def shift(n, r):
                    wait.ge(m_split, n * SPLIT + SPLIT)
                    for j in range(SHIFT):
                        sp.dma_start(q6[r][DOTS + j:DOTS + j + 1, :, :].rearrange("p h t -> p (h t)"),
                                     mparts[:, j, :]).then_inc(shifted[r], 16)

                for n in range(RING - 1):
                    load(n, n)
                shift(0, 0)
                def step(it, place, n):
                    k = it * RING + place
                    if exists(n, RING - 1):
                        load(k + RING - 1, (place + RING - 1) % RING)
                    if exists(n, 1):
                        shift(k + 1, (place + 1) % RING)

                steps(sp, step)

            @block.tensor
            def _(pe):
                pe.wait_ge(const_set, 2)
                pe.wait_ge(ones_set, RING)

                def item(it, place, m):
                    h, i, half = m // (QT * NQ), m // NQ % QT, m % NQ
                    f = ITEMS * place + m
                    r = place % RING
                    pe.wait_ge(item_max[f % BANKS], it * ITEMS + f // BANKS)
                    nc.tensor.matmul(sq[f % BANKS][:, :], q6[r][0:DOTS, h, i * P:(i + 1) * P],
                                     k6[r][0:DOTS, h, half * CH:(half + 1) * CH],
                                     start=True, stop=True).then_inc(item_scored, 1)

                def turn_maxima(it, place):
                    n = it * RING + place
                    pe.wait_ge(max_done, n + 1)
                    pe.wait_ge(m_split, n * SPLIT)
                    nc.tensor.transpose(pm[0:GH * QT, 0:P], negm[:, :], ident[:, :]).then_inc(m_turned, 1)

                def mix(it, place, w):
                    c, j = divmod(w, QT)
                    if j == 0:
                        pe.wait_ge(out_taken, (it * RING + place) * NQ + c)
                    last = FILLS * place + GH * w + GH - 1
                    for b in range(BANKS):
                        f = last - (last - b) % BANKS
                        pe.wait_ge(exp_done[b], it * FILLS + f // BANKS + 1)
                    for h in range(GH):
                        ins = nc.tensor.matmul(po[h * VW:(h + 1) * VW, :], vh[place % RING][:, j, h, :],
                                               probs[w % PR][:, h, :], start=j == 0, stop=j == QT - 1)
                    ins.then_inc(pv_done[w % PR], 1)

                def unit(it, place, w, n):
                    if w == 0:
                        pe.wait_ge(shifted[place % RING], (it + place // RING + 1) * SHIFT * 16)
                    c, j = divmod(w, QT)
                    early = w >= UNITS - LEAD
                    of = place + 1 + early
                    if early and w == UNITS - LEAD and exists(n, 2):
                        pe.wait_ge(loaded[of % RING], (it + of // RING + 1) * LOADS * 16)
                    for h in range(GH):
                        f = FILLS * place + GH * w + h
                        r = place % RING
                        pe.wait_ge(exp_done[f % BANKS], it * FILLS + f // BANKS)
                        nc.tensor.matmul(sk[f % BANKS][:, :], k6[r][0:DOTS + SHIFT, h, j * P:(j + 1) * P],
                                         q6[r][0:DOTS + SHIFT, h, c * CH:(c + 1) * CH],
                                         start=True, stop=True).then_inc(scored, 1)
                        if exists(n, 1 + early):
                            item(it, of, (w + LEAD) % UNITS * PER + h)

                def step(it, place, n):
                    for w in range(1, UNITS):
                        unit(it, place, w, n)
                        mix(it, place, w - 1)
                        if w == UNITS - LEAD and exists(n, 1):
                            turn_maxima(it, place + 1)
                    if exists(n, 1):
                        unit(it, place + 1, 0, n if n is None else n + 1)
                    mix(it, place, UNITS - 1)

                assert PER == GH and HELD == PER
                pe.wait_ge(loaded[0], LOADS * 16)
                for m in range(ITEMS):
                    item(0, 0, m)
                pe.wait_ge(loaded[1], LOADS * 16)
                for m in range(HELD):
                    item(0, 1, m)
                turn_maxima(0, 0)
                for m in range(HELD, EARLY):
                    item(0, 1, m)
                unit(0, 0, 0, 0)
                steps(pe, step)

            @block.scalar
            def _(act):
                def fill(it, place, g):
                    w, h = divmod(g, GH)
                    if h == 0:
                        act.wait_ge(pv_done[w % PR], (it * RING + place) * (UNITS // PR) + w // PR)
                    f = FILLS * place + g
                    act.wait_ge(scored, it * (RING * FILLS) + f + 1)
                    nc.scalar.activation(probs[w % PR][:, h, :], sk[f % BANKS][:, :], ACT.Exp,
                                         scale=DH ** -0.5).then_inc(exp_done[f % BANKS], 1)

                def take_out(n, c):
                    w = (c + 1) * QT - 1
                    act.wait_ge(pv_done[w % PR], n * (UNITS // PR) + w // PR + 1)
                    act.wait_ge(stored[c], n * 16)
                    nc.scalar.activation(outT[c][:, :], po[:, :], ACT.Copy).then_inc(out_taken, 1)

                def store(n, c):
                    act.wait_ge(out_taken, n * NQ + c + 1)
                    act.dma_start(ot_d[n, :, c * CH:(c + 1) * CH], outT[c][:, :]).then_inc(stored[c], 16)

                TAKE = GH + 1

                def step(it, place, n):
                    k = it * RING + place
                    for g in range(TAKE + 1, FILLS + TAKE + 1):
                        if g < FILLS:
                            fill(it, place, g)
                        elif exists(n, 1):
                            fill(it, place + 1, g - FILLS)
                        for c in range(NQ):
                            done = (c + 1) * QT * GH
                            if g == done + TAKE - 1:
                                take_out(k, c)
                            if g == done + TAKE:
                                store(k, c)

                for g in range(TAKE + 1):
                    fill(0, 0, g)
                steps(act, step)
                for c in range(NQ):
                    act.wait_ge(stored[c], STEPS * 16)

            @block.vector
            def _(dve):
                for i in range(RING):
                    nc.vector.memset(k6[i][DOTS:P, :, :].rearrange("p h t -> p (h t)"), 1.0).then_inc(ones_set, 1)

                def maxima(it, place, first, end):
                    if first == 0:
                        dve.wait_ge(max_done, it * RING + place)
                    for m in range(first, end):
                        f = ITEMS * place + m
                        dve.wait_ge(item_scored, it * (RING * ITEMS) + f + 1)
                        nc.vector.tensor_reduce(halfmax[:, m:m + 1], sq[f % BANKS][:, :], AX.X, ALU.max)\
                            .then_inc(item_max[f % BANKS], 1)

                def larger(it, place):
                    last = ITEMS * place + ITEMS - 1
                    for b in range(BANKS):
                        f = last - (last - b) % BANKS
                        dve.wait_ge(item_max[b], it * ITEMS + f // BANKS + 1)
                    dve.wait_ge(m_turned, it * RING + place)
                    nc.vector.tensor_reduce(negm[:, :], halfmax[:, :].rearrange("p (t a) -> p t a", a=NQ),
                                            AX.X, ALU.max, negate=True).then_inc(max_done, 1)

                def split(it, place):
                    n = it * RING + place
                    dve.wait_ge(m_turned, n + 1)
                    nc.vector.tensor_copy(mT[:, :], pm[0:GH * QT, 0:P]).then_inc(m_split, 1)
                    dve.wait_ge(m_split, n * SPLIT + 1)
                    if place:
                        dve.wait_ge(shifted[place - 1], (it + 1) * SHIFT * 16)
                    nc.vector.tensor_copy(mparts[:, 0, :], mT[:, :]).then_inc(m_split, 1)
                    dve.wait_ge(m_split, n * SPLIT + 2)
                    nc.vector.tensor_tensor(mrest[:, :], mT[:, :], mparts[:, 0, :], ALU.subtract).then_inc(m_split, 1)
                    dve.wait_ge(m_split, n * SPLIT + 3)
                    nc.vector.tensor_copy(mparts[:, 1, :], mrest[:, :]).then_inc(m_split, 1)
                    dve.wait_ge(m_split, n * SPLIT + 4)
                    nc.vector.tensor_tensor(mparts[:, 2, :], mrest[:, :], mparts[:, 1, :], ALU.subtract)\
                        .then_inc(m_split, 1)

                def step(it, place, n):
                    if exists(n, 1):
                        maxima(it, place + 1, EARLY, ITEMS)
                        larger(it, place + 1)
                    if exists(n, 2):
                        maxima(it, place + 2, 0, HELD)
                    if exists(n, 1):
                        split(it, place + 1)
                    if exists(n, 2):
                        maxima(it, place + 2, HELD, EARLY)

                maxima(0, 0, 0, ITEMS)
                larger(0, 0)
                maxima(0, 1, 0, HELD)
                split(0, 0)
                maxima(0, 1, HELD, EARLY)
                steps(dve, step)


def feed_forward(nc, ot_d, xn_d, ya_d, ffw, ws_out, out):
    with ExitStack() as ctx:
        sb = lambda name, shape, dt=F32: ctx.enter_context(nc.sbuf_tensor(name, shape, dt))
        sem = ctx.enter_context(stage_semaphores(nc))
        sems = lambda name, n=2: [sem(f"{name}{s}") for s in range(n)]
        two = lambda name, shape, dt=F32: [sb(f"{name}{s}", shape, dt) for s in range(2)]
        R = GATES
        TURNS = NCH // 2 - 1
        wo, wr, bias, n1, n2 = ffw.out, ffw.gate, ffw.bias, ffw.n1, ffw.n2
        w2s = ffw.experts
        w_in = {"routed": ffw.routed, "shared": ffw.shared}
        wso = sb("f_wso", [P, KH, D])
        ident = sb("f_ident", [P, P])
        before = sb("f_before", [P, 1, E * E])
        val = sb("f_val", [P, KD, CH])
        tot = sb("f_tot", [P, KD, CH])
        saT = sb("f_saT", [P, KD, CH])
        xn = sb("f_xn", [P, TPC, D])
        ya = two("f_ya", [P, TPC, D])
        sq = sb("f_sq", [P, D])
        ss = sb("f_ss", [P, TPC])
        ms = sb("f_ms", [P, TPC])
        sd = sb("f_sd", [P, TPC])
        rstd = sb("f_rstd", [P, TPC])
        x1 = two("f_x1", [P, TPC, D])
        x1T = sb("f_x1T", [P, KD, CH])
        x1p = [sb(f"f_x1p{part}", [P, KD, CH], F32R) for part in (HI, LO)]
        sil = two("f_sil", [P, CH])
        whole = two("f_whole", [P, CH])
        h1 = [sb(f"f_h1p{part}", [P, KH, CH], F32R) for part in (HI, LO)]
        hs = sb("f_hs", [P, KH, CH])
        lg = sb("f_lg", [P, TPC, R])
        gmax = sb("f_gmax", [P, TPC, 1])
        emax = sb("f_emax", [P, TPC, 2])
        ex = sb("f_ex", [P, TPC, R])
        exs = sb("f_exs", [P, TPC, R])
        gsum = sb("f_gsum", [P, TPC, 1])
        esum = sb("f_esum", [P, TPC, 2])
        ginv = sb("f_ginv", [P, TPC, 1])
        einv = sb("f_einv", [P, TPC, 2])
        gp = sb("f_gp", [P, TPC, 2])
        pe_ = sb("f_pe", [P, TPC, E])
        gt = sb("f_gt", [P, TPC, E, E])
        ge = sb("f_ge", [P, TPC, E, E])
        rank = sb("f_rank", [P, TPC, E])
        wt = two("f_wt", [P, TPC, E])
        sq2 = sb("f_sq2", [P, D])
        ss2 = sb("f_ss2", [P, TPC])
        ms2 = sb("f_ms2", [P, TPC])
        sd2 = sb("f_sd2", [P, TPC])
        rstd2 = sb("f_rstd2", [P, TPC])
        pair = [ctx.enter_context(nc.psum_tensor(f"f_pair{i}", [P, 2, CH], F32)) for i in range(2)]
        ob = [ctx.enter_context(nc.psum_tensor(f"f_ob{i}", [P, CH], F32)) for i in range(4)]
        FILLS = 3 + 2 * KH
        OUTS = E // 2 + 1

        weights = sem("f_weights")
        const_set = sem("f_const_set")
        values_in = sem("f_values_in")
        xn_in = sem("f_xn_in")
        ya_in = sems("f_ya_in")
        sa_done = sem("f_sa_done")
        made = sem("f_made")
        free = sems("f_free")
        squared = sem("f_squared")
        ms_done = sem("f_ms_done")
        sd_done = sem("f_sd_done")
        x1_done = sems("f_x1_done")
        x1_rounded = sem("f_x1_rounded")
        x1_split = sem("f_x1_split")
        h_rounded = sem("f_h_rounded")
        h_split = sem("f_h_split")
        logits = sem("f_logits")
        exped = sem("f_exped")
        sil_done = sems("f_sil_done")
        routed = sems("f_routed")
        tile_made = sem("f_tile_made")
        tile_free = sems("f_tile_free", 4)
        squared2 = sem("f_squared2")
        ms2_done = sem("f_ms2_done")
        sd2_done = sem("f_sd2_done")
        fin_done = sems("f_fin_done")
        stored = sems("f_stored")
        chain = sem("f_chain")
        FIRST, STEP = 23, 39

        begun = sem("f_begun")
        with nc.Block() as block:

            pair_at = lambda place, j: (FILLS * place + j) % 2
            uses = lambda it, place, j: it * FILLS + (FILLS * place + j) // 2
            fills = lambda it, place, j: it * 2 * FILLS + FILLS * place + j
            WO, XT, GATE, HIDDEN = 0, 1, 2, 3

            @block.gpsimd
            def _(pool):
                nc.gpsimd.memset(ident[:, :], 0.0).then_inc(const_set, 1)
                nc.gpsimd.memset(before[:, :, :].rearrange("p o n -> p (o n)"), 1.0).then_inc(const_set, 1)
                pool.wait_ge(const_set, 2)
                nc.gpsimd.affine_select(out=ident[:, :], in_=ident[:, :], compare_op=ALU.not_equal, fill=1.0,
                                        base=0, pattern=[[-1, P]], channel_multiplier=1).then_inc(const_set, 1)
                b2 = before[:, 0, :].rearrange("p (e j) -> p e j", j=E)
                nc.gpsimd.affine_select(out=b2, in_=b2, compare_op=ALU.is_gt, fill=0.0,
                                        base=0, pattern=[[1, E], [-1, E]], channel_multiplier=0).then_inc(const_set, 1)

            @block.sync
            def _(sp):
                wait = Waits(sp, begun)
                sp.dma_start(wso[:, :, :], ws_out.rearrange("(k p) m -> p k m", p=P)).then_inc(weights, 16)
                rows = lambda a, c: a[bass.ds(c * CH, CH), :].rearrange("(j p) d -> p j d", p=P)

                def load_values(c):
                    for m in range(KD):
                        for g in range(2):
                            src = ot_d[(c // 2) * NG + 2 * m + g, :, bass.ds((c % 2) * CH, CH)]\
                                .rearrange("(h w) t -> h w t", w=VW)
                            at = slice(g * P // 2, (g + 1) * P // 2)
                            sp.dma_start(val[at, m, :], src[:, 0:DH, :]).then_inc(values_in, 16)
                            sp.dma_start(tot[at, m, :], src[:, DH:VW, :]).then_inc(values_in, 16)

                def load_xn(c):
                    sp.dma_start(xn[:, :, :], rows(xn_d, c)).then_inc(xn_in, 16)

                def load_ya(c, s):
                    sp.dma_start(ya[s][:, :, :], rows(ya_d, c)).then_inc(ya_in[s], 16)

                def store(it, s):
                    wait.ge(fin_done[s], it + 1)
                    sp.dma_start(rows(out, it * 2 + s), ya[s][:, :, :]).then_inc(stored[s], 16)

                load_values(0)
                load_xn(0)
                for s in range(2):
                    load_ya(s, s)
                sp.wait_ge(sa_done, KD)
                load_values(1)
                sp.wait_ge(free[pair_at(0, WO)], 1)
                load_xn(1)
                sp.wait_ge(sa_done, 2 * KD)
                load_values(2)
                for first, turns in ((0, TURNS - 1), (TURNS - 1, 1)):
                    with sp.Fori(first, first + turns) as it:
                        for s in range(2):
                            c = it * 2 + s
                            wait.ge(free[pair_at(s + 1, WO)], uses(it, s + 1, WO) + 1)
                            load_xn(c + 2)
                            if first == 0 or s == 0:
                                wait.ge(sa_done, (c + 3) * KD)
                                load_values(c + 3)
                            store(it, s)
                            wait.ge(stored[s], it * 16 + 16)
                            load_ya(c + 2, s)
                for s in range(2):
                    store(TURNS, s)
                for s in range(2):
                    sp.wait_ge(stored[s], (TURNS + 1) * 16)

            VALUES = 4 * KD * 16
            def shared_done(eng, it, place):
                for j in (HIDDEN + 2 * KH - 2, HIDDEN + 2 * KH - 1):
                    eng.wait_ge(free[pair_at(place, j)], uses(it, place, j) + 1)

            def out_at(it, place, j, g):
                f = OUTS * (TPC * place + j) + g
                return f % 4, it * (2 * OUTS * TPC // 4) + f // 4

            @block.tensor
            def _(pe):
                def begin(it, place, j):
                    pe.wait_ge(free[pair_at(place, j)], uses(it, place, j))
                    return pair[pair_at(place, j)]

                def out_projection(it, place):
                    pe.wait_ge(sa_done, (it * 2 + place + 1) * KD)
                    ps = begin(it, place, WO)
                    for j in range(TPC):
                        for k in range(KD):
                            ins = nc.tensor.matmul(ps[:, j // 2, (j % 2) * D:(j % 2 + 1) * D],
                                                   saT[:, k, j * P:(j + 1) * P], wo[:, k, :],
                                                   start=k == 0, stop=k == KD - 1)
                    ins.then_inc(made, 1)

                def turn(it, place):
                    s = place % 2
                    pe.wait_ge(x1_done[s], it + place // 2 + 1)
                    ps = begin(it, place, XT)
                    for m in range(KD):
                        for j in range(TPC):
                            ins = nc.tensor.transpose(ps[:, m, j * P:(j + 1) * P],
                                                      x1[s][:, j, m * P:(m + 1) * P], ident[:, :])
                    ins.then_inc(made, 1)

                def gates(it, place):
                    pe.wait_ge(free[pair_at(place, XT)], uses(it, place, XT) + 1)
                    ps = begin(it, place, GATE)
                    for j in range(TPC):
                        for k in range(KD):
                            ins = nc.tensor.matmul(ps[:, 0, j * R:(j + 1) * R], x1T[:, k, j * P:(j + 1) * P],
                                                   wr[:, k, :], start=k == 0, stop=k == KD - 1)
                    ins.then_inc(made, 1)

                def hidden(it, place):
                    pe.wait_ge(x1_split, it * 2 + place + 1)
                    for f in range(2 * KH):
                        w = w_in["routed" if f < KH else "shared"]
                        ps = begin(it, place, HIDDEN + f)
                        for half in range(2):
                            at = half * HID + f % KH * P
                            terms = [(k, a, b) for k in range(KD) for a, b in PASSES]
                            for n, (k, a, b) in enumerate(terms):
                                ins = nc.tensor.matmul(ps[:, half, :], w[a][:, k, at:at + P], x1p[b][:, k, :],
                                                       start=n == 0, stop=n == len(terms) - 1)
                        ins.then_inc(made, 1)

                def outputs(it, place, j):
                    for g in range(OUTS):
                        b, used = out_at(it, place, j, g)
                        pe.wait_ge(tile_free[b], used)
                        if g == 0 and j == 0:
                            pe.wait_ge(h_split, (it * 2 + place) * KH + KH)
                        if g == OUTS - 1 and j == 0:
                            shared_done(pe, it, place)
                        at = slice(j * P, (j + 1) * P)
                        if g < OUTS - 1:
                            terms = [(k, left, right) for k in range(KH) for left, right in PASSES]
                            for n, (k, left, right) in enumerate(terms):
                                ins = nc.tensor.matmul(ob[b][:, :], h1[left][:, k, at],
                                                       w2s[right][:, 2 * g:2 * g + 2, k, :],
                                                       start=n == 0, stop=n == len(terms) - 1)
                        else:
                            for k in range(KH):
                                ins = nc.tensor.matmul(ob[b][:, 0:D], hs[:, k, at], wso[:, k, :],
                                                       start=k == 0, stop=k == KH - 1)
                        ins.then_inc(tile_made, 1)

                def step(it, place, follow):
                    outputs(it, place, 0)
                    if follow:
                        out_projection(it, place + 1)
                    outputs(it, place, 1)
                    outputs(it, place, 2)
                    if follow:
                        turn(it, place + 1)
                    outputs(it, place, 3)
                    if follow:
                        gates(it, place + 1)
                        hidden(it, place + 1)

                pe.wait_ge(const_set, 4)
                out_projection(0, 0)
                turn(0, 0)
                gates(0, 0)
                pe.wait_ge(weights, 16)
                hidden(0, 0)
                with pe.Fori(0, TURNS) as it:
                    for s in range(2):
                        step(it, s, True)
                step(TURNS, 0, True)
                step(TURNS, 1, False)

            @block.scalar
            def _(act):
                def squares(it, place):
                    n = it * 2 + place
                    act.wait_ge(free[pair_at(place, WO)], uses(it, place, WO) + 1)
                    for j in range(TPC):
                        nc.scalar.activation(sq[:, :], x1[place % 2][:, j, :], ACT.Square,
                                             accum_out=ss[:, j:j + 1]).then_inc(squared, 1)
                        act.wait_ge(squared, n * TPC + j + 1)
                    act.wait_ge(ms_done, n + 1)
                    nc.scalar.activation(sd[:, :], ms[:, :], ACT.Sqrt).then_inc(sd_done, 1)

                def take_turned(it, place):
                    n = it * 2 + place
                    used = free[pair_at(place, XT)]
                    act.wait_ge(made, fills(it, place, XT) + 1)
                    act.wait_ge(x1_split, n)
                    nc.scalar.activation(x1T[:, :, :], pair[pair_at(place, XT)][:, :, :], ACT.Copy).then_inc(used, 1)
                    act.wait_ge(used, uses(it, place, XT) + 1)
                    nc.scalar.activation(x1p[HI][:, :, :], x1T[:, :, :], ACT.Copy).then_inc(x1_rounded, 1)

                def hidden(it, place):
                    n = it * 2 + place
                    act.wait_ge(logits, n + 1)
                    nc.scalar.activation(ex[:, :, :], exs[:, :, :], ACT.Exp).then_inc(exped, 1)
                    for f in range(2 * KH):
                        act.wait_ge(made, fills(it, place, HIDDEN + f) + 1)
                        j, before = (HIDDEN + f - 2, place) if f >= 2 else (HIDDEN + f - 2 + 2 * KH, place - 1)
                        act.wait_ge(free[pair_at(before, j)], uses(it, before, j) + 1)
                        nc.scalar.activation(sil[f % 2][:, :], pair[pair_at(place, HIDDEN + f)][:, 0, :], ACT.Silu)\
                            .then_inc(sil_done[f % 2], 1)
                        if 1 <= f <= KH:
                            act.wait_ge(free[pair_at(place, HIDDEN + f - 1)], uses(it, place, HIDDEN + f - 1) + 1)
                            nc.scalar.activation(h1[HI][:, f - 1, :], whole[(f - 1) % 2][:, :], ACT.Copy)\
                                .then_inc(h_rounded, 1)

                def final(it, place):
                    n = it * 2 + place
                    s = place % 2
                    b, used = out_at(it, place, TPC - 1, OUTS - 1)
                    act.wait_ge(tile_free[b], used + 1)
                    for j in range(TPC):
                        nc.scalar.activation(sq2[:, :], x1[s][:, j, :], ACT.Square,
                                             accum_out=ss2[:, j:j + 1]).then_inc(squared2, 1)
                        act.wait_ge(squared2, n * TPC + j + 1)
                    act.wait_ge(ms2_done, n + 1)
                    nc.scalar.activation(sd2[:, :], ms2[:, :], ACT.Sqrt).then_inc(sd2_done, 1)

                def step(it, place, follow):
                    if follow:
                        squares(it, place + 1)
                        take_turned(it, place + 1)
                        hidden(it, place + 1)
                    final(it, place)

                squares(0, 0)
                take_turned(0, 0)
                hidden(0, 0)
                with act.Fori(0, TURNS) as it:
                    for s in range(2):
                        step(it, s, True)
                step(TURNS, 0, True)
                step(TURNS, 1, False)

            @block.vector
            def _(dve):
                dve.wait_ge(const_set, 4)

                class Links:

                    def __init__(self, base):
                        self.base, self.n = base, 0

                    def __call__(self, ins):
                        self.n += 1
                        ins.then_inc(chain, 1)
                        dve.wait_ge(chain, self.base + self.n)

                def head(it, place, m, link):
                    if m == 0:
                        dve.wait_ge(values_in, (it * 2 + place + 1) * VALUES)
                    link(nc.vector.reciprocal(tot[:, m, :], tot[:, m, :]))
                    nc.vector.tensor_tensor(saT[:, m, :], val[:, m, :], tot[:, m, :], ALU.mult).then_inc(sa_done, 1)

                def residual(it, place, link):
                    s = place % 2
                    dve.wait_ge(made, fills(it, place, WO) + 1)
                    dve.wait_ge(xn_in, (it * 2 + place + 1) * 16)
                    dve.wait_ge(fin_done[s], it + place // 2)
                    nc.vector.tensor_tensor(x1[s][:, :, :].rearrange("p j d -> p (j d)"),
                                            pair[pair_at(place, WO)][:, :, :].rearrange("p a b -> p (a b)"),
                                            xn[:, :, :].rearrange("p j d -> p (j d)"), ALU.add)\
                        .then_inc(free[pair_at(place, WO)], 1)

                def normalise(it, place, link):
                    n = it * 2 + place
                    s = place % 2
                    dve.wait_ge(squared, n * TPC + TPC)
                    nc.vector.tensor_scalar(ms[:, :], ss[:, :], 1.0 / D, RMS_EPS, ALU.mult, ALU.add)\
                        .then_inc(ms_done, 1)
                    dve.wait_ge(sd_done, n + 1)
                    link(nc.vector.reciprocal(rstd[:, :], sd[:, :]))
                    for j in range(TPC):
                        ins = nc.vector.scalar_tensor_tensor(x1[s][:, j, :], x1[s][:, j, :], rstd[:, j:j + 1], n1[:, :],
                                                             ALU.mult, ALU.mult)
                    ins.then_inc(x1_done[s], 1)

                def route(it, place, link):
                    s = place % 2
                    ps = pair[pair_at(place, GATE)]
                    done = uses(it, place, GATE) + 1
                    four = [P, TPC, E, E]
                    dve.wait_ge(made, fills(it, place, GATE) + 1)
                    nc.vector.tensor_tensor(lg[:, :, :], ps[:, 0, 0:TPC * R].rearrange("p (j r) -> p j r", r=R),
                                            bias[:, :, :].broadcast_to([P, TPC, R]), ALU.add)\
                        .then_inc(free[pair_at(place, GATE)], 1)
                    dve.wait_ge(free[pair_at(place, GATE)], done)
                    link(nc.vector.tensor_reduce(gmax[:, :, 0], lg[:, :, 0:2], AX.X, ALU.max))
                    for g in range(2):
                        link(nc.vector.tensor_reduce(emax[:, :, g], lg[:, :, 2 + g * EPG:2 + (g + 1) * EPG],
                                                     AX.X, ALU.max))
                    nc.vector.tensor_tensor(exs[:, :, 0:2], lg[:, :, 0:2], gmax[:, :, :].broadcast_to([P, TPC, 2]),
                                            ALU.subtract)
                    for g in range(2):
                        at = slice(2 + g * EPG, 2 + (g + 1) * EPG)
                        ins = nc.vector.tensor_tensor(exs[:, :, at], lg[:, :, at],
                                                      emax[:, :, g:g + 1].broadcast_to([P, TPC, EPG]), ALU.subtract)
                    ins.then_inc(logits, 1)
                    dve.wait_ge(exped, it * 2 + place + 1)
                    link(nc.vector.tensor_reduce(gsum[:, :, 0], ex[:, :, 0:2], AX.X, ALU.add))
                    link(nc.vector.tensor_reduce(esum[:, :, :],
                                                 ex[:, :, 2:R].rearrange("p t (g e) -> p t g e", g=2), AX.X, ALU.add))
                    link(nc.vector.reciprocal(ginv[:, :, :], gsum[:, :, :]))
                    link(nc.vector.reciprocal(einv[:, :, :], esum[:, :, :]))
                    link(nc.vector.tensor_tensor(gp[:, :, 0], ex[:, :, 0], ex[:, :, 1], ALU.is_ge))
                    link(nc.vector.tensor_scalar(gp[:, :, 1], gp[:, :, 0], -1.0, 1.0, ALU.mult, ALU.add))
                    link(nc.vector.tensor_tensor(gp[:, :, :], gp[:, :, :], ginv[:, :, :].broadcast_to([P, TPC, 2]),
                                                 ALU.mult))
                    link(nc.vector.tensor_tensor(gp[:, :, :], gp[:, :, :], einv[:, :, :], ALU.mult))
                    for g in range(2):
                        at = slice(g * EPG, (g + 1) * EPG)
                        link(nc.vector.tensor_tensor(pe_[:, :, at], ex[:, :, 2 + g * EPG:2 + (g + 1) * EPG],
                                                     gp[:, :, g:g + 1].broadcast_to([P, TPC, EPG]), ALU.mult))
                    theirs = pe_[:, :, :].unsqueeze(2).broadcast_to(four)
                    own = pe_[:, :, :].unsqueeze(3).broadcast_to(four)
                    link(nc.vector.tensor_tensor(gt[:, :, :, :], theirs, own, ALU.is_gt))
                    link(nc.vector.tensor_tensor(ge[:, :, :, :], theirs, own, ALU.is_ge))
                    flat = lambda a: a[:, :, :, :].rearrange("p t e j -> p t (e j)")
                    link(nc.vector.tensor_tensor(flat(ge), flat(ge), before[:, :, :].broadcast_to([P, TPC, E * E]),
                                                 ALU.mult))
                    link(nc.vector.tensor_tensor(flat(gt), flat(gt), flat(ge), ALU.max))
                    link(nc.vector.tensor_reduce(rank[:, :, :], gt[:, :, :, :], AX.X, ALU.add))
                    nc.vector.scalar_tensor_tensor(wt[s][:, :, :], rank[:, :, :], 2.0, pe_[:, :, :],
                                                   ALU.is_lt, ALU.mult).then_inc(routed[s], 1)

                def split_turned(it, place):
                    dve.wait_ge(x1_rounded, it * 2 + place + 1)
                    nc.vector.tensor_tensor(x1p[LO][:, :, :], x1T[:, :, :], x1p[HI][:, :, :].bitcast(F32),
                                            ALU.subtract).then_inc(x1_split, 1)

                def gate_hidden(it, place, link, follow):
                    n = it * 2 + place

                    def split(f):
                        dve.wait_ge(h_rounded, n * KH + f + 1)
                        nc.vector.tensor_tensor(h1[LO][:, f, :], whole[f % 2][:, :], h1[HI][:, f, :].bitcast(F32),
                                                ALU.subtract).then_inc(h_split, 1)

                    for f in range(2 * KH):
                        p = pair_at(place, HIDDEN + f)
                        dve.wait_ge(sil_done[f % 2], n * KH + f // 2 + 1)
                        if f < KH:
                            dve.wait_ge(h_split, max(f - 1, 0) + n * KH)
                        nc.vector.tensor_tensor(whole[f % 2][:, :] if f < KH else hs[:, f - KH, :], sil[f % 2][:, :],
                                                pair[p][:, 1, :], ALU.mult).then_inc(free[p], 1)
                        if 1 <= f <= KH:
                            split(f - 1)
                        if follow and f >= KH and (f - KH) % 2 == 0:
                            head(it, place + 1, (f - KH) // 2, link)

                def sums(it, place, j, link):
                    s = place % 2
                    if j == 0:
                        dve.wait_ge(routed[s], it + place // 2 + 1)
                    for g in range(OUTS):
                        b, used = out_at(it, place, j, g)
                        dve.wait_ge(tile_made, (it * 2 + place) * TPC * OUTS + OUTS * j + g + 1)
                        if g < OUTS - 1:
                            link(nc.vector.scalar_tensor_tensor(
                                x1[s][:, j, :], ob[b][:, 0:D], wt[s][:, j, 2 * g:2 * g + 1],
                                x1[s][:, j, :], ALU.mult, ALU.add))
                            nc.vector.scalar_tensor_tensor(
                                x1[s][:, j, :], ob[b][:, D:2 * D], wt[s][:, j, 2 * g + 1:2 * g + 2],
                                x1[s][:, j, :], ALU.mult, ALU.add).then_inc(tile_free[b], 1)
                        else:
                            nc.vector.tensor_tensor(x1[s][:, j, :], ob[b][:, 0:D], x1[s][:, j, :], ALU.add)\
                                .then_inc(tile_free[b], 1)
                        dve.wait_ge(tile_free[b], used + 1)

                def final(it, place, link):
                    n = it * 2 + place
                    s = place % 2
                    dve.wait_ge(squared2, n * TPC + TPC)
                    nc.vector.tensor_scalar(ms2[:, :], ss2[:, :], 1.0 / D, RMS_EPS, ALU.mult, ALU.add)\
                        .then_inc(ms2_done, 1)
                    dve.wait_ge(sd2_done, n + 1)
                    link(nc.vector.reciprocal(rstd2[:, :], sd2[:, :]))
                    for j in range(TPC):
                        ins = nc.vector.scalar_tensor_tensor(x1[s][:, j, :], x1[s][:, j, :], rstd2[:, j:j + 1],
                                                             n2[:, :], ALU.mult, ALU.mult)
                    link(ins)
                    dve.wait_ge(ya_in[s], (it + place // 2) * 16 + 16)
                    nc.vector.tensor_tensor(ya[s][:, :, :], x1[s][:, :, :], ya[s][:, :, :], ALU.add)\
                        .then_inc(fin_done[s], 1)

                def step(it, place, link, follow, follow2):
                    sums(it, place, 0, link)
                    if follow:
                        residual(it, place + 1, link)
                    sums(it, place, 1, link)
                    if follow:
                        normalise(it, place + 1, link)
                    sums(it, place, 2, link)
                    if follow:
                        split_turned(it, place + 1)
                    sums(it, place, 3, link)
                    if follow:
                        route(it, place + 1, link)
                        gate_hidden(it, place + 1, link, follow2)
                    final(it, place, link)

                link = Links(0)
                for m in range(KD):
                    head(0, 0, m, link)
                residual(0, 0, link)
                normalise(0, 0, link)
                split_turned(0, 0)
                route(0, 0, link)
                gate_hidden(0, 0, link, True)
                assert link.n == FIRST, link.n
                with dve.Fori(0, TURNS) as it:
                    link = Links(it * (2 * STEP) + FIRST)
                    for s in range(2):
                        step(it, s, link, True, True)
                    assert link.n == 2 * STEP, link.n
                link = Links(TURNS * 2 * STEP + FIRST)
                step(TURNS, 0, link, True, False)
                step(TURNS, 1, link, False, False)


def layer(nc, x, w_kv_t, w_q, w_kc, w_vc, w_k, w_v, w_o, ws_in, ws_out, w1, w2, w_g, w_e, b_g, b_e, n1_w, n2_w,
          rope_cos, rope_sin, out):
    dram = lambda name, shape, dt=F32: nc.dram_tensor(name, shape, dt, kind="Internal").ap()
    tokens = x.rearrange("b s d -> (b s) d")
    xn_d = dram("xn_d", (N, D))
    xx_d = dram("xx_d", (N, D))
    xnT_d = dram("xnT_d", (D, N))
    kaT_d = dram("kaT_d", (D, N))
    va_d = dram("va_d", (N, D))
    vh_d = dram("vh_d", (N, H * VW))
    q_d = dram("q_d", (3, D, N), BF16)
    k_d = dram("k_d", (3, D, N), BF16)
    ya_d = dram("ya_d", (N, D))
    ot_d = dram("ot_d", (B * NG, P, S))
    project(nc, tokens, w_kv_t, w_q, w_kc, w_vc, w_k, w_v, rope_cos, rope_sin,
            xn_d, xx_d, xnT_d, kaT_d, va_d, vh_d, q_d, k_d)
    causal_attention(nc, xnT_d, kaT_d, va_d, xx_d, ya_d)
    with ExitStack() as ctx:
        ffw = FeedForwardWeights(nc, ctx, w_o, ws_in, w1, w2, w_g, w_e, b_g, b_e, n1_w, n2_w)
        head_attention(nc, q_d, k_d, vh_d, ot_d, ffw)
        feed_forward(nc, ot_d, xn_d, ya_d, ffw, ws_out, out.rearrange("b s d -> (b s) d"))


def rope_tables():
    import numpy as np
    inv = (1.0 / np.float32(10000.0) ** (np.arange(0, DH, 2, dtype=np.float32) / np.float32(DH))).astype(np.float32)
    angle = (np.arange(S, dtype=np.float32)[None, :] * inv[:, None]).astype(np.float32)
    row = np.arange(P) % DH
    sign = np.where(row % 2 == 0, -1.0, 1.0).astype(np.float32)
    cos = np.cos(angle.astype(np.float64)).astype(np.float32)[row // 2]
    sin = np.sin(angle.astype(np.float64)).astype(np.float32)[row // 2] * sign[:, None]
    return np.ascontiguousarray(cos), np.ascontiguousarray(sin)


_INS = ["L0_attn_x", "L0_attn_W", "L0_ffn_Wq", "L0_ffn_Wk_c", "L0_ffn_Wv_c", "L0_ffn_Wk", "L0_ffn_Wv", "L0_ffn_Wo",
        "L0_ffn_W_shared_in", "L0_ffn_W_shared_out", "L0_ffn_W1_shared", "L0_ffn_W2_experts", "L0_ffn_Wg_gate",
        "L0_ffn_We_gate", "L0_ffn_group_bias", "L0_ffn_expert_bias", "L0_ffn_norm1_w", "L0_ffn_norm2_w"]


def kernel(**inputs):
    import numpy as np
    import concourse.bacc as bacc
    from concourse.bass_utils import run_bass_kernel_spmd

    nc = bacc.Bacc("TRN2", target_bir_lowering=False, num_devices=1)
    arrays = {}
    for name in _INS:
        a = np.asarray(inputs[name])
        arrays["in_" + name] = np.ascontiguousarray(a.T if name == "L0_attn_W" else a)
    arrays["in_rope_cos"], arrays["in_rope_sin"] = rope_tables()
    args = [nc.dram_tensor(n, a.shape, mybir.dt.from_np(a.dtype), kind="ExternalInput").ap()
            for n, a in arrays.items()]
    out = nc.dram_tensor("out_dram", (B, S, D), F32, kind="ExternalOutput").ap()
    layer(nc, *args, out)
    r = run_bass_kernel_spmd(nc, [arrays], core_ids=[0])
    return r.results[0]["out_dram"]
```

```python
import concourse.bass as bass
from concourse import mybir
from contextlib import ExitStack, contextmanager

F32 = mybir.dt.float32
BF16 = mybir.dt.bfloat16
F32R = mybir.dt.float32r
ACT = mybir.ActivationFunctionType
ALU = mybir.AluOpType
AX = mybir.AxisListType

P = 128
B, S, D = 4, 1024, 256
N = B * S
CH = 512
NCH = N // CH
TPC = CH // P
KD = D // P
H, DH = 16, 16
GH = 4
NG = H // GH
VW = 2 * DH
HID, E = 512, 8
EPG = 4
KH = HID // P
GATES = 2 + E
DC = D // 4
QT = S // P
LN_EPS, RMS_EPS = 1e-5, 1e-6
MASKED = -3.0e38
HI, LO = 0, 1
PASSES = ((HI, HI), (HI, LO), (LO, HI))
QTERM = (0, 0, 1, 0, 2, 1)
KTERM = (0, 1, 0, 2, 0, 1)
NT = len(QTERM)
DOTS = NT * DH
SHIFT = 3


@contextmanager
def stage_semaphores(nc):
    taken = []

    def take(name):
        taken.append(nc.alloc_semaphore(name))
        return taken[-1]

    yield take
    nc.clear_and_free_semaphores(taken)
    nc.all_engine_barrier()


class Waits:

    def __init__(self, sp, passed):
        self.sp, self.passed = sp, passed

    def ge(self, sem, value):
        self.sp.wait_ge(sem, value)
        self.sp.sem_inc(self.passed, 1)


class HeadInputs:

    RING = 3
    AHEAD = RING - 1
    LOADS = 2 * NT

    def __init__(self, nc, ctx, q_d, k_d, vh_d):
        self.dram = (q_d, k_d, vh_d)
        self.q6, self.k6, self.vh = [], [], []
        self.values = ctx.enter_context(nc.sbuf_tensor("h_values", [P, QT, GH, DH], F32))
        for i in range(self.AHEAD):
            self.add_set(nc, ctx)

    def add_set(self, nc, ctx):
        i = len(self.vh)
        sb = lambda name, shape, dt: ctx.enter_context(nc.sbuf_tensor(f"{name}{i}", shape, dt))
        self.q6.append(sb("h_q", [P, GH, S], BF16))
        self.k6.append(sb("h_k", [P, GH, S], BF16))
        self.vh.append(sb("h_v", [P, QT, GH, VW], F32))

    def spare(self, i):
        return (self.q6, self.k6)[i % 2][i // 2][:, :, :].rearrange("p h t -> p (h t)").bitcast(F32)

    def spare_values(self, i):
        return self.vh[i][:, :, :, :].rearrange("p j h w -> p (j h w)")

    def at(self, eng, n):
        t0, h0 = (n // NG) * S, (n % NG) * GH
        return (t0, h0) if isinstance(n, int) else (eng.snap(t0), eng.snap(h0))

    def load(self, eng, n, r, signal, values_signal=None, at=None):
        q_d, k_d, _ = self.dram
        t0, h0 = at or self.at(eng, n)
        for t in range(NT):
            for dst, src, term in ((self.q6, q_d, QTERM[t]), (self.k6, k_d, KTERM[t])):
                eng.dma_start(dst[r][t * DH:(t + 1) * DH, :, :],
                              src[term, bass.ds(h0 * DH, GH * DH), bass.ds(t0, S)]
                              .rearrange("(h d) t -> d h t", d=DH)).then_inc(signal, 16)
        if values_signal is not None:
            self.load_values(eng, t0, h0, values_signal)

    def load_values(self, eng, t0, h0, signal):
        eng.dma_start(self.values[:, :, :, :].rearrange("p j h d -> p j (h d)"),
                      self.dram[2][bass.ds(t0, S), bass.ds(h0 * DH, GH * DH)]
                      .rearrange("(j p) c -> p j c", p=P)).then_inc(signal, 16)

    def places(self, r):
        return self.vh[r][:, :, :, 0:DH]


class Turning:

    LINKS = 9
    STORES = 6

    def __init__(self, nc, ctx, heads, q_d, k_d):
        sb = lambda name, shape, dt=F32: ctx.enter_context(nc.sbuf_tensor(name, shape, dt))
        self.nc = nc
        self.dram = (q_d, k_d)
        self.cos = sb("t_cos", [P, 2, CH])
        self.sin = sb("t_sin", [P, 2, CH])
        self.parts = [sb(f"t_parts{s}", [P, 3, 2 * KD, CH], BF16) for s in range(2)]
        spare = lambda i: heads.spare(i).rearrange("p (m n) -> p m n", n=CH)
        self.qk, self.swap, self.rot, self.rest = (spare(i) for i in range(4))

    def store(self, eng, t0, s, signal):
        cols = lambda a: a[:, bass.ds(t0, CH)].rearrange("(m p) t -> p m t", p=P)
        for r in range(3):
            for i, dst in enumerate(self.dram):
                eng.dma_start(cols(dst[r]), self.parts[s][:, r, i * KD:(i + 1) * KD, :]).then_inc(signal, 16)

    def finish(self, pool, link):
        gp, (parts0, parts1) = self.nc.gpsimd, self.parts
        table = lambda a: a[:, 1:2, :].broadcast_to([P, 2 * KD, CH])

        steps = iter(range(1, self.LINKS + 1))

        def step(ins):
            ins.then_inc(link, 1)
            pool.wait_ge(link, next(steps))

        def rests(parts):
            step(gp.tensor_tensor(self.rest, self.rot, parts[:, 0, :, :], ALU.subtract))
            step(gp.tensor_copy(parts[:, 1, :, :], self.rest))
            step(gp.tensor_tensor(parts[:, 2, :, :], self.rest, parts[:, 1, :, :], ALU.subtract))

        rests(parts0)
        gp.tensor_tensor(self.rot, self.qk, table(self.cos), ALU.mult)
        step(gp.tensor_tensor(self.swap, self.swap, table(self.sin), ALU.mult))
        step(gp.tensor_tensor(self.rot, self.rot, self.swap, ALU.add))
        step(gp.tensor_copy(parts1[:, 0, :, :], self.rot))
        rests(parts1)


def project(nc, x, w_kv_t, w_q, w_kc, w_vc, w_k, w_v, rope_cos, rope_sin,
            xn_d, xnT_d, kaT_d, va_d, vh_d, causal, turning):
    with ExitStack() as ctx:
        sb = lambda name, shape, dt=F32: ctx.enter_context(nc.sbuf_tensor(name, shape, dt))
        sem = ctx.enter_context(stage_semaphores(nc))
        sems = lambda name: [sem(f"{name}{s}") for s in range(2)]
        two = lambda name, shape, dt=F32: [sb(f"{name}{s}", shape, dt) for s in range(2)]
        wkv = sb("p_wkv", [P, KD, 2 * D])
        wq = sb("p_wq", [P, KD, D])
        wkvc = sb("p_wkvc", [P, KD, 2 * DC])
        wk = sb("p_wk", [P, D])
        wv = sb("p_wv", [P, D])
        cos, sin, parts = turning.cos, turning.sin, turning.parts
        qk, swap, rot, rest = turning.qk, turning.swap, turning.rot, turning.rest
        ident = sb("p_ident", [P, P])
        xin = two("p_xin", [P, TPC, D])
        xn = two("p_xn", [P, TPC, D])
        stats = sb("p_stats", [P, TPC, 6])
        fence = sb("p_fence", [P, 1])
        mv = sb("p_mv", [P, TPC, 2])
        veps = two("p_veps", [P, TPC])
        sd = two("p_sd", [P, TPC])
        rstd = sb("p_rstd", [P, TPC])
        xnT = two("p_xnT", [P, KD, CH])
        kaT = two("p_kaT", [P, KD, CH])
        va = two("p_va", [P, TPC, D])
        kvc = two("p_kvc", [P, CH])
        vh = two("p_vh", [P, TPC, D])
        ps = [ctx.enter_context(nc.psum_tensor(f"p_ps{i}", [P, 2, CH], F32)) for i in range(4)]
        T, KA, VA, Q, KVC, K, V = range(7)
        BANKS = {T: 0, KVC: 1, KA: 2, VA: 3, Q: 0, K: 1, V: 2}

        weights = sem("p_weights")
        tables = sem("p_tables")
        zeros_set = sem("p_zeros_set")
        ident_set = sem("p_ident_set")
        x_in = sems("p_x_in")
        xn_done = sems("p_xn_done")
        var_done = sems("p_var_done")
        sd_done = sems("p_sd_done")
        made = [sems(f"p_made{j}") for j in range(7)]
        taken = [sems(f"p_taken{j}") for j in range(7)]
        sw_done = sems("p_sw_done")
        sin_done = sems("p_sin_done")
        rot_done = sems("p_rot_done")
        hi_done = sems("p_hi_done")
        rest_done = sems("p_rest_done")
        mid_done = sems("p_mid_done")
        lo_done = sems("p_lo_done")
        st = {n: sems("p_st_" + n) for n in ("xn", "xnT", "kaT", "va", "vh", "parts")}
        chain = sem("p_chain")
        LINKS = 3
        TURNS = NCH // 2

        def near(it, s, d):
            return it + (s + d) // 2, (s + d) % 2

        def slots(eng, slot):
            for c in range(2):
                slot(0, c, c)
            with eng.Fori(1, TURNS - 1) as it:
                for s in range(2):
                    slot(it, s, None)
            for c in range(NCH - 2, NCH):
                slot(c // 2, c % 2, c)

        def exists(c, d):
            return c is None or 0 <= c + d < NCH

        causal_in = sem("p_causal_in")
        CAUSAL_FROM = NCH - 2
        passed = sem("p_passed")
        with nc.Block() as block:

            @block.gpsimd
            def _(pool):
                nc.gpsimd.memset(ident[:, :], 0.0).then_inc(ident_set, 1)
                pool.wait_ge(ident_set, 1)
                nc.gpsimd.affine_select(out=ident[:, :], in_=ident[:, :], compare_op=ALU.not_equal, fill=1.0,
                                        base=0, pattern=[[-1, P]], channel_multiplier=1).then_inc(ident_set, 1)
                pool.wait_ge(tables, 32)

                def sine(it, s):
                    pool.wait_ge(sw_done[s], it + 1)
                    for j in range(2 * KD):
                        last = nc.gpsimd.tensor_tensor(swap[:, j, :], swap[:, j, :], sin[:, s, :], ALU.mult)
                    last.then_inc(sin_done[s], 1)

                def slot(it, s, c):
                    if exists(c, -1):
                        sine(*near(it, s, -1))

                slots(pool, slot)

            @block.sync
            def _(sp):
                wait = Waits(sp, passed)
                rows = lambda a, t0: a[bass.ds(t0, CH), :].rearrange("(j p) d -> p j d", p=P)
                cols = lambda a, t0: a[:, bass.ds(t0, CH)].rearrange("(m p) t -> p m t", p=P)

                def load(it, s):
                    t0 = (it * 2 + s) * CH
                    sp.dma_start(xin[s][:, :, :], rows(x, t0)).then_inc(x_in[s], 16)

                def store_norm(it, s):
                    t0 = (it * 2 + s) * CH
                    wait.ge(xn_done[s], it + 1)
                    sp.dma_start(rows(xn_d, t0), xn[s][:, :, :]).then_inc(st["xn"][s], 16)

                def store_causal(it, s):
                    t0 = (it * 2 + s) * CH
                    wait.ge(taken[T][s], it + 1)
                    sp.dma_start(cols(xnT_d, t0), xnT[s][:, :, :]).then_inc(st["xnT"][s], 16)
                    wait.ge(taken[KA][s], it + 1)
                    sp.dma_start(cols(kaT_d, t0), kaT[s][:, :, :]).then_inc(st["kaT"][s], 16)
                    wait.ge(taken[VA][s], it + 1)
                    sp.dma_start(rows(va_d, t0), va[s][:, :, :]).then_inc(st["va"][s], 16)

                def store_values(it, s):
                    t0 = (it * 2 + s) * CH
                    wait.ge(taken[V][s], it + 1)
                    sp.dma_start(rows(vh_d, t0), vh[s][:, :, :]).then_inc(st["vh"][s], 16)

                def store_parts(it, s):
                    t0 = (it * 2 + s) * CH
                    wait.ge(lo_done[s], it + 1)
                    turning.store(sp, t0, s, st["parts"][s])

                def slot(it, s, c):
                    if c == CAUSAL_FROM:
                        for name in ("xnT", "kaT", "va"):
                            for half in range(2):
                                sp.wait_ge(st[name][half], -(-(c - half) // 2) * 16)
                        causal.load(sp, 0, 0, causal_in)
                    if exists(c, 2):
                        load(*near(it, s, 2))
                    if exists(c, 0):
                        store_causal(it, s)
                    if exists(c, -2):
                        store_parts(*near(it, s, -2))
                    if exists(c, 1):
                        store_norm(*near(it, s, 1))
                    if exists(c, 0):
                        store_values(it, s)

                load(0, 0)
                sp.dma_start(cos[:, :, :], rope_cos.rearrange("p (s n) -> p s n", s=2)).then_inc(tables, 16)
                sp.dma_start(sin[:, :, :], rope_sin.rearrange("p (s n) -> p s n", s=2)).then_inc(tables, 16)
                load(0, 1)
                store_norm(0, 0)
                slots(sp, slot)
                sp.wait_ge(causal_in, CausalInputs.LOADS * 16)
                for name, each in st.items():
                    for s in range(2):
                        sp.wait_ge(each[s], (NCH // 2 - 1) * 96 if name == "parts" else NCH // 2 * 16)

            @block.scalar
            def _(act):
                act.dma_start(wkv[:, :, :], w_kv_t.rearrange("(k p) m -> p k m", p=P)).then_inc(weights, 16)
                act.dma_start(wq[:, :, :], w_q.rearrange("(k p) m -> p k m", p=P)).then_inc(weights, 16)
                act.dma_start(wkvc[:, :, 0:DC], w_kc.rearrange("(k p) m -> p k m", p=P)).then_inc(weights, 16)
                act.dma_start(wkvc[:, :, DC:2 * DC], w_vc.rearrange("(k p) m -> p k m", p=P)).then_inc(weights, 16)
                act.wait_ge(zeros_set, 2)
                act.dma_start(wk[0:DC, :], w_k).then_inc(weights, 16)
                act.dma_start(wv[DC:2 * DC, :], w_v).then_inc(weights, 16)
                def root(it, s):
                    act.wait_ge(var_done[s], it + 1)
                    nc.scalar.activation(sd[s][:, :], veps[s][:, :], ACT.Sqrt).then_inc(sd_done[s], 1)

                def take(it, s, j):
                    dst, src, stored = {
                        T: (xnT[s][:, :, :], ps[BANKS[T]][:, :, :], "xnT"),
                        KA: (kaT[s][:, :, :], ps[BANKS[KA]][:, :, :], "kaT"),
                        VA: (va[s][:, :, :].rearrange("p j d -> p (j d)"),
                             ps[BANKS[VA]][:, :, :].rearrange("p a b -> p (a b)"), "va"),
                        Q: (qk[:, 0:KD, :], ps[BANKS[Q]][:, :, :], None),
                        KVC: (kvc[s][:, :], ps[BANKS[KVC]][:, 0, :], None),
                        K: (qk[:, KD:2 * KD, :], ps[BANKS[K]][:, :, :], None),
                        V: (vh[s][:, :, :].rearrange("p j d -> p (j d)"),
                            ps[BANKS[V]][:, :, :].rearrange("p a b -> p (a b)"), "vh")}[j]
                    act.wait_ge(made[j][s], it + 1)
                    if stored:
                        act.wait_ge(st[stored][s], it * 16)
                    nc.scalar.activation(dst, src, ACT.Copy).then_inc(taken[j][s], 1)

                def high(it, s):
                    act.wait_ge(rot_done[s], it + 1)
                    act.wait_ge(st["parts"][s], it * 96)
                    nc.scalar.activation(parts[s][:, 0, :, :], rot[:, :, :], ACT.Copy).then_inc(hi_done[s], 1)

                def middle(it, s):
                    act.wait_ge(rest_done[s], it + 1)
                    nc.scalar.activation(parts[s][:, 1, :, :], rest[:, :, :], ACT.Copy).then_inc(mid_done[s], 1)

                def slot(it, s, c):
                    if exists(c, 0):
                        take(it, s, KVC)
                        take(it, s, KA)
                    if exists(c, -2):
                        middle(*near(it, s, -2))
                    if exists(c, 0):
                        take(it, s, VA)
                    if exists(c, 1):
                        root(*near(it, s, 1))
                    if exists(c, 0):
                        if exists(c, -1):
                            before, half = near(it, s, -1)
                            act.wait_ge(sw_done[half], before + 1)
                        take(it, s, Q)
                        take(it, s, K)
                        if exists(c, 1):
                            take(*near(it, s, 1), T)
                        take(it, s, V)
                    if exists(c, -1):
                        high(*near(it, s, -1))

                root(0, 0)
                take(0, 0, T)
                slots(act, slot)

            @block.vector
            def _(dve):
                nc.vector.memset(wk[DC:2 * DC, :], 0.0).then_inc(zeros_set, 1)
                nc.vector.memset(wv[0:DC, :], 0.0).then_inc(zeros_set, 1)

                def link(ins, count):
                    ins.then_inc(chain, 1)
                    dve.wait_ge(chain, count)

                def variance(it, s):
                    n = it * 2 + s
                    dve.wait_ge(x_in[s], it * 16 + 16)
                    for j in range(TPC):
                        ins = nc.vector.bn_stats(stats[:, j, :], xin[s][:, j, :])
                    link(ins, n * LINKS + 1)
                    nc.vector.memset(fence[:, :], 0.0)
                    for j in range(TPC):
                        ins = nc.vector.bn_aggr(mv[:, j, :], stats[:, j, :])
                    link(ins, n * LINKS + 2)
                    nc.vector.tensor_scalar(veps[s][:, :], mv[:, :, 1], LN_EPS, None, ALU.add).then_inc(var_done[s], 1)

                def norm(it, s):
                    n = it * 2 + s
                    dve.wait_ge(sd_done[s], it + 1)
                    link(nc.vector.reciprocal(rstd[:, :], sd[s][:, :]), n * LINKS + 3)
                    dve.wait_ge(st["xn"][s], it * 16)
                    dve.wait_ge(made[T][s], it)
                    for j in range(TPC):
                        ins = nc.vector.tensor_scalar(xn[s][:, j, :], xin[s][:, j, :], mv[:, j, 0:1],
                                                      rstd[:, j:j + 1], ALU.subtract, ALU.mult)
                    ins.then_inc(xn_done[s], 1)

                def turn(it, s, before):
                    dve.wait_ge(taken[Q][s], it + 1)
                    dve.wait_ge(taken[K][s], it + 1)
                    if before:
                        dve.wait_ge(rest_done[before[1]], before[0] + 1)
                        dve.wait_ge(rot_done[before[1]], before[0] + 1)
                    nc.vector.tensor_tensor(rot[:, :, :], qk[:, :, :],
                                            cos[:, s:s + 1, :].broadcast_to([P, 2 * KD, CH]), ALU.mult)
                    partners(it, s)

                def partners(it, s):
                    nc.vector.stream_shuffle(swap[:, :, :], qk[:, :, :],
                                             [i ^ 1 for i in range(32)]).then_inc(sw_done[s], 1)

                def turned(it, s):
                    dve.wait_ge(sin_done[s], it + 1)
                    nc.vector.tensor_tensor(rot[:, :, :], rot[:, :, :], swap[:, :, :],
                                            ALU.add).then_inc(rot_done[s], 1)

                def first_rest(it, s, before):
                    dve.wait_ge(hi_done[s], it + 1)
                    if before:
                        dve.wait_ge(lo_done[before[1]], before[0] + 1)
                    nc.vector.tensor_tensor(rest[:, :, :], rot[:, :, :], parts[s][:, 0, :, :],
                                            ALU.subtract).then_inc(rest_done[s], 1)

                def low(it, s):
                    dve.wait_ge(mid_done[s], it + 1)
                    nc.vector.tensor_tensor(parts[s][:, 2, :, :], rest[:, :, :], parts[s][:, 1, :, :],
                                            ALU.subtract).then_inc(lo_done[s], 1)

                def slot(it, s, c):
                    if exists(c, -2):
                        first_rest(*near(it, s, -2), near(it, s, -3) if exists(c, -3) else None)
                    if exists(c, -1):
                        turn(*near(it, s, -1), near(it, s, -2) if exists(c, -2) else None)
                    if exists(c, 1):
                        variance(*near(it, s, 1))
                    if exists(c, 1):
                        norm(*near(it, s, 1))
                    if exists(c, -2):
                        low(*near(it, s, -2))
                    if exists(c, -1):
                        turned(*near(it, s, -1))

                variance(0, 0)
                norm(0, 0)
                slots(dve, slot)
                for j in (Q, K):
                    dve.wait_ge(taken[j][1], TURNS)
                dve.wait_ge(rot_done[0], TURNS)
                partners(TURNS - 1, 1)
                dve.wait_ge(sw_done[1], TURNS)

            @block.tensor
            def _(pe):
                def free(it, s, j):
                    if s:
                        pe.wait_ge(taken[j][0], it + 1)
                    else:
                        pe.wait_ge(taken[j][1], it)

                def product(j, s, out, lhs, rhs, signal):
                    for k in range(KD):
                        ins = nc.tensor.matmul(out, lhs(k), rhs(k), start=k == 0, stop=k == KD - 1)
                    if signal:
                        ins.then_inc(made[j][s], 1)

                def transposes(it, s, before):
                    pe.wait_ge(xn_done[s], it + 1)
                    if before:
                        pe.wait_ge(taken[Q][before[1]], before[0] + 1)
                    for m in range(KD):
                        for j in range(TPC):
                            ins = nc.tensor.transpose(ps[BANKS[T]][:, m, j * P:(j + 1) * P],
                                                      xn[s][:, j, m * P:(m + 1) * P], ident[:, :])
                    ins.then_inc(made[T][s], 1)

                def slot(it, s, c):
                    x_t = lambda k: xnT[s][:, k, :]
                    pe.wait_ge(taken[T][s], it + 1)
                    free(it, s, K)
                    product(KVC, s, ps[BANKS[KVC]][:, 0, :], lambda k: wkvc[:, k, :], x_t, True)
                    free(it, s, V)
                    for m in range(KD):
                        product(KA, s, ps[BANKS[KA]][:, m, :], lambda k: wkv[:, k, m * P:(m + 1) * P],
                                x_t, m == KD - 1)
                    free(it, s, VA)
                    for j in range(TPC):
                        product(VA, s, ps[BANKS[VA]][:, j // 2, (j % 2) * D:(j % 2 + 1) * D],
                                lambda k: xnT[s][:, k, j * P:(j + 1) * P], lambda k: wkv[:, k, D:2 * D],
                                j == TPC - 1)
                    for m in range(KD):
                        product(Q, s, ps[BANKS[Q]][:, m, :], lambda k: wq[:, k, m * P:(m + 1) * P],
                                x_t, m == KD - 1)
                    pe.wait_ge(taken[KVC][s], it + 1)
                    for m in range(KD):
                        ins = nc.tensor.matmul(ps[BANKS[K]][:, m, :], wk[:, m * P:(m + 1) * P],
                                               kvc[s][:, :], start=True, stop=True)
                    ins.then_inc(made[K][s], 1)
                    if exists(c, 1):
                        transposes(*near(it, s, 1), (it, s))
                    pe.wait_ge(taken[KA][s], it + 1)
                    for j in range(TPC):
                        ins = nc.tensor.matmul(ps[BANKS[V]][:, j // 2, (j % 2) * D:(j % 2 + 1) * D],
                                               kvc[s][:, j * P:(j + 1) * P], wv[:, :], start=True, stop=True)
                    ins.then_inc(made[V][s], 1)

                pe.wait_ge(ident_set, 2)
                transposes(0, 0, None)
                pe.wait_ge(weights, 6 * 16)
                slots(pe, slot)


class CausalInputs:

    LOADS = 4

    def __init__(self, nc, ctx, xnT_d, kaT_d, va_d, x):
        self.dram = (xnT_d, kaT_d, va_d, x)
        self.sets = []
        self.add_set(nc, ctx)

    def add_set(self, nc, ctx):
        s = len(self.sets)
        sb = lambda name, shape: ctx.enter_context(nc.sbuf_tensor(f"{name}{s}", shape, F32))
        self.sets.append((sb("c_qT", [P, KD, S]), sb("c_kT", [P, KD, S]),
                          sb("c_va", [P, QT, D]), sb("c_x", [P, QT, D])))

    def load(self, eng, b, s, signal):
        rows = lambda a: a[bass.ds(b * S, S), :].rearrange("(j p) d -> p j d", p=P)
        cols = lambda a: a[:, bass.ds(b * S, S)].rearrange("(m p) t -> p m t", p=P)
        for dst, src, view in zip(self.sets[s], self.dram, (cols, cols, rows, rows)):
            eng.dma_start(dst[:, :, :], view(src)).then_inc(signal, 16)


def causal_attention(nc, inputs, ya_d, heads, turning):
    with ExitStack() as ctx:
        sb = lambda name, shape, dt=F32: ctx.enter_context(nc.sbuf_tensor(name, shape, dt))
        sem = ctx.enter_context(stage_semaphores(nc))
        sems = lambda name: [sem(f"{name}{s}") for s in range(2)]
        two = lambda name, shape: [sb(f"{name}{s}", shape) for s in range(2)]
        ident = sb("a_ident", [P, P])
        mask = sb("a_mask", [P, P])
        inputs.add_set(nc, ctx)
        qT, kT, va, x = zip(*inputs.sets)
        negm = two("a_negm", [P, 1])
        probs = two("a_probs", [P, S])
        rowsum = two("a_rowsum", [P, 1])
        inv = two("a_inv", [P, 1])
        pT = [[sb(f"a_pT{s}_{part}", [P, QT, P], F32R) for part in (HI, LO)] for s in range(2)]
        vp = [[sb(f"a_v{s}_{part}", [P, QT, D], F32R) for part in (HI, LO)] for s in range(2)]
        ya = two("a_ya", [P, D])
        sc = [ctx.enter_context(nc.psum_tensor(f"a_sc{i}", [P, S], F32)) for i in range(2)]
        tp = [ctx.enter_context(nc.psum_tensor(f"a_tp{i}", [P, 4, P], F32)) for i in range(2)]
        out = [ctx.enter_context(nc.psum_tensor(f"a_out{i}", [P, CH], F32)) for i in range(2)]

        const_set = sem("a_const_set")
        loaded = sems("a_loaded")
        heads_in = sem("a_heads_in")
        turning_links = sem("a_turning_links")
        parts_stored = sem("a_parts_stored")
        values_in = sem("a_values_in")
        values_spread = sem("a_values_spread")
        sum_ones_set = sem("a_sum_ones_set")
        passed = sem("a_passed")
        scored = sems("a_scored")
        masked = sems("a_masked")
        max_done = sems("a_max_done")
        exp_done = sems("a_exp_done")
        turned = sems("a_turned")
        turned_rounded = sems("a_turned_rounded")
        turned_out = sems("a_turned_out")
        v_rounded = sems("a_v_rounded")
        v_split = sems("a_v_split")
        mixed = sems("a_mixed")
        inv_done = sems("a_inv_done")
        ya_done = sems("a_ya_done")
        ya_stored = sems("a_ya_stored")
        U = 2 * QT
        ORDER = [t for i in range(QT // 2) for t in (QT - 1 - i, i)]
        where = lambda u: (u // QT, ORDER[u % QT])
        GROUPS = [[(g, min(4, i + 1 - g)) for g in range(0, i + 1, 4)] for i in range(QT)]
        FIRST = [sum(len(GROUPS[where(v)[1]]) for v in range(u)) for u in range(U)]
        PER = FIRST[-1] + len(GROUPS[where(U - 1)[1]])
        assert PER % 2 == 0
        with nc.Block() as block:

            @block.gpsimd
            def _(pool):
                nc.gpsimd.memset(ident[:, :], 0.0).then_inc(const_set, 1)
                nc.gpsimd.memset(mask[:, :], 0.0).then_inc(const_set, 1)
                pool.wait_ge(const_set, 2)
                nc.gpsimd.affine_select(out=ident[:, :], in_=ident[:, :], compare_op=ALU.not_equal, fill=1.0,
                                        base=0, pattern=[[-1, P]], channel_multiplier=1).then_inc(const_set, 1)
                nc.gpsimd.affine_select(out=mask[:, :], in_=mask[:, :], compare_op=ALU.is_ge, fill=MASKED,
                                        base=0, pattern=[[-1, P]], channel_multiplier=1).then_inc(const_set, 1)
                turning.finish(pool, turning_links)
                for s in range(2):
                    turning.store(pool, (NCH - 2 + s) * CH, s, parts_stored)
                for n in range(HeadInputs.AHEAD):
                    heads.load(pool, n, n, heads_in)
                for n in range(HeadInputs.AHEAD):
                    nc.gpsimd.memset(heads.vh[n][:, :, :, :].rearrange("p j h w -> p (j h w)"), 1.0)\
                        .then_inc(sum_ones_set, 1)
                    pool.wait_ge(values_spread, n)
                    heads.load_values(pool, n // NG * S, n % NG * GH, values_in)
                    pool.wait_ge(values_in, (n + 1) * 16)
                    pool.wait_ge(sum_ones_set, n + 1)
                    nc.gpsimd.tensor_copy(heads.places(n), heads.values[:, :, :, :]).then_inc(values_spread, 1)
                pool.wait_ge(values_spread, HeadInputs.AHEAD)
                pool.wait_ge(parts_stored, 2 * Turning.STORES * 16)
                pool.wait_ge(heads_in, HeadInputs.AHEAD * HeadInputs.LOADS * 16)

            @block.sync
            def _(sp):
                wait = Waits(sp, passed)

                def turn(it, more):
                    for u in range(U):
                        s, i = where(u)
                        wait.ge(ya_done[u % 2], it * (U // 2) + u // 2 + 1)
                        sp.dma_start(ya_d[bass.ds((it * 2 + s) * S + i * P, P), :], ya[u % 2][:, :])\
                            .then_inc(ya_stored[u % 2], 16)
                        if more and u % QT == QT - 1:
                            inputs.load(sp, it * 2 + 2 + s, s, loaded[s])

                inputs.load(sp, 1, 1, loaded[1])
                with sp.Fori(0, B // 2 - 1) as it:
                    turn(it, True)
                turn(B // 2 - 1, False)
                for r in range(2):
                    sp.wait_ge(ya_stored[r], B * QT // 2 * 16)

            @block.tensor
            def _(pe):
                pe.wait_ge(const_set, 4)
                with pe.Fori(0, B // 2) as it:
                    def score(u):
                        s, i = where(u)
                        if u % QT == 0:
                            pe.wait_ge(loaded[s], (it + s) * CausalInputs.LOADS * 16)
                        pe.wait_ge(exp_done[u % 2], it * (U // 2) + u // 2)
                        n = (i + 1) * P
                        for c in range(0, n, CH):
                            w = min(CH, n - c)
                            for k in range(KD):
                                ins = nc.tensor.matmul(sc[u % 2][:, c:c + w], qT[s][:, k, i * P:(i + 1) * P],
                                                       kT[s][:, k, c:c + w], start=k == 0, stop=k == KD - 1)
                        ins.then_inc(scored[u % 2], 1)

                    score(0)
                    score(1)
                    for u in range(U):
                        s, i = where(u)
                        pe.wait_ge(exp_done[u % 2], it * (U // 2) + u // 2 + 1)
                        for g, (first, count) in enumerate(GROUPS[i]):
                            f = FIRST[u] + g
                            pe.wait_ge(turned_out[f % 2], it * (PER // 2) + f // 2)
                            for j in range(first, first + count):
                                ins = nc.tensor.transpose(tp[f % 2][:, j - first, :],
                                                          probs[u % 2][:, j * P:(j + 1) * P], ident[:, :])
                            ins.then_inc(turned[f % 2], 1)
                        if u + 2 < U:
                            score(u + 2)
                        pe.wait_ge(ya_done[u % 2], it * (U // 2) + u // 2)
                        if u % QT == 0:
                            pe.wait_ge(v_split[s], it + 1)
                        for g, (first, count) in enumerate(GROUPS[i]):
                            f = FIRST[u] + g
                            pe.wait_ge(turned_out[f % 2], it * (PER // 2) + f // 2 + 1)
                            for j in range(first, first + count):
                                for n, (left, right) in enumerate(PASSES):
                                    ins = nc.tensor.matmul(out[u % 2][:, 0:D], pT[u % 2][left][:, j, :],
                                                           vp[s][right][:, j, :], start=j == 0 and n == 0,
                                                           stop=j == i and n == len(PASSES) - 1)
                        ins.then_inc(mixed[u % 2], 1)

            @block.scalar
            def _(act):
                with act.Fori(0, B // 2) as it:
                    for u in range(U):
                        s, i = where(u)
                        if u % QT == 0:
                            act.wait_ge(loaded[s], (it + s) * CausalInputs.LOADS * 16)
                            nc.scalar.activation(vp[s][HI][:, :, :], va[s][:, :, :], ACT.Copy).then_inc(v_rounded[s], 1)
                        act.wait_ge(max_done[u % 2], it * (U // 2) + u // 2 + 1)
                        act.wait_ge(mixed[u % 2], it * (U // 2) + u // 2)
                        act.wait_ge(inv_done[u % 2], it * (U // 2) + u // 2)
                        nc.scalar.activation(probs[u % 2][:, 0:(i + 1) * P], sc[u % 2][:, 0:(i + 1) * P], ACT.Exp,
                                             bias=negm[u % 2][:, :], accum_out=rowsum[u % 2][:, :])\
                            .then_inc(exp_done[u % 2], 1)
                        for g, (first, count) in enumerate(GROUPS[i]):
                            f = FIRST[u] + g
                            act.wait_ge(turned[f % 2], it * (PER // 2) + f // 2 + 1)
                            nc.scalar.activation(pT[u % 2][HI][:, first:first + count, :], tp[f % 2][:, 0:count, :],
                                                 ACT.Copy).then_inc(turned_rounded[f % 2], 1)

            @block.vector
            def _(dve):
                dve.wait_ge(const_set, 4)
                with dve.Fori(0, B // 2) as it:
                    def maximum(u):
                        s, i = where(u)
                        dve.wait_ge(scored[u % 2], it * (U // 2) + u // 2 + 1)
                        diag = sc[u % 2][:, i * P:(i + 1) * P]
                        nc.vector.tensor_tensor(diag, diag, mask[:, :], ALU.add).then_inc(masked[u % 2], 1)
                        dve.wait_ge(masked[u % 2], it * (U // 2) + u // 2 + 1)
                        nc.vector.tensor_reduce(negm[u % 2][:, :], sc[u % 2][:, 0:(i + 1) * P], AX.X, ALU.max,
                                                negate=True).then_inc(max_done[u % 2], 1)

                    def finish(u):
                        s, i = where(u)
                        dve.wait_ge(mixed[u % 2], it * (U // 2) + u // 2 + 1)
                        dve.wait_ge(inv_done[u % 2], it * (U // 2) + u // 2 + 1)
                        dve.wait_ge(ya_stored[u % 2], (it * (U // 2) + u // 2) * 16)
                        nc.vector.scalar_tensor_tensor(ya[u % 2][:, :], out[u % 2][:, 0:D], inv[u % 2][:, :],
                                                       x[s][:, i, :], ALU.mult, ALU.add).then_inc(ya_done[u % 2], 1)

                    maximum(0)
                    maximum(1)
                    for u in range(U):
                        s, i = where(u)
                        if u % QT == 0:
                            dve.wait_ge(v_rounded[s], it + 1)
                            nc.vector.tensor_tensor(vp[s][LO][:, :, :], va[s][:, :, :],
                                                    vp[s][HI][:, :, :].bitcast(F32), ALU.subtract)\
                                .then_inc(v_split[s], 1)
                        dve.wait_ge(exp_done[u % 2], it * (U // 2) + u // 2 + 1)
                        dve.wait_ge(ya_done[u % 2], it * (U // 2) + u // 2)
                        nc.vector.reciprocal(inv[u % 2][:, :], rowsum[u % 2][:, :]).then_inc(inv_done[u % 2], 1)
                        for g, (first, count) in enumerate(GROUPS[i]):
                            f = FIRST[u] + g
                            at = (slice(None), slice(first, first + count), slice(None))
                            dve.wait_ge(turned_rounded[f % 2], it * (PER // 2) + f // 2 + 1)
                            nc.vector.tensor_tensor(pT[u % 2][LO][at], tp[f % 2][:, 0:count, :],
                                                    pT[u % 2][HI][at].bitcast(F32), ALU.subtract)\
                                .then_inc(turned_out[f % 2], 1)
                        if u >= 1:
                            finish(u - 1)
                        if u + 2 < U:
                            maximum(u + 2)
                    finish(U - 1)


class FeedForwardWeights:

    def __init__(self, nc, ctx, w_o, ws_in, w1, w2, w_g, w_e, b_g, b_e, n1_w, n2_w):
        sb = lambda name, shape, dt=F32: ctx.enter_context(nc.sbuf_tensor(name, shape, dt))
        self.out = sb("w_out", [P, KD, D])
        self.gate = sb("w_gate", [P, KD, GATES])
        self.bias = sb("w_bias", [P, 1, GATES])
        self.n1 = sb("w_n1", [P, D])
        self.n2 = sb("w_n2", [P, D])
        self.experts = [sb(f"w_experts{part}", [P, E, KH, D], F32R) for part in (HI, LO)]
        self.routed = [sb(f"w_routed{part}", [P, KD, 2 * HID], F32R) for part in (HI, LO)]
        self.shared = [sb(f"w_shared{part}", [P, KD, 2 * HID], F32R) for part in (HI, LO)]
        fan = lambda v: v.rearrange("(o n) -> o n", o=1).broadcast_to([P, v.shape[0]])
        part = lambda w: w.rearrange("(k p) m -> p k m", p=P)
        self.transfers = (
            (self.out[:, :, :], part(w_o)), (self.n1[:, :], fan(n1_w)), (self.n2[:, :], fan(n2_w)),
            (self.gate[:, :, 0:2], part(w_g)), (self.gate[:, :, 2:GATES], part(w_e)),
            (self.bias[:, 0, 0:2], fan(b_g)), (self.bias[:, 0, 2:GATES], fan(b_e)))
        self.pieces = [(part(w2[e]), [w[:, e, :, :] for w in self.experts]) for e in range(E)]
        for dst, src in ((self.routed, w1), (self.shared, ws_in)):
            self.pieces += [(src[k * P:(k + 1) * P, :], [w[:, k, :] for w in dst]) for k in range(KD)]


class FirstChunk:

    def __init__(self, nc, ctx, ot_d, xn_d):
        sb = lambda name, shape: ctx.enter_context(nc.sbuf_tensor(name, shape, F32))
        self.dram = (ot_d, xn_d)
        self.val = sb("i_val", [P, KD, CH])
        self.tot = sb("i_tot", [P, KD, CH])
        self.saT = sb("i_saT", [P, KD, CH])
        self.xn = sb("i_xn", [P, TPC, D])

    VALUES = 4 * KD * 16

    def load_values(self, eng, c, signal):
        for m in range(KD):
            for g in range(2):
                src = self.dram[0][(c // 2) * NG + 2 * m + g, :, bass.ds((c % 2) * CH, CH)]\
                    .rearrange("(h w) t -> h w t", w=VW)
                at = slice(g * P // 2, (g + 1) * P // 2)
                eng.dma_start(self.val[at, m, :], src[:, 0:DH, :]).then_inc(signal, 16)
                eng.dma_start(self.tot[at, m, :], src[:, DH:VW, :]).then_inc(signal, 16)

    def load_xn(self, eng, c, signal):
        eng.dma_start(self.xn[:, :, :], self.dram[1][bass.ds(c * CH, CH), :].rearrange("(j p) d -> p j d", p=P))\
            .then_inc(signal, 16)


def head_attention(nc, inputs, ot_d, ffw, first_chunk):
    with ExitStack() as ctx:
        sb = lambda name, shape, dt=F32: ctx.enter_context(nc.sbuf_tensor(name, shape, dt))
        sem = ctx.enter_context(stage_semaphores(nc))
        sems = lambda name, n: [sem(f"{name}{i}") for i in range(n)]
        RING = HeadInputs.RING
        STEPS = B * NG
        TURNS = (STEPS - 2) // RING
        NQ = S // CH
        UNITS = NQ * QT
        FILLS = UNITS * GH
        ITEMS = GH * QT * NQ
        BANKS = 3
        PER = ITEMS // UNITS
        LEAD = 4
        EARLY = LEAD * PER
        HELD = PER
        PR = 2
        LOADS = HeadInputs.LOADS
        AHEAD = HeadInputs.AHEAD
        SPLIT = 5
        inputs.add_set(nc, ctx)
        q6, k6, vh = inputs.q6, inputs.k6, inputs.vh
        probs = [sb(f"h_p{i}", [P, GH, CH]) for i in range(PR)]
        outT = [sb(f"h_o{i}", [P, CH]) for i in range(NQ)]
        ident = sb("h_ident", [P, P])
        one = sb("h_one", [P, 1], BF16)
        halfmax = sb("h_halfmax", [P, ITEMS])
        negm = sb("h_negm", [P, GH * QT])
        mT = sb("h_mT", [GH * QT, P])
        mrest = sb("h_mrest", [GH * QT, P])
        mparts = sb("h_mparts", [GH * QT, SHIFT, P], BF16)
        bank = lambda name: ctx.enter_context(nc.psum_tensor(name, [P, CH], F32))
        sk = [bank(f"h_sk{i}") for i in range(BANKS)]
        sq = [bank(f"h_sq{i}") for i in range(BANKS)]
        po = bank("h_po")
        pm = bank("h_pm")

        const_set = sem("h_const_set")
        ones_set = sem("h_ones_set")
        loaded = sems("h_loaded", RING)
        shifted = sems("h_shifted", RING)
        scored = sem("h_scored")
        exp_done = sems("h_exp_done", BANKS)
        pv_done = sems("h_pv_done", PR)
        out_taken = sem("h_out_taken")
        stored = sems("h_stored", NQ)
        item_scored = sem("h_item_scored")
        item_max = sems("h_item_max", BANKS)
        max_done = sem("h_max_done")
        m_turned = sem("h_m_turned")
        m_split = sem("h_m_split")
        piece = sb("h_piece", [P, KH * D])
        assert KH * D == 2 * HID
        piece_in = sem("h_piece_in")
        chunk_in = sem("h_chunk_in")
        sum_ones_set = sem("h_sum_ones_set")
        values_in = sem("h_values_in")
        spread_of = sems("h_spread_of", RING)
        inverted = sem("h_inverted")
        sa_made = sem("h_sa_made")
        others_in = sem("h_others_in")
        rounded = sem("h_rounded")
        rests_done = sem("h_rests_done")

        def steps(eng, step):
            with eng.Fori(0, TURNS) as it:
                for place in range(RING):
                    step(it, place, None)
            for n in range(TURNS * RING, STEPS):
                step(n // RING, n % RING, n)

        def exists(n, d):
            return n is None or n + d < STEPS

        passed = sem("h_passed")
        with nc.Block() as block:

            @block.gpsimd
            def _(pool):
                nc.gpsimd.memset(vh[RING - 1][:, :, :, :].rearrange("p j h w -> p (j h w)"), 1.0)\
                    .then_inc(sum_ones_set, 1)
                pool.wait_ge(sum_ones_set, 1)
                nc.gpsimd.memset(one[:, :], 1.0).then_inc(const_set, 1)
                nc.gpsimd.memset(ident[:, :], 0.0).then_inc(const_set, 1)
                pool.wait_ge(const_set, 2)
                nc.gpsimd.affine_select(out=ident[:, :], in_=ident[:, :], compare_op=ALU.not_equal, fill=1.0,
                                        base=0, pattern=[[-1, P]], channel_multiplier=1).then_inc(const_set, 1)
                for dst, src in ffw.transfers:
                    pool.dma_start(dst, src).then_inc(others_in, 16)
                for n, (src, (hi, lo)) in enumerate(ffw.pieces):
                    whole = piece[:, :].rearrange("p (k m) -> p k m", m=D) if len(src.shape) == 3 else piece[:, :]
                    pool.wait_ge(rests_done, n)
                    pool.dma_start(whole, src).then_inc(piece_in, 16)
                    pool.wait_ge(piece_in, n * 16 + 16)
                    nc.gpsimd.tensor_copy(hi, whole).then_inc(rounded, 1)
                    pool.wait_ge(rounded, n + 1)
                    nc.gpsimd.tensor_tensor(lo, whole, hi.bitcast(F32), ALU.subtract).then_inc(rests_done, 1)
                pool.wait_ge(rests_done, len(ffw.pieces))
                pool.wait_ge(others_in, len(ffw.transfers) * 16)

            @block.sync
            def _(sp):
                wait = Waits(sp, passed)
                def load(n, r, values_used):
                    at = inputs.at(sp, n)
                    if not isinstance(n, int) or n >= RING:
                        wait.ge(pv_done[(UNITS - 1) % PR], (n - RING + 1) * (UNITS // PR))
                    wait.ge(*values_used)
                    inputs.load(sp, n, r, loaded[r], values_in, at)

                def shift(n, r):
                    wait.ge(m_split, n * SPLIT + SPLIT)
                    for j in range(SHIFT):
                        sp.dma_start(q6[r][DOTS + j:DOTS + j + 1, :, :].rearrange("p h t -> p (h t)"),
                                     mparts[:, j, :]).then_inc(shifted[r], 16)

                shift(0, 0)
                def step(it, place, n):
                    k = it * RING + place
                    if n == STEPS - 2:
                        for c in range(NQ):
                            sp.wait_ge(stored[c], (n - 1) * 16)
                        first_chunk.load_values(sp, 0, chunk_in)
                        first_chunk.load_xn(sp, 0, chunk_in)
                    if exists(n, RING - 1):
                        last = place + AHEAD - 1
                        load(k + AHEAD, (place + AHEAD) % RING,
                             (spread_of[last % RING], it + last // RING + (last % RING >= AHEAD)))
                    if exists(n, 1):
                        shift(k + 1, (place + 1) % RING)

                steps(sp, step)

            @block.tensor
            def _(pe):
                pe.wait_ge(const_set, 3)

                def item(it, place, m):
                    h, i, half = m // (QT * NQ), m // NQ % QT, m % NQ
                    f = ITEMS * place + m
                    r = place % RING
                    pe.wait_ge(item_max[f % BANKS], it * ITEMS + f // BANKS)
                    nc.tensor.matmul(sq[f % BANKS][:, :], q6[r][0:DOTS, h, i * P:(i + 1) * P],
                                     k6[r][0:DOTS, h, half * CH:(half + 1) * CH],
                                     start=True, stop=True).then_inc(item_scored, 1)

                def turn_maxima(it, place):
                    n = it * RING + place
                    pe.wait_ge(max_done, n + 1)
                    pe.wait_ge(m_split, n * SPLIT)
                    nc.tensor.transpose(pm[0:GH * QT, 0:P], negm[:, :], ident[:, :]).then_inc(m_turned, 1)

                def mix(it, place, w):
                    c, j = divmod(w, QT)
                    if j == 0:
                        pe.wait_ge(out_taken, (it * RING + place) * NQ + c)
                    if w == 0:
                        pe.wait_ge(spread_of[place % RING], it + place // RING + (place % RING >= AHEAD))
                    last = FILLS * place + GH * w + GH - 1
                    for b in range(BANKS):
                        f = last - (last - b) % BANKS
                        pe.wait_ge(exp_done[b], it * FILLS + f // BANKS + 1)
                    for h in range(GH):
                        ins = nc.tensor.matmul(po[h * VW:(h + 1) * VW, :], vh[place % RING][:, j, h, :],
                                               probs[w % PR][:, h, :], start=j == 0, stop=j == QT - 1)
                    ins.then_inc(pv_done[w % PR], 1)

                def unit(it, place, w, n):
                    if w == 0:
                        pe.wait_ge(shifted[place % RING], (it + place // RING + 1) * SHIFT * 16)
                    c, j = divmod(w, QT)
                    early = w >= UNITS - LEAD
                    of = place + 1 + early
                    if early and w == UNITS - LEAD and exists(n, 2):
                        times = it + of // RING + (of % RING >= HeadInputs.AHEAD)
                        pe.wait_ge(loaded[of % RING], times * LOADS * 16)
                    for h in range(GH):
                        f = FILLS * place + GH * w + h
                        r = place % RING
                        pe.wait_ge(exp_done[f % BANKS], it * FILLS + f // BANKS)
                        nc.tensor.matmul(sk[f % BANKS][:, :], k6[r][0:DOTS + SHIFT, h, j * P:(j + 1) * P],
                                         q6[r][0:DOTS + SHIFT, h, c * CH:(c + 1) * CH],
                                         start=True, stop=True).then_inc(scored, 1)
                        if exists(n, 1 + early):
                            item(it, of, (w + LEAD) % UNITS * PER + h)

                def step(it, place, n):
                    for w in range(1, UNITS):
                        unit(it, place, w, n)
                        mix(it, place, w - 1)
                        if w == UNITS - LEAD and exists(n, 1):
                            turn_maxima(it, place + 1)
                    if exists(n, 1):
                        unit(it, place + 1, 0, n if n is None else n + 1)
                    mix(it, place, UNITS - 1)

                assert PER == GH and HELD == PER
                for m in range(ITEMS):
                    item(0, 0, m)
                for m in range(HELD):
                    item(0, 1, m)
                turn_maxima(0, 0)
                for m in range(HELD, EARLY):
                    item(0, 1, m)
                pe.wait_ge(ones_set, RING)
                unit(0, 0, 0, 0)
                steps(pe, step)

            @block.scalar
            def _(act):
                def fill(it, place, g):
                    w, h = divmod(g, GH)
                    if h == 0:
                        act.wait_ge(pv_done[w % PR], (it * RING + place) * (UNITS // PR) + w // PR)
                    f = FILLS * place + g
                    act.wait_ge(scored, it * (RING * FILLS) + f + 1)
                    nc.scalar.activation(probs[w % PR][:, h, :], sk[f % BANKS][:, :], ACT.Exp,
                                         scale=DH ** -0.5).then_inc(exp_done[f % BANKS], 1)

                def take_out(n, c):
                    w = (c + 1) * QT - 1
                    act.wait_ge(pv_done[w % PR], n * (UNITS // PR) + w // PR + 1)
                    act.wait_ge(stored[c], n * 16)
                    nc.scalar.activation(outT[c][:, :], po[:, :], ACT.Copy).then_inc(out_taken, 1)

                def store(n, c):
                    act.wait_ge(out_taken, n * NQ + c + 1)
                    act.dma_start(ot_d[n, :, c * CH:(c + 1) * CH], outT[c][:, :]).then_inc(stored[c], 16)

                TAKE = GH + 1
                SPREAD = FILLS // 2 - 2

                def step(it, place, n):
                    k = it * RING + place
                    for g in range(TAKE + 1, FILLS + TAKE + 1):
                        if g < FILLS:
                            fill(it, place, g)
                        elif exists(n, 1):
                            fill(it, place + 1, g - FILLS)
                        for c in range(NQ):
                            done = (c + 1) * QT * GH
                            if g == done + TAKE - 1:
                                take_out(k, c)
                            if g == done + TAKE:
                                store(k, c)
                        if g == SPREAD and exists(n, AHEAD):
                            r = (place + AHEAD) % RING
                            act.wait_ge(values_in, (k + 1) * 16)
                            nc.scalar.activation(inputs.places(r), inputs.values[:, :, :, :], ACT.Copy)\
                                .then_inc(spread_of[r], 1)

                act.wait_ge(const_set, 3)
                for keys in k6:
                    nc.scalar.activation(keys[DOTS:P, :, :].rearrange("p h t -> p (h t)"),
                                         one[DOTS:P, :].broadcast_to([P - DOTS, GH * S]), ACT.Copy)\
                        .then_inc(ones_set, 1)
                act.wait_ge(sum_ones_set, 1)
                for g in range(TAKE + 1):
                    fill(0, 0, g)
                steps(act, step)
                for c in range(NQ):
                    act.wait_ge(stored[c], STEPS * 16)

            @block.vector
            def _(dve):
                def maxima(it, place, first, end):
                    if first == 0:
                        dve.wait_ge(max_done, it * RING + place)
                    for m in range(first, end):
                        f = ITEMS * place + m
                        dve.wait_ge(item_scored, it * (RING * ITEMS) + f + 1)
                        nc.vector.tensor_reduce(halfmax[:, m:m + 1], sq[f % BANKS][:, :], AX.X, ALU.max)\
                            .then_inc(item_max[f % BANKS], 1)

                def larger(it, place):
                    last = ITEMS * place + ITEMS - 1
                    for b in range(BANKS):
                        f = last - (last - b) % BANKS
                        dve.wait_ge(item_max[b], it * ITEMS + f // BANKS + 1)
                    dve.wait_ge(m_turned, it * RING + place)
                    nc.vector.tensor_reduce(negm[:, :], halfmax[:, :].rearrange("p (t a) -> p t a", a=NQ),
                                            AX.X, ALU.max, negate=True).then_inc(max_done, 1)

                def split(it, place, stage):
                    n = it * RING + place
                    if stage == 0:
                        dve.wait_ge(m_turned, n + 1)
                    else:
                        dve.wait_ge(m_split, n * SPLIT + stage)
                    if stage == 1 and place:
                        dve.wait_ge(shifted[(place - 1) % RING], (it + (place - 1) // RING + 1) * SHIFT * 16)
                    if stage == 0:
                        ins = nc.vector.tensor_copy(mT[:, :], pm[0:GH * QT, 0:P])
                    elif stage == 1:
                        ins = nc.vector.tensor_copy(mparts[:, 0, :], mT[:, :])
                    elif stage == 2:
                        ins = nc.vector.tensor_tensor(mrest[:, :], mT[:, :], mparts[:, 0, :], ALU.subtract)
                    elif stage == 3:
                        ins = nc.vector.tensor_copy(mparts[:, 1, :], mrest[:, :])
                    else:
                        ins = nc.vector.tensor_tensor(mparts[:, 2, :], mrest[:, :], mparts[:, 1, :], ALU.subtract)
                    ins.then_inc(m_split, 1)

                def split_among(it, place, more):
                    for stage in range(SPLIT):
                        if more:
                            maxima(it, place + 1, HELD + stage, HELD + stage + 1)
                        split(it, place, stage)
                    if more:
                        maxima(it, place + 1, HELD + SPLIT, EARLY)

                def step(it, place, n):
                    if exists(n, 1):
                        maxima(it, place + 1, EARLY, ITEMS)
                        larger(it, place + 1)
                    if exists(n, 2):
                        maxima(it, place + 2, 0, HELD)
                    if exists(n, 1):
                        split_among(it, place + 1, exists(n, 2))

                maxima(0, 0, 0, ITEMS)
                larger(0, 0)
                maxima(0, 1, 0, HELD)
                split_among(0, 0, True)
                steps(dve, step)

                dve.wait_ge(chunk_in, FirstChunk.VALUES + 16)
                chunk = first_chunk
                nc.vector.reciprocal(chunk.tot[:, :, :], chunk.tot[:, :, :]).then_inc(inverted, 1)
                dve.wait_ge(inverted, 1)
                nc.vector.tensor_tensor(chunk.saT[:, :, :], chunk.val[:, :, :], chunk.tot[:, :, :], ALU.mult)\
                    .then_inc(sa_made, 1)
                dve.wait_ge(sa_made, 1)


def feed_forward(nc, inputs, heads, ya_d, ffw, ws_out, out):
    with ExitStack() as ctx:
        sb = lambda name, shape, dt=F32: ctx.enter_context(nc.sbuf_tensor(name, shape, dt))
        sem = ctx.enter_context(stage_semaphores(nc))
        sems = lambda name, n=2: [sem(f"{name}{s}") for s in range(n)]
        two = lambda name, shape, dt=F32: [sb(f"{name}{s}", shape, dt) for s in range(2)]
        R = GATES
        TURNS = NCH // 2 - 1
        wo, wr, bias, n1, n2 = ffw.out, ffw.gate, ffw.bias, ffw.n1, ffw.n2
        w2s = ffw.experts
        w_in = {"routed": ffw.routed, "shared": ffw.shared}
        wso = [sb(f"f_wso{part}", [P, KH, D], F32R) for part in (HI, LO)]
        ident = heads.spare_values(1)[:, 0:P]
        before = heads.spare_values(1)[:, P:P + E * E].rearrange("p (o n) -> p o n", o=1)
        val, tot, saT, xn = inputs.val, inputs.tot, inputs.saT, inputs.xn
        tiles = lambda i, n: heads.spare(i).rearrange("p (s m n) -> p s m n", s=2, n=n)
        ya = [tiles(0, D)[:, s] for s in range(2)]
        x1 = [tiles(1, D)[:, s] for s in range(2)]
        scratch = heads.spare(2)
        sil = [scratch[:, s * CH:(s + 1) * CH] for s in range(2)]
        sq, sq2 = (scratch[:, 2 * CH + s * D:2 * CH + (s + 1) * D] for s in range(2))
        gt, ge = (scratch[:, 3 * CH + s * D:3 * CH + (s + 1) * D].rearrange("p (t e j) -> p t e j", t=TPC, e=E)
                  for s in range(2))
        assert TPC * E * E == D
        wso_whole = heads.spare_values(0).rearrange("p (k m) -> p k m", m=D)
        x1T = tiles(3, CH)[:, 0]
        whole = [tiles(3, CH)[:, 1, s] for s in range(2)]
        ss = sb("f_ss", [P, TPC])
        ms = sb("f_ms", [P, TPC])
        sd = sb("f_sd", [P, TPC])
        rstd = sb("f_rstd", [P, TPC])
        x1p = [sb(f"f_x1p{part}", [P, KD, CH], F32R) for part in (HI, LO)]
        h = [sb(f"f_h{part}", [P, 2 * KH, CH], F32R) for part in (HI, LO)]
        lg = sb("f_lg", [P, TPC, R])
        gmax = sb("f_gmax", [P, TPC, 1])
        emax = sb("f_emax", [P, TPC, 2])
        ex = sb("f_ex", [P, TPC, R])
        exs = sb("f_exs", [P, TPC, R])
        gsum = sb("f_gsum", [P, TPC, 1])
        esum = sb("f_esum", [P, TPC, 2])
        ginv = sb("f_ginv", [P, TPC, 1])
        einv = sb("f_einv", [P, TPC, 2])
        gp = sb("f_gp", [P, TPC, 2])
        pe_ = sb("f_pe", [P, TPC, E])
        rank = sb("f_rank", [P, TPC, E])
        wt = two("f_wt", [P, TPC, E])
        ss2 = sb("f_ss2", [P, TPC])
        ms2 = sb("f_ms2", [P, TPC])
        sd2 = sb("f_sd2", [P, TPC])
        rstd2 = sb("f_rstd2", [P, TPC])
        pair = [ctx.enter_context(nc.psum_tensor(f"f_pair{i}", [P, 2, CH], F32)) for i in range(2)]
        ob = [ctx.enter_context(nc.psum_tensor(f"f_ob{i}", [P, CH], F32)) for i in range(4)]
        FILLS = 3 + 2 * KH
        OUTS = E // 2 + 1

        weights = sem("f_weights")
        const_set = sem("f_const_set")
        values_in = sem("f_values_in")
        xn_in = sem("f_xn_in")
        ya_in = sems("f_ya_in")
        ya_whole = sems("f_ya_whole")
        sa_done = sem("f_sa_done")
        SA = KH
        made = sem("f_made")
        free = sems("f_free")
        squared = sem("f_squared")
        ms_done = sem("f_ms_done")
        sd_done = sem("f_sd_done")
        x1_done = sems("f_x1_done")
        x1_rounded = sem("f_x1_rounded")
        x1_split = sem("f_x1_split")
        h_rounded = sem("f_h_rounded")
        h_split = sem("f_h_split")
        wso_rounded = sem("f_wso_rounded")
        wso_split = sem("f_wso_split")
        logits = sem("f_logits")
        exped = sem("f_exped")
        sil_done = sems("f_sil_done")
        routed = sems("f_routed")
        tile_made = sem("f_tile_made")
        tile_free = sems("f_tile_free", 4)
        squared2 = sem("f_squared2")
        ms2_done = sem("f_ms2_done")
        sd2_done = sem("f_sd2_done")
        fin_done = sems("f_fin_done")
        stored = sems("f_stored")
        chain = sem("f_chain")
        FIRST, STEP = 27, 41

        passed = sem("f_passed")
        with nc.Block() as block:

            pair_at = lambda place, j: (FILLS * place + j) % 2
            uses = lambda it, place, j: it * FILLS + (FILLS * place + j) // 2
            fills = lambda it, place, j: it * 2 * FILLS + FILLS * place + j
            WO, XT, GATE, HIDDEN = 0, 1, 2, 3

            @block.gpsimd
            def _(pool):
                nc.gpsimd.memset(ident[:, :], 0.0).then_inc(const_set, 1)
                nc.gpsimd.memset(before[:, :, :].rearrange("p o n -> p (o n)"), 1.0).then_inc(const_set, 1)
                pool.wait_ge(const_set, 2)
                nc.gpsimd.affine_select(out=ident[:, :], in_=ident[:, :], compare_op=ALU.not_equal, fill=1.0,
                                        base=0, pattern=[[-1, P]], channel_multiplier=1).then_inc(const_set, 1)
                b2 = before[:, 0, :].rearrange("p (e j) -> p e j", j=E)
                nc.gpsimd.affine_select(out=b2, in_=b2, compare_op=ALU.is_gt, fill=0.0,
                                        base=0, pattern=[[1, E], [-1, E]], channel_multiplier=0).then_inc(const_set, 1)
                pool.wait_ge(weights, 16)
                nc.gpsimd.tensor_copy(wso[HI][:, :, :], wso_whole).then_inc(wso_rounded, 1)
                pool.wait_ge(wso_rounded, 1)
                nc.gpsimd.tensor_tensor(wso[LO][:, :, :], wso_whole, wso[HI][:, :, :].bitcast(F32), ALU.subtract)\
                    .then_inc(wso_split, 1)
                with pool.Fori(0, NCH // 2) as it:
                    for s in range(2):
                        pool.wait_ge(xn_in, (it * 2 + s) * 16)
                        pool.wait_ge(ya_in[s], it * 16 + 16)
                        nc.gpsimd.tensor_tensor(ya[s], ya[s], xn[:, :, :], ALU.add).then_inc(ya_whole[s], 1)
                        for f in range(2 * KH):
                            pool.wait_ge(h_rounded, (it * 2 + s) * (2 * KH) + f + 1)
                            nc.gpsimd.tensor_tensor(h[LO][:, f, :], whole[f % 2], h[HI][:, f, :].bitcast(F32),
                                                    ALU.subtract).then_inc(h_split, 1)

            @block.sync
            def _(sp):
                wait = Waits(sp, passed)
                sp.dma_start(wso_whole, ws_out.rearrange("(k p) m -> p k m", p=P)).then_inc(weights, 16)
                rows = lambda a, c: a[bass.ds(c * CH, CH), :].rearrange("(j p) d -> p j d", p=P)

                load_values = lambda c: inputs.load_values(sp, c, values_in)
                load_xn = lambda c: inputs.load_xn(sp, c, xn_in)

                def load_ya(c, s):
                    sp.dma_start(ya[s][:, :, :], rows(ya_d, c)).then_inc(ya_in[s], 16)

                def store(it, s):
                    wait.ge(fin_done[s], it + 1)
                    sp.dma_start(rows(out, it * 2 + s), ya[s][:, :, :]).then_inc(stored[s], 16)

                load_values(1)
                for s in range(2):
                    load_ya(s, s)
                sp.wait_ge(free[pair_at(0, WO)], 1)
                sp.wait_ge(ya_whole[0], 1)
                load_xn(1)
                sp.wait_ge(sa_done, SA)
                load_values(2)
                for first, turns in ((0, TURNS - 1), (TURNS - 1, 1)):
                    with sp.Fori(first, first + turns) as it:
                        for s in range(2):
                            c = it * 2 + s
                            wait.ge(free[pair_at(s + 1, WO)], uses(it, s + 1, WO) + 1)
                            wait.ge(ya_whole[(s + 1) % 2], it + (s + 1) // 2 + 1)
                            load_xn(c + 2)
                            if first == 0 or s == 0:
                                wait.ge(sa_done, (c + 2) * SA)
                                load_values(c + 3)
                            store(it, s)
                            wait.ge(stored[s], it * 16 + 16)
                            load_ya(c + 2, s)
                for s in range(2):
                    store(TURNS, s)
                for s in range(2):
                    sp.wait_ge(stored[s], (TURNS + 1) * 16)

            VALUES = FirstChunk.VALUES
            def out_at(it, place, j, g):
                f = OUTS * (TPC * place + j) + g
                return f % 4, it * (2 * OUTS * TPC // 4) + f // 4

            @block.tensor
            def _(pe):
                def begin(it, place, j):
                    pe.wait_ge(free[pair_at(place, j)], uses(it, place, j))
                    return pair[pair_at(place, j)]

                def out_projection(it, place):
                    pe.wait_ge(sa_done, (it * 2 + place) * SA)
                    ps = begin(it, place, WO)
                    for j in range(TPC):
                        for k in range(KD):
                            ins = nc.tensor.matmul(ps[:, j // 2, (j % 2) * D:(j % 2 + 1) * D],
                                                   saT[:, k, j * P:(j + 1) * P], wo[:, k, :],
                                                   start=k == 0, stop=k == KD - 1)
                    ins.then_inc(made, 1)

                def turn(it, place):
                    s = place % 2
                    pe.wait_ge(x1_done[s], it + place // 2 + 1)
                    ps = begin(it, place, XT)
                    for m in range(KD):
                        for j in range(TPC):
                            ins = nc.tensor.transpose(ps[:, m, j * P:(j + 1) * P],
                                                      x1[s][:, j, m * P:(m + 1) * P], ident[:, :])
                    ins.then_inc(made, 1)

                def gates(it, place):
                    pe.wait_ge(free[pair_at(place, XT)], uses(it, place, XT) + 1)
                    ps = begin(it, place, GATE)
                    for j in range(TPC):
                        for k in range(KD):
                            ins = nc.tensor.matmul(ps[:, 0, j * R:(j + 1) * R], x1T[:, k, j * P:(j + 1) * P],
                                                   wr[:, k, :], start=k == 0, stop=k == KD - 1)
                    ins.then_inc(made, 1)

                def hidden(it, place):
                    pe.wait_ge(x1_split, it * 2 + place + 1)
                    for f in range(2 * KH):
                        w = w_in["routed" if f < KH else "shared"]
                        ps = begin(it, place, HIDDEN + f)
                        for half in range(2):
                            at = half * HID + f % KH * P
                            terms = [(k, a, b) for k in range(KD) for a, b in PASSES]
                            for n, (k, a, b) in enumerate(terms):
                                ins = nc.tensor.matmul(ps[:, half, :], w[a][:, k, at:at + P], x1p[b][:, k, :],
                                                       start=n == 0, stop=n == len(terms) - 1)
                        ins.then_inc(made, 1)

                def outputs(it, place, j):
                    for g in range(OUTS):
                        b, used = out_at(it, place, j, g)
                        pe.wait_ge(tile_free[b], used)
                        if g == 0 and j == 0:
                            pe.wait_ge(h_split, (it * 2 + place) * (2 * KH) + KH)
                        if g == OUTS - 1 and j == 0:
                            pe.wait_ge(h_split, (it * 2 + place) * (2 * KH) + 2 * KH)
                        at = slice(j * P, (j + 1) * P)
                        shared = g == OUTS - 1
                        to = ob[b][:, 0:D] if shared else ob[b][:, :]
                        terms = [(k, left, right) for k in range(KH) for left, right in PASSES]
                        for n, (k, left, right) in enumerate(terms):
                            weight = wso[right][:, k, :] if shared else w2s[right][:, 2 * g:2 * g + 2, k, :]
                            ins = nc.tensor.matmul(to, h[left][:, KH * shared + k, at], weight,
                                                   start=n == 0, stop=n == len(terms) - 1)
                        ins.then_inc(tile_made, 1)

                def step(it, place, follow):
                    outputs(it, place, 0)
                    if follow:
                        out_projection(it, place + 1)
                    outputs(it, place, 1)
                    outputs(it, place, 2)
                    if follow:
                        turn(it, place + 1)
                    outputs(it, place, 3)
                    if follow:
                        gates(it, place + 1)
                        hidden(it, place + 1)

                pe.wait_ge(const_set, 4)
                out_projection(0, 0)
                turn(0, 0)
                gates(0, 0)
                pe.wait_ge(wso_split, 1)
                hidden(0, 0)
                with pe.Fori(0, TURNS) as it:
                    for s in range(2):
                        step(it, s, True)
                step(TURNS, 0, True)
                step(TURNS, 1, False)

            @block.scalar
            def _(act):
                def squares(it, place):
                    n = it * 2 + place
                    act.wait_ge(free[pair_at(place, WO)], uses(it, place, WO) + 1)
                    for j in range(TPC):
                        nc.scalar.activation(sq[:, :], x1[place % 2][:, j, :], ACT.Square,
                                             accum_out=ss[:, j:j + 1]).then_inc(squared, 1)
                        act.wait_ge(squared, n * TPC + j + 1)
                    act.wait_ge(ms_done, n + 1)
                    nc.scalar.activation(sd[:, :], ms[:, :], ACT.Sqrt).then_inc(sd_done, 1)

                def take_turned(it, place):
                    n = it * 2 + place
                    used = free[pair_at(place, XT)]
                    act.wait_ge(made, fills(it, place, XT) + 1)
                    act.wait_ge(x1_split, n)
                    nc.scalar.activation(x1T[:, :, :], pair[pair_at(place, XT)][:, :, :], ACT.Copy).then_inc(used, 1)
                    act.wait_ge(used, uses(it, place, XT) + 1)
                    nc.scalar.activation(x1p[HI][:, :, :], x1T[:, :, :], ACT.Copy).then_inc(x1_rounded, 1)

                def hidden(it, place):
                    n = it * 2 + place
                    act.wait_ge(logits, n + 1)
                    nc.scalar.activation(ex[:, :, :], exs[:, :, :], ACT.Exp).then_inc(exped, 1)
                    def first_part(f):
                        act.wait_ge(free[pair_at(place, HIDDEN + f)], uses(it, place, HIDDEN + f) + 1)
                        nc.scalar.activation(h[HI][:, f, :], whole[f % 2], ACT.Copy).then_inc(h_rounded, 1)

                    for f in range(2 * KH):
                        act.wait_ge(made, fills(it, place, HIDDEN + f) + 1)
                        j, before = (HIDDEN + f - 2, place) if f >= 2 else (HIDDEN + f - 2 + 2 * KH, place - 1)
                        act.wait_ge(free[pair_at(before, j)], uses(it, before, j) + 1)
                        nc.scalar.activation(sil[f % 2], pair[pair_at(place, HIDDEN + f)][:, 0, :], ACT.Silu)\
                            .then_inc(sil_done[f % 2], 1)
                        if f:
                            first_part(f - 1)
                    first_part(2 * KH - 1)

                def final(it, place):
                    n = it * 2 + place
                    s = place % 2
                    b, used = out_at(it, place, TPC - 1, OUTS - 1)
                    act.wait_ge(tile_free[b], used + 1)
                    for j in range(TPC):
                        nc.scalar.activation(sq2[:, :], x1[s][:, j, :], ACT.Square,
                                             accum_out=ss2[:, j:j + 1]).then_inc(squared2, 1)
                        act.wait_ge(squared2, n * TPC + j + 1)
                    act.wait_ge(ms2_done, n + 1)
                    nc.scalar.activation(sd2[:, :], ms2[:, :], ACT.Sqrt).then_inc(sd2_done, 1)

                def step(it, place, follow):
                    if follow:
                        squares(it, place + 1)
                        take_turned(it, place + 1)
                        hidden(it, place + 1)
                    final(it, place)

                squares(0, 0)
                take_turned(0, 0)
                hidden(0, 0)
                with act.Fori(0, TURNS) as it:
                    for s in range(2):
                        step(it, s, True)
                step(TURNS, 0, True)
                step(TURNS, 1, False)

            @block.vector
            def _(dve):
                dve.wait_ge(const_set, 4)

                class Links:

                    def __init__(self, base):
                        self.base, self.n = base, 0

                    def __call__(self, ins):
                        self.n += 1
                        ins.then_inc(chain, 1)
                        dve.wait_ge(chain, self.base + self.n)

                def head(it, place, q, link):
                    if q == 0:
                        dve.wait_ge(values_in, (it * 2 + place) * VALUES)
                    at = (slice(None), q // 2, slice(q % 2 * (CH // 2), (q % 2 + 1) * (CH // 2)))
                    link(nc.vector.reciprocal(tot[at], tot[at]))
                    nc.vector.tensor_tensor(saT[at], val[at], tot[at], ALU.mult).then_inc(sa_done, 1)

                def residual(it, place, link):
                    s = place % 2
                    dve.wait_ge(made, fills(it, place, WO) + 1)
                    dve.wait_ge(xn_in, (it * 2 + place) * 16)
                    dve.wait_ge(fin_done[s], it + place // 2)
                    nc.vector.tensor_tensor(x1[s][:, :, :].rearrange("p j d -> p (j d)"),
                                            pair[pair_at(place, WO)][:, :, :].rearrange("p a b -> p (a b)"),
                                            xn[:, :, :].rearrange("p j d -> p (j d)"), ALU.add)\
                        .then_inc(free[pair_at(place, WO)], 1)

                def normalise(it, place, link):
                    n = it * 2 + place
                    s = place % 2
                    dve.wait_ge(squared, n * TPC + TPC)
                    nc.vector.tensor_scalar(ms[:, :], ss[:, :], 1.0 / D, RMS_EPS, ALU.mult, ALU.add)\
                        .then_inc(ms_done, 1)
                    dve.wait_ge(sd_done, n + 1)
                    link(nc.vector.reciprocal(rstd[:, :], sd[:, :]))
                    for j in range(TPC):
                        ins = nc.vector.scalar_tensor_tensor(x1[s][:, j, :], x1[s][:, j, :], rstd[:, j:j + 1], n1[:, :],
                                                             ALU.mult, ALU.mult)
                    ins.then_inc(x1_done[s], 1)

                def route(it, place, link):
                    ps = pair[pair_at(place, GATE)]
                    done = uses(it, place, GATE) + 1
                    dve.wait_ge(made, fills(it, place, GATE) + 1)
                    nc.vector.tensor_tensor(lg[:, :, :], ps[:, 0, 0:TPC * R].rearrange("p (j r) -> p j r", r=R),
                                            bias[:, :, :].broadcast_to([P, TPC, R]), ALU.add)\
                        .then_inc(free[pair_at(place, GATE)], 1)
                    dve.wait_ge(free[pair_at(place, GATE)], done)
                    link(nc.vector.tensor_reduce(gmax[:, :, 0], lg[:, :, 0:2], AX.X, ALU.max))
                    for g in range(2):
                        link(nc.vector.tensor_reduce(emax[:, :, g], lg[:, :, 2 + g * EPG:2 + (g + 1) * EPG],
                                                     AX.X, ALU.max))
                    nc.vector.tensor_tensor(exs[:, :, 0:2], lg[:, :, 0:2], gmax[:, :, :].broadcast_to([P, TPC, 2]),
                                            ALU.subtract)
                    for g in range(2):
                        at = slice(2 + g * EPG, 2 + (g + 1) * EPG)
                        ins = nc.vector.tensor_tensor(exs[:, :, at], lg[:, :, at],
                                                      emax[:, :, g:g + 1].broadcast_to([P, TPC, EPG]), ALU.subtract)
                    ins.then_inc(logits, 1)

                def weigh(it, place, link):
                    s = place % 2
                    four = [P, TPC, E, E]
                    dve.wait_ge(exped, it * 2 + place + 1)
                    link(nc.vector.tensor_reduce(gsum[:, :, 0], ex[:, :, 0:2], AX.X, ALU.add))
                    link(nc.vector.tensor_reduce(esum[:, :, :],
                                                 ex[:, :, 2:R].rearrange("p t (g e) -> p t g e", g=2), AX.X, ALU.add))
                    link(nc.vector.reciprocal(ginv[:, :, :], gsum[:, :, :]))
                    link(nc.vector.reciprocal(einv[:, :, :], esum[:, :, :]))
                    link(nc.vector.tensor_tensor(gp[:, :, 0], ex[:, :, 0], ex[:, :, 1], ALU.is_ge))
                    link(nc.vector.tensor_scalar(gp[:, :, 1], gp[:, :, 0], -1.0, 1.0, ALU.mult, ALU.add))
                    link(nc.vector.tensor_tensor(gp[:, :, :], gp[:, :, :], ginv[:, :, :].broadcast_to([P, TPC, 2]),
                                                 ALU.mult))
                    link(nc.vector.tensor_tensor(gp[:, :, :], gp[:, :, :], einv[:, :, :], ALU.mult))
                    for g in range(2):
                        at = slice(g * EPG, (g + 1) * EPG)
                        link(nc.vector.tensor_tensor(pe_[:, :, at], ex[:, :, 2 + g * EPG:2 + (g + 1) * EPG],
                                                     gp[:, :, g:g + 1].broadcast_to([P, TPC, EPG]), ALU.mult))
                    theirs = pe_[:, :, :].unsqueeze(2).broadcast_to(four)
                    own = pe_[:, :, :].unsqueeze(3).broadcast_to(four)
                    link(nc.vector.tensor_tensor(gt[:, :, :, :], theirs, own, ALU.is_gt))
                    link(nc.vector.tensor_tensor(ge[:, :, :, :], theirs, own, ALU.is_ge))
                    flat = lambda a: a[:, :, :, :].rearrange("p t e j -> p t (e j)")
                    link(nc.vector.tensor_tensor(flat(ge), flat(ge), before[:, :, :].broadcast_to([P, TPC, E * E]),
                                                 ALU.mult))
                    link(nc.vector.tensor_tensor(flat(gt), flat(gt), flat(ge), ALU.max))
                    link(nc.vector.tensor_reduce(rank[:, :, :], gt[:, :, :, :], AX.X, ALU.add))
                    nc.vector.scalar_tensor_tensor(wt[s][:, :, :], rank[:, :, :], 2.0, pe_[:, :, :],
                                                   ALU.is_lt, ALU.mult).then_inc(routed[s], 1)

                def split_turned(it, place):
                    dve.wait_ge(x1_rounded, it * 2 + place + 1)
                    nc.vector.tensor_tensor(x1p[LO][:, :, :], x1T[:, :, :], x1p[HI][:, :, :].bitcast(F32),
                                            ALU.subtract).then_inc(x1_split, 1)

                def gate_hidden(it, place, link, follow):
                    n = it * 2 + place

                    for f in range(2 * KH):
                        p = pair_at(place, HIDDEN + f)
                        dve.wait_ge(sil_done[f % 2], n * KH + f // 2 + 1)
                        dve.wait_ge(h_split, max(f - 1, 0) + n * (2 * KH))
                        nc.vector.tensor_tensor(whole[f % 2], sil[f % 2], pair[p][:, 1, :], ALU.mult)\
                            .then_inc(free[p], 1)
                        if follow and f >= KH:
                            head(it, place + 1, f - KH, link)

                def sums(it, place, j, link):
                    s = place % 2
                    if j == 0:
                        dve.wait_ge(routed[s], it + place // 2 + 1)
                    for g in range(OUTS):
                        b, used = out_at(it, place, j, g)
                        dve.wait_ge(tile_made, (it * 2 + place) * TPC * OUTS + OUTS * j + g + 1)
                        if g < OUTS - 1:
                            link(nc.vector.scalar_tensor_tensor(
                                x1[s][:, j, :], ob[b][:, 0:D], wt[s][:, j, 2 * g:2 * g + 1],
                                x1[s][:, j, :], ALU.mult, ALU.add))
                            nc.vector.scalar_tensor_tensor(
                                x1[s][:, j, :], ob[b][:, D:2 * D], wt[s][:, j, 2 * g + 1:2 * g + 2],
                                x1[s][:, j, :], ALU.mult, ALU.add).then_inc(tile_free[b], 1)
                        else:
                            nc.vector.tensor_tensor(x1[s][:, j, :], ob[b][:, 0:D], x1[s][:, j, :], ALU.add)\
                                .then_inc(tile_free[b], 1)
                        dve.wait_ge(tile_free[b], used + 1)

                def final(it, place, link):
                    n = it * 2 + place
                    s = place % 2
                    dve.wait_ge(squared2, n * TPC + TPC)
                    nc.vector.tensor_scalar(ms2[:, :], ss2[:, :], 1.0 / D, RMS_EPS, ALU.mult, ALU.add)\
                        .then_inc(ms2_done, 1)
                    dve.wait_ge(sd2_done, n + 1)
                    link(nc.vector.reciprocal(rstd2[:, :], sd2[:, :]))
                    for j in range(TPC):
                        ins = nc.vector.scalar_tensor_tensor(x1[s][:, j, :], x1[s][:, j, :], rstd2[:, j:j + 1],
                                                             n2[:, :], ALU.mult, ALU.mult)
                    link(ins)
                    dve.wait_ge(ya_whole[s], it + place // 2 + 1)
                    nc.vector.tensor_tensor(ya[s][:, :, :], x1[s][:, :, :], ya[s][:, :, :], ALU.add)\
                        .then_inc(fin_done[s], 1)

                def step(it, place, link, follow, follow2):
                    if follow:
                        residual(it, place + 1, link)
                    sums(it, place, 1, link)
                    if follow:
                        normalise(it, place + 1, link)
                    sums(it, place, 2, link)
                    if follow:
                        split_turned(it, place + 1)
                    sums(it, place, 3, link)
                    if follow:
                        route(it, place + 1, link)
                        gate_hidden(it, place + 1, link, follow2)
                        weigh(it, place + 1, link)
                        sums(it, place + 1, 0, link)
                    final(it, place, link)

                link = Links(0)
                residual(0, 0, link)
                normalise(0, 0, link)
                split_turned(0, 0)
                route(0, 0, link)
                gate_hidden(0, 0, link, True)
                weigh(0, 0, link)
                sums(0, 0, 0, link)
                assert link.n == FIRST, link.n
                with dve.Fori(0, TURNS) as it:
                    link = Links(it * (2 * STEP) + FIRST)
                    for s in range(2):
                        step(it, s, link, True, True)
                    assert link.n == 2 * STEP, link.n
                link = Links(TURNS * 2 * STEP + FIRST)
                step(TURNS, 0, link, True, False)
                step(TURNS, 1, link, False, False)


def layer(nc, x, w_kv_t, w_q, w_kc, w_vc, w_k, w_v, w_o, ws_in, ws_out, w1, w2, w_g, w_e, b_g, b_e, n1_w, n2_w,
          rope_cos, rope_sin, out):
    dram = lambda name, shape, dt=F32: nc.dram_tensor(name, shape, dt, kind="Internal").ap()
    tokens = x.rearrange("b s d -> (b s) d")
    xn_d = dram("xn_d", (N, D))
    xnT_d = dram("xnT_d", (D, N))
    kaT_d = dram("kaT_d", (D, N))
    va_d = dram("va_d", (N, D))
    vh_d = dram("vh_d", (N, D))
    q_d = dram("q_d", (3, D, N), BF16)
    k_d = dram("k_d", (3, D, N), BF16)
    ya_d = dram("ya_d", (N, D))
    ot_d = dram("ot_d", (B * NG, P, S))
    with ExitStack() as ctx:
        heads = HeadInputs(nc, ctx, q_d, k_d, vh_d)
        with ExitStack() as first_stages:
            causal = CausalInputs(nc, first_stages, xnT_d, kaT_d, va_d, tokens)
            turning = Turning(nc, first_stages, heads, q_d, k_d)
            project(nc, tokens, w_kv_t, w_q, w_kc, w_vc, w_k, w_v, rope_cos, rope_sin,
                    xn_d, xnT_d, kaT_d, va_d, vh_d, causal, turning)
            causal_attention(nc, causal, ya_d, heads, turning)
        ffw = FeedForwardWeights(nc, ctx, w_o, ws_in, w1, w2, w_g, w_e, b_g, b_e, n1_w, n2_w)
        first_chunk = FirstChunk(nc, ctx, ot_d, xn_d)
        head_attention(nc, heads, ot_d, ffw, first_chunk)
        feed_forward(nc, first_chunk, heads, ya_d, ffw, ws_out, out.rearrange("b s d -> (b s) d"))


def rope_tables():
    import numpy as np
    inv = (1.0 / np.float32(10000.0) ** (np.arange(0, DH, 2, dtype=np.float32) / np.float32(DH))).astype(np.float32)
    angle = (np.arange(S, dtype=np.float32)[None, :] * inv[:, None]).astype(np.float32)
    row = np.arange(P) % DH
    sign = np.where(row % 2 == 0, -1.0, 1.0).astype(np.float32)
    cos = np.cos(angle.astype(np.float64)).astype(np.float32)[row // 2]
    sin = np.sin(angle.astype(np.float64)).astype(np.float32)[row // 2] * sign[:, None]
    return np.ascontiguousarray(cos), np.ascontiguousarray(sin)


_INS = ["L0_attn_x", "L0_attn_W", "L0_ffn_Wq", "L0_ffn_Wk_c", "L0_ffn_Wv_c", "L0_ffn_Wk", "L0_ffn_Wv", "L0_ffn_Wo",
        "L0_ffn_W_shared_in", "L0_ffn_W_shared_out", "L0_ffn_W1_shared", "L0_ffn_W2_experts", "L0_ffn_Wg_gate",
        "L0_ffn_We_gate", "L0_ffn_group_bias", "L0_ffn_expert_bias", "L0_ffn_norm1_w", "L0_ffn_norm2_w"]


def kernel(**inputs):
    import numpy as np
    import concourse.bacc as bacc
    from concourse.bass_utils import run_bass_kernel_spmd

    nc = bacc.Bacc("TRN2", target_bir_lowering=False, num_devices=1)
    arrays = {}
    for name in _INS:
        a = np.asarray(inputs[name])
        arrays["in_" + name] = np.ascontiguousarray(a.T if name == "L0_attn_W" else a)
    arrays["in_rope_cos"], arrays["in_rope_sin"] = rope_tables()
    args = [nc.dram_tensor(n, a.shape, mybir.dt.from_np(a.dtype), kind="ExternalInput").ap()
            for n, a in arrays.items()]
    out = nc.dram_tensor("out_dram", (B, S, D), F32, kind="ExternalOutput").ap()
    layer(nc, *args, out)
    r = run_bass_kernel_spmd(nc, [arrays], core_ids=[0])
    return r.results[0]["out_dram"]
```
